# Optimizing a Trainium2 kernel written in Bass

```python
import numpy as np
import jax
import jax.numpy as jnp

def _softmax(x, axis=-1):
    return jax.nn.softmax(x, axis=axis)

def _gelu(x):
    return jax.nn.gelu(x, approximate=True)

def _silu(x):
    return jax.nn.silu(x)

def _sigmoid(x):
    return jax.nn.sigmoid(x)

def _layernorm(x, axis=-1, eps=1e-05):
    m = jnp.mean(x, axis=axis, keepdims=True)
    v = jnp.var(x, axis=axis, keepdims=True)
    return (x - m) / jnp.sqrt(v + eps)

def _scatter_add(tgt, idx, src, axis=0):
    return tgt.at[idx].add(src)

def _segment_sum(src, seg, n):
    return jax.ops.segment_sum(src, seg, n)
kernel_name = 'mk_xattn_seq_d4_seqx_r8_2126ea'

def setup_inputs(seed: int=0):
    np.random.seed(seed)
    _w = jnp.asarray

    def _rec_inputs():
        import jax
        import jax.numpy as jnp
        _rk = jax.random.key(seed)
        x = -0.000917 + 0.9994 * jax.random.normal(jax.random.fold_in(_rk, 1), (2, 512, 128), jnp.float32)
        _lenS = 512 - jax.random.randint(jax.random.fold_in(_rk, 7), (2,), 0, max(1, 512 // 4) + 1, jnp.int32)
        _lenS2 = 32 - jax.random.randint(jax.random.fold_in(_rk, 8), (2,), 0, max(1, 32 // 4) + 1, jnp.int32)
        _ctx_768P = jax.random.normal(jax.random.fold_in(_rk, 11), (2, 16, 96), jnp.float32)
        _ctx_768c = jax.random.dirichlet(jax.random.fold_in(_rk, 511), 0.3 * jnp.ones((16,), jnp.float32), (2, 32))
        _ctx_768t = jnp.einsum('bsk,bkd->bsd', _ctx_768c, _ctx_768P)
        _ctx_768t = _ctx_768t * jax.lax.rsqrt(jnp.mean(jnp.square(_ctx_768t)) + 1e-12) * 0.953939
        ctx_768 = 0.000947723 + 1.00027 * (_ctx_768t + 0.3 * jax.random.normal(jax.random.fold_in(_rk, 611), (2, 32, 96), jnp.float32))
        _validS = jnp.arange(512)[None, :] < _lenS[:, None]
        _validS2 = jnp.arange(32)[None, :] < _lenS2[:, None]
        _causal = jnp.tril(jnp.ones((512, 512), dtype=bool))
        mask_BxS_bf0 = jnp.logical_not(jnp.ones((2, 512), dtype=bool))
        mask_BxS2_bf0 = jnp.logical_not(jnp.ones((2, 32), dtype=bool))
        return (x, ctx_768, mask_BxS_bf0, mask_BxS2_bf0)
    x, ctx_768, mask_BxS_bf0, mask_BxS2_bf0 = _rec_inputs()

    def _L0_xattn_setup():
        import jax, jax.numpy as jnp
        import numpy as np
        D_DEC, D_ENC, H, D_MLP = (128, 96, 16, 512)
        HD = D_DEC // H

        def _layernorm(x, w, b, eps=1e-05):
            m = x.mean(-1, keepdims=True)
            v = ((x - m) ** 2).mean(-1, keepdims=True)
            return (x - m) / jnp.sqrt(v + eps) * w + b

        def _decoder_block(x, enc, tgt_mask, enc_mask, ln1_w, ln1_b, qkv_w, qkv_b, proj_w, proj_b, ln2_w, ln2_b, q_w, q_b, k_w, k_b, v_w, v_b, out_w, out_b, ln3_w, ln3_b, mlp1_w, mlp1_b, mlp2_w, mlp2_b):
            B, T, C = x.shape
            S = enc.shape[1]
            scale = HD ** (-0.5)
            neg = jnp.asarray(-jnp.inf, x.dtype)
            h = _layernorm(x, ln1_w, ln1_b)
            qkv = (h @ qkv_w + qkv_b).reshape(B, T, 3, H, HD)
            q, k, v = [qkv[:, :, i].transpose(0, 2, 1, 3) for i in range(3)]
            attn = jnp.einsum('bhtd,bhsd->bhts', q, k) * scale
            causal = jnp.triu(jnp.ones((T, T), bool), 1)
            attn = jnp.where(causal[None, None], neg, attn)
            attn = jnp.where(tgt_mask[:, None, None, :], neg, attn)
            attn = jax.nn.softmax(attn, axis=-1)
            sa = jnp.einsum('bhts,bhsd->bhtd', attn, v).transpose(0, 2, 1, 3).reshape(B, T, C)
            x = x + sa @ proj_w + proj_b
            h = _layernorm(x, ln2_w, ln2_b)
            q = (h @ q_w + q_b).reshape(B, T, H, HD).transpose(0, 2, 1, 3)
            k = (enc @ k_w + k_b).reshape(B, S, H, HD).transpose(0, 2, 1, 3)
            v = (enc @ v_w + v_b).reshape(B, S, H, HD).transpose(0, 2, 1, 3)
            attn = jnp.einsum('bhtd,bhsd->bhts', q, k) * scale
            attn = jnp.where(enc_mask[:, None, None, :], neg, attn)
            attn = jax.nn.softmax(attn, axis=-1)
            ca = jnp.einsum('bhts,bhsd->bhtd', attn, v).transpose(0, 2, 1, 3).reshape(B, T, C)
            x = x + ca @ out_w + out_b
            h = _layernorm(x, ln3_w, ln3_b)
            h = jax.nn.gelu(h @ mlp1_w + mlp1_b, approximate=False)
            x = x + h @ mlp2_w + mlp2_b
            return x
        key = jax.random.key(seed)
        ks = jax.random.split(key, 16)
        B, T, S = (4, 128, 72)

        def lin(k, din, dout):
            kw, kb = jax.random.split(k)
            bound = 1.0 / np.sqrt(din)
            W = jax.random.uniform(kw, (din, dout), jnp.float32, -bound, bound)
            b = jax.random.uniform(kb, (dout,), jnp.float32, -bound, bound)
            return (W, b)
        qkv_w, qkv_b = lin(ks[0], D_DEC, 3 * D_DEC)
        proj_w, proj_b = lin(ks[1], D_DEC, D_DEC)
        q_w, q_b = lin(ks[2], D_DEC, D_DEC)
        k_w, k_b = lin(ks[3], D_ENC, D_DEC)
        v_w, v_b = lin(ks[4], D_ENC, D_DEC)
        out_w, out_b = lin(ks[5], D_DEC, D_DEC)
        mlp1_w, mlp1_b = lin(ks[6], D_DEC, D_MLP)
        mlp2_w, mlp2_b = lin(ks[7], D_MLP, D_DEC)
        return {'x': jax.random.normal(ks[8], (B, T, D_DEC), jnp.float32), 'enc': jax.random.normal(ks[9], (B, S, D_ENC), jnp.float32), 'tgt_key_padding_mask': jnp.zeros((B, T), bool), 'enc_padding_mask': jnp.zeros((B, S), bool), 'ln1_w': jnp.ones((D_DEC,)), 'ln1_b': jnp.zeros((D_DEC,)), 'qkv_w': qkv_w, 'qkv_b': qkv_b, 'proj_w': proj_w, 'proj_b': proj_b, 'ln2_w': jnp.ones((D_DEC,)), 'ln2_b': jnp.zeros((D_DEC,)), 'q_w': q_w, 'q_b': q_b, 'k_w': k_w, 'k_b': k_b, 'v_w': v_w, 'v_b': v_b, 'out_w': out_w, 'out_b': out_b, 'ln3_w': jnp.ones((D_DEC,)), 'ln3_b': jnp.zeros((D_DEC,)), 'mlp1_w': mlp1_w, 'mlp1_b': mlp1_b, 'mlp2_w': mlp2_w, 'mlp2_b': mlp2_b}
    _L0_xattn_all = _L0_xattn_setup()
    _L0_xattn_in = {k: v for k, v in _L0_xattn_all.items() if k in ('ln1_w', 'ln1_b', 'qkv_w', 'qkv_b', 'proj_w', 'proj_b', 'ln2_w', 'ln2_b', 'q_w', 'q_b', 'k_w', 'k_b', 'v_w', 'v_b', 'out_w', 'out_b', 'ln3_w', 'ln3_b', 'mlp1_w', 'mlp1_b', 'mlp2_w', 'mlp2_b')}
    del _L0_xattn_all

    def _L1_xattn_setup():
        import jax, jax.numpy as jnp
        import numpy as np
        DIM, HEADS, DHEAD, CTX_DIM = (128, 16, 64, 96)
        INNER = HEADS * DHEAD
        FF_HID = 4 * DIM
        EPS = 1e-05

        def _ln(x, g, b):
            mu = jnp.mean(x, axis=-1, keepdims=True)
            var = jnp.mean(jnp.square(x - mu), axis=-1, keepdims=True)
            return (x - mu) * jax.lax.rsqrt(var + EPS) * g + b

        def _attn(x, ctx, Wq, Wk, Wv, Wo, bo):
            b, n, _ = x.shape
            m = ctx.shape[1]
            q = (x @ Wq).reshape(b, n, HEADS, DHEAD)
            k = (ctx @ Wk).reshape(b, m, HEADS, DHEAD)
            v = (ctx @ Wv).reshape(b, m, HEADS, DHEAD)
            scale = DHEAD ** (-0.5)
            sim = jnp.einsum('bihd,bjhd->bhij', q, k) * scale
            attn = jax.nn.softmax(sim, axis=-1)
            out = jnp.einsum('bhij,bjhd->bihd', attn, v).reshape(b, n, INNER)
            return out @ Wo + bo
        key = jax.random.key(seed)
        ks = jax.random.split(key, 24)

        def w(k, shape, fan_in):
            return jax.random.normal(k, shape, jnp.float32) * fan_in ** (-0.5)
        inp = {'x': jax.random.normal(ks[0], (2, 256, DIM), jnp.float32), 'context': jax.random.normal(ks[1], (2, 77, CTX_DIM), jnp.float32), 'Wq1': w(ks[2], (DIM, INNER), DIM), 'Wk1': w(ks[3], (DIM, INNER), DIM), 'Wv1': w(ks[4], (DIM, INNER), DIM), 'Wo1': w(ks[5], (INNER, DIM), INNER), 'bo1': jnp.zeros((DIM,), jnp.float32), 'Wq2': w(ks[6], (DIM, INNER), DIM), 'Wk2': w(ks[7], (CTX_DIM, INNER), CTX_DIM), 'Wv2': w(ks[8], (CTX_DIM, INNER), CTX_DIM), 'Wo2': w(ks[9], (INNER, DIM), INNER), 'bo2': jnp.zeros((DIM,), jnp.float32), 'Wp': w(ks[10], (DIM, 2 * FF_HID), DIM), 'bp': jnp.zeros((2 * FF_HID,), jnp.float32), 'W2': w(ks[11], (FF_HID, DIM), FF_HID), 'b2': jnp.zeros((DIM,), jnp.float32), 'g1': jnp.ones((DIM,), jnp.float32), 'be1': jnp.zeros((DIM,), jnp.float32), 'g2': jnp.ones((DIM,), jnp.float32), 'be2': jnp.zeros((DIM,), jnp.float32), 'g3': jnp.ones((DIM,), jnp.float32), 'be3': jnp.zeros((DIM,), jnp.float32)}
        return inp
    _L1_xattn_all = _L1_xattn_setup()
    _L1_xattn_in = {k: v for k, v in _L1_xattn_all.items() if k in ('Wq1', 'Wk1', 'Wv1', 'Wo1', 'bo1', 'Wq2', 'Wk2', 'Wv2', 'Wo2', 'bo2', 'Wp', 'bp', 'W2', 'b2', 'g1', 'be1', 'g2', 'be2', 'g3', 'be3')}
    del _L1_xattn_all

    def _L2_xattn_setup():
        import jax, jax.numpy as jnp
        import numpy as np
        B, N, D = (1, 256, 128)
        H, DH = (16, 64)
        CN, CD = (77, 96)
        FF = 4 * D
        EPS = 1e-05
        SCALE = DH ** (-0.5)

        def layer_norm(x, g, b):
            mu = jnp.mean(x, axis=-1, keepdims=True)
            var = jnp.var(x, axis=-1, keepdims=True)
            return (x - mu) * jax.lax.rsqrt(var + EPS) * g + b

        def cross_attention(x, ctx, wq, wk, wv, wo, bo):
            b, n, _ = x.shape
            m = ctx.shape[1]
            q = (x @ wq.T).reshape(b, n, H, DH)
            k = (ctx @ wk.T).reshape(b, m, H, DH)
            v = (ctx @ wv.T).reshape(b, m, H, DH)
            sim = jnp.einsum('bihd,bjhd->bhij', q, k) * SCALE
            attn = jax.nn.softmax(sim, axis=-1)
            out = jnp.einsum('bhij,bjhd->bihd', attn, v).reshape(b, n, H * DH)
            return out @ wo.T + bo

        def geglu_ffn(x, w_geglu, b_geglu, w_ffout, b_ffout):
            proj = x @ w_geglu.T + b_geglu
            h, gate = (proj[..., :FF], proj[..., FF:])
            h = h * jax.nn.gelu(gate, approximate=False)
            return h @ w_ffout.T + b_ffout
        key = jax.random.key(seed)
        ks = jax.random.split(key, 24)
        s = 0.02
        n = lambda k, shape: jax.random.normal(k, shape, dtype=jnp.float32) * s
        return {'hidden_states': jax.random.normal(ks[0], (B, N, D), dtype=jnp.float32), 'context': jax.random.normal(ks[1], (B, CN, CD), dtype=jnp.float32), 'wq1': n(ks[2], (H * DH, D)), 'wk1': n(ks[3], (H * DH, D)), 'wv1': n(ks[4], (H * DH, D)), 'wo1': n(ks[5], (D, H * DH)), 'bo1': jnp.zeros((D,), jnp.float32), 'wq2': n(ks[6], (H * DH, D)), 'wk2': n(ks[7], (H * DH, CD)), 'wv2': n(ks[8], (H * DH, CD)), 'wo2': n(ks[9], (D, H * DH)), 'bo2': jnp.zeros((D,), jnp.float32), 'w_geglu': n(ks[10], (2 * FF, D)), 'b_geglu': jnp.zeros((2 * FF,), jnp.float32), 'w_ffout': n(ks[11], (D, FF)), 'b_ffout': jnp.zeros((D,), jnp.float32), 'ln1_g': jnp.ones((D,), jnp.float32), 'ln1_b': jnp.zeros((D,), jnp.float32), 'ln2_g': jnp.ones((D,), jnp.float32), 'ln2_b': jnp.zeros((D,), jnp.float32), 'ln3_g': jnp.ones((D,), jnp.float32), 'ln3_b': jnp.zeros((D,), jnp.float32)}
    _L2_xattn_all = _L2_xattn_setup()
    _L2_xattn_in = {k: v for k, v in _L2_xattn_all.items() if k in ('wq1', 'wk1', 'wv1', 'wo1', 'bo1', 'wq2', 'wk2', 'wv2', 'wo2', 'bo2', 'w_geglu', 'b_geglu', 'w_ffout', 'b_ffout', 'ln1_g', 'ln1_b', 'ln2_g', 'ln2_b', 'ln3_g', 'ln3_b')}
    del _L2_xattn_all

    def _L3_xattn_setup():
        import jax, jax.numpy as jnp
        import numpy as np
        DIM = 128
        HEADS = 16
        D_HEAD = 64
        INNER = HEADS * D_HEAD
        CTX_DIM = 96
        FF_INNER = 4 * DIM
        SCALE = D_HEAD ** (-0.5)

        def _layer_norm(x, w, b, eps=1e-05):
            mu = jnp.mean(x, axis=-1, keepdims=True)
            var = jnp.var(x, axis=-1, keepdims=True)
            return (x - mu) * jax.lax.rsqrt(var + eps) * w + b

        def _attention(x, ctx, wq, wk, wv, wo, wob):

            def split_heads(t):
                b, n, _ = t.shape
                return t.reshape(b, n, HEADS, D_HEAD).transpose(0, 2, 1, 3)
            q = split_heads(x @ wq)
            k = split_heads(ctx @ wk)
            v = split_heads(ctx @ wv)
            sim = jnp.einsum('bhid,bhjd->bhij', q, k) * SCALE
            attn = jax.nn.softmax(sim, axis=-1)
            out = jnp.einsum('bhij,bhjd->bhid', attn, v)
            b, h, n, d = out.shape
            out = out.transpose(0, 2, 1, 3).reshape(b, n, h * d)
            return out @ wo + wob
        key = jax.random.key(seed)
        ks = jax.random.split(key, 24)
        g = lambda k, shape: jax.random.normal(k, shape, dtype=jnp.float32) * 0.02
        inp = {'x': jax.random.normal(ks[0], (1, 512, DIM), dtype=jnp.float32), 'context': jax.random.normal(ks[1], (1, 77, CTX_DIM), dtype=jnp.float32), 'n1_w': jnp.ones((DIM,), jnp.float32), 'n1_b': jnp.zeros((DIM,), jnp.float32), 'n2_w': jnp.ones((DIM,), jnp.float32), 'n2_b': jnp.zeros((DIM,), jnp.float32), 'n3_w': jnp.ones((DIM,), jnp.float32), 'n3_b': jnp.zeros((DIM,), jnp.float32), 'q1_w': g(ks[2], (DIM, INNER)), 'k1_w': g(ks[3], (DIM, INNER)), 'v1_w': g(ks[4], (DIM, INNER)), 'o1_w': g(ks[5], (INNER, DIM)), 'o1_b': jnp.zeros((DIM,), jnp.float32), 'q2_w': g(ks[6], (DIM, INNER)), 'k2_w': g(ks[7], (CTX_DIM, INNER)), 'v2_w': g(ks[8], (CTX_DIM, INNER)), 'o2_w': g(ks[9], (INNER, DIM)), 'o2_b': jnp.zeros((DIM,), jnp.float32), 'ff1_w': g(ks[10], (DIM, 2 * FF_INNER)), 'ff1_b': jnp.zeros((2 * FF_INNER,), jnp.float32), 'ff2_w': g(ks[11], (FF_INNER, DIM)), 'ff2_b': jnp.zeros((DIM,), jnp.float32)}
        return inp
    _L3_xattn_all = _L3_xattn_setup()
    _L3_xattn_in = {k: v for k, v in _L3_xattn_all.items() if k in ('n1_w', 'n1_b', 'n2_w', 'n2_b', 'n3_w', 'n3_b', 'q1_w', 'k1_w', 'v1_w', 'o1_w', 'o1_b', 'q2_w', 'k2_w', 'v2_w', 'o2_w', 'o2_b', 'ff1_w', 'ff1_b', 'ff2_w', 'ff2_b')}
    del _L3_xattn_all
    return {'x': x, 'ctx_768': ctx_768, 'mask_BxS_bf0': mask_BxS_bf0, 'mask_BxS2_bf0': mask_BxS2_bf0, 'L0_xattn_ln1_w': _L0_xattn_in['ln1_w'], 'L0_xattn_ln1_b': _L0_xattn_in['ln1_b'], 'L0_xattn_qkv_w': _L0_xattn_in['qkv_w'], 'L0_xattn_qkv_b': _L0_xattn_in['qkv_b'], 'L0_xattn_proj_w': _L0_xattn_in['proj_w'], 'L0_xattn_proj_b': _L0_xattn_in['proj_b'], 'L0_xattn_ln2_w': _L0_xattn_in['ln2_w'], 'L0_xattn_ln2_b': _L0_xattn_in['ln2_b'], 'L0_xattn_q_w': _L0_xattn_in['q_w'], 'L0_xattn_q_b': _L0_xattn_in['q_b'], 'L0_xattn_k_w': _L0_xattn_in['k_w'], 'L0_xattn_k_b': _L0_xattn_in['k_b'], 'L0_xattn_v_w': _L0_xattn_in['v_w'], 'L0_xattn_v_b': _L0_xattn_in['v_b'], 'L0_xattn_out_w': _L0_xattn_in['out_w'], 'L0_xattn_out_b': _L0_xattn_in['out_b'], 'L0_xattn_ln3_w': _L0_xattn_in['ln3_w'], 'L0_xattn_ln3_b': _L0_xattn_in['ln3_b'], 'L0_xattn_mlp1_w': _L0_xattn_in['mlp1_w'], 'L0_xattn_mlp1_b': _L0_xattn_in['mlp1_b'], 'L0_xattn_mlp2_w': _L0_xattn_in['mlp2_w'], 'L0_xattn_mlp2_b': _L0_xattn_in['mlp2_b'], 'L1_xattn_Wq1': _L1_xattn_in['Wq1'], 'L1_xattn_Wk1': _L1_xattn_in['Wk1'], 'L1_xattn_Wv1': _L1_xattn_in['Wv1'], 'L1_xattn_Wo1': _L1_xattn_in['Wo1'], 'L1_xattn_bo1': _L1_xattn_in['bo1'], 'L1_xattn_Wq2': _L1_xattn_in['Wq2'], 'L1_xattn_Wk2': _L1_xattn_in['Wk2'], 'L1_xattn_Wv2': _L1_xattn_in['Wv2'], 'L1_xattn_Wo2': _L1_xattn_in['Wo2'], 'L1_xattn_bo2': _L1_xattn_in['bo2'], 'L1_xattn_Wp': _L1_xattn_in['Wp'], 'L1_xattn_bp': _L1_xattn_in['bp'], 'L1_xattn_W2': _L1_xattn_in['W2'], 'L1_xattn_b2': _L1_xattn_in['b2'], 'L1_xattn_g1': _L1_xattn_in['g1'], 'L1_xattn_be1': _L1_xattn_in['be1'], 'L1_xattn_g2': _L1_xattn_in['g2'], 'L1_xattn_be2': _L1_xattn_in['be2'], 'L1_xattn_g3': _L1_xattn_in['g3'], 'L1_xattn_be3': _L1_xattn_in['be3'], 'L2_xattn_wq1': _L2_xattn_in['wq1'], 'L2_xattn_wk1': _L2_xattn_in['wk1'], 'L2_xattn_wv1': _L2_xattn_in['wv1'], 'L2_xattn_wo1': _L2_xattn_in['wo1'], 'L2_xattn_bo1': _L2_xattn_in['bo1'], 'L2_xattn_wq2': _L2_xattn_in['wq2'], 'L2_xattn_wk2': _L2_xattn_in['wk2'], 'L2_xattn_wv2': _L2_xattn_in['wv2'], 'L2_xattn_wo2': _L2_xattn_in['wo2'], 'L2_xattn_bo2': _L2_xattn_in['bo2'], 'L2_xattn_w_geglu': _L2_xattn_in['w_geglu'], 'L2_xattn_b_geglu': _L2_xattn_in['b_geglu'], 'L2_xattn_w_ffout': _L2_xattn_in['w_ffout'], 'L2_xattn_b_ffout': _L2_xattn_in['b_ffout'], 'L2_xattn_ln1_g': _L2_xattn_in['ln1_g'], 'L2_xattn_ln1_b': _L2_xattn_in['ln1_b'], 'L2_xattn_ln2_g': _L2_xattn_in['ln2_g'], 'L2_xattn_ln2_b': _L2_xattn_in['ln2_b'], 'L2_xattn_ln3_g': _L2_xattn_in['ln3_g'], 'L2_xattn_ln3_b': _L2_xattn_in['ln3_b'], 'L3_xattn_n1_w': _L3_xattn_in['n1_w'], 'L3_xattn_n1_b': _L3_xattn_in['n1_b'], 'L3_xattn_n2_w': _L3_xattn_in['n2_w'], 'L3_xattn_n2_b': _L3_xattn_in['n2_b'], 'L3_xattn_n3_w': _L3_xattn_in['n3_w'], 'L3_xattn_n3_b': _L3_xattn_in['n3_b'], 'L3_xattn_q1_w': _L3_xattn_in['q1_w'], 'L3_xattn_k1_w': _L3_xattn_in['k1_w'], 'L3_xattn_v1_w': _L3_xattn_in['v1_w'], 'L3_xattn_o1_w': _L3_xattn_in['o1_w'], 'L3_xattn_o1_b': _L3_xattn_in['o1_b'], 'L3_xattn_q2_w': _L3_xattn_in['q2_w'], 'L3_xattn_k2_w': _L3_xattn_in['k2_w'], 'L3_xattn_v2_w': _L3_xattn_in['v2_w'], 'L3_xattn_o2_w': _L3_xattn_in['o2_w'], 'L3_xattn_o2_b': _L3_xattn_in['o2_b'], 'L3_xattn_ff1_w': _L3_xattn_in['ff1_w'], 'L3_xattn_ff1_b': _L3_xattn_in['ff1_b'], 'L3_xattn_ff2_w': _L3_xattn_in['ff2_w'], 'L3_xattn_ff2_b': _L3_xattn_in['ff2_b']}

def reference(x, ctx_768, mask_BxS_bf0, mask_BxS2_bf0, L0_xattn_ln1_w, L0_xattn_ln1_b, L0_xattn_qkv_w, L0_xattn_qkv_b, L0_xattn_proj_w, L0_xattn_proj_b, L0_xattn_ln2_w, L0_xattn_ln2_b, L0_xattn_q_w, L0_xattn_q_b, L0_xattn_k_w, L0_xattn_k_b, L0_xattn_v_w, L0_xattn_v_b, L0_xattn_out_w, L0_xattn_out_b, L0_xattn_ln3_w, L0_xattn_ln3_b, L0_xattn_mlp1_w, L0_xattn_mlp1_b, L0_xattn_mlp2_w, L0_xattn_mlp2_b, L1_xattn_Wq1, L1_xattn_Wk1, L1_xattn_Wv1, L1_xattn_Wo1, L1_xattn_bo1, L1_xattn_Wq2, L1_xattn_Wk2, L1_xattn_Wv2, L1_xattn_Wo2, L1_xattn_bo2, L1_xattn_Wp, L1_xattn_bp, L1_xattn_W2, L1_xattn_b2, L1_xattn_g1, L1_xattn_be1, L1_xattn_g2, L1_xattn_be2, L1_xattn_g3, L1_xattn_be3, L2_xattn_wq1, L2_xattn_wk1, L2_xattn_wv1, L2_xattn_wo1, L2_xattn_bo1, L2_xattn_wq2, L2_xattn_wk2, L2_xattn_wv2, L2_xattn_wo2, L2_xattn_bo2, L2_xattn_w_geglu, L2_xattn_b_geglu, L2_xattn_w_ffout, L2_xattn_b_ffout, L2_xattn_ln1_g, L2_xattn_ln1_b, L2_xattn_ln2_g, L2_xattn_ln2_b, L2_xattn_ln3_g, L2_xattn_ln3_b, L3_xattn_n1_w, L3_xattn_n1_b, L3_xattn_n2_w, L3_xattn_n2_b, L3_xattn_n3_w, L3_xattn_n3_b, L3_xattn_q1_w, L3_xattn_k1_w, L3_xattn_v1_w, L3_xattn_o1_w, L3_xattn_o1_b, L3_xattn_q2_w, L3_xattn_k2_w, L3_xattn_v2_w, L3_xattn_o2_w, L3_xattn_o2_b, L3_xattn_ff1_w, L3_xattn_ff1_b, L3_xattn_ff2_w, L3_xattn_ff2_b):
    import jax
    import jax.numpy as jnp

    def _L0_xattn_ref(x, enc, tgt_key_padding_mask, enc_padding_mask, ln1_w, ln1_b, qkv_w, qkv_b, proj_w, proj_b, ln2_w, ln2_b, q_w, q_b, k_w, k_b, v_w, v_b, out_w, out_b, ln3_w, ln3_b, mlp1_w, mlp1_b, mlp2_w, mlp2_b):
        import jax, jax.numpy as jnp
        import numpy as np
        D_DEC, D_ENC, H, D_MLP = (128, 96, 16, 512)
        HD = D_DEC // H

        def _layernorm(x, w, b, eps=1e-05):
            m = x.mean(-1, keepdims=True)
            v = ((x - m) ** 2).mean(-1, keepdims=True)
            return (x - m) / jnp.sqrt(v + eps) * w + b

        def _decoder_block(x, enc, tgt_mask, enc_mask, ln1_w, ln1_b, qkv_w, qkv_b, proj_w, proj_b, ln2_w, ln2_b, q_w, q_b, k_w, k_b, v_w, v_b, out_w, out_b, ln3_w, ln3_b, mlp1_w, mlp1_b, mlp2_w, mlp2_b):
            B, T, C = x.shape
            S = enc.shape[1]
            scale = HD ** (-0.5)
            neg = jnp.asarray(-jnp.inf, x.dtype)
            h = _layernorm(x, ln1_w, ln1_b)
            qkv = (h @ qkv_w + qkv_b).reshape(B, T, 3, H, HD)
            q, k, v = [qkv[:, :, i].transpose(0, 2, 1, 3) for i in range(3)]
            attn = jnp.einsum('bhtd,bhsd->bhts', q, k) * scale
            causal = jnp.triu(jnp.ones((T, T), bool), 1)
            attn = jnp.where(causal[None, None], neg, attn)
            attn = jnp.where(tgt_mask[:, None, None, :], neg, attn)
            attn = jax.nn.softmax(attn, axis=-1)
            sa = jnp.einsum('bhts,bhsd->bhtd', attn, v).transpose(0, 2, 1, 3).reshape(B, T, C)
            x = x + sa @ proj_w + proj_b
            h = _layernorm(x, ln2_w, ln2_b)
            q = (h @ q_w + q_b).reshape(B, T, H, HD).transpose(0, 2, 1, 3)
            k = (enc @ k_w + k_b).reshape(B, S, H, HD).transpose(0, 2, 1, 3)
            v = (enc @ v_w + v_b).reshape(B, S, H, HD).transpose(0, 2, 1, 3)
            attn = jnp.einsum('bhtd,bhsd->bhts', q, k) * scale
            attn = jnp.where(enc_mask[:, None, None, :], neg, attn)
            attn = jax.nn.softmax(attn, axis=-1)
            ca = jnp.einsum('bhts,bhsd->bhtd', attn, v).transpose(0, 2, 1, 3).reshape(B, T, C)
            x = x + ca @ out_w + out_b
            h = _layernorm(x, ln3_w, ln3_b)
            h = jax.nn.gelu(h @ mlp1_w + mlp1_b, approximate=False)
            x = x + h @ mlp2_w + mlp2_b
            return x
        return _decoder_block(x, enc, tgt_key_padding_mask, enc_padding_mask, ln1_w, ln1_b, qkv_w, qkv_b, proj_w, proj_b, ln2_w, ln2_b, q_w, q_b, k_w, k_b, v_w, v_b, out_w, out_b, ln3_w, ln3_b, mlp1_w, mlp1_b, mlp2_w, mlp2_b)

    def _L1_xattn_ref(x, context, Wq1, Wk1, Wv1, Wo1, bo1, Wq2, Wk2, Wv2, Wo2, bo2, Wp, bp, W2, b2, g1, be1, g2, be2, g3, be3):
        import jax, jax.numpy as jnp
        import numpy as np
        DIM, HEADS, DHEAD, CTX_DIM = (128, 16, 64, 96)
        INNER = HEADS * DHEAD
        FF_HID = 4 * DIM
        EPS = 1e-05

        def _ln(x, g, b):
            mu = jnp.mean(x, axis=-1, keepdims=True)
            var = jnp.mean(jnp.square(x - mu), axis=-1, keepdims=True)
            return (x - mu) * jax.lax.rsqrt(var + EPS) * g + b

        def _attn(x, ctx, Wq, Wk, Wv, Wo, bo):
            b, n, _ = x.shape
            m = ctx.shape[1]
            q = (x @ Wq).reshape(b, n, HEADS, DHEAD)
            k = (ctx @ Wk).reshape(b, m, HEADS, DHEAD)
            v = (ctx @ Wv).reshape(b, m, HEADS, DHEAD)
            scale = DHEAD ** (-0.5)
            sim = jnp.einsum('bihd,bjhd->bhij', q, k) * scale
            attn = jax.nn.softmax(sim, axis=-1)
            out = jnp.einsum('bhij,bjhd->bihd', attn, v).reshape(b, n, INNER)
            return out @ Wo + bo
        h = _ln(x, g1, be1)
        x = _attn(h, h, Wq1, Wk1, Wv1, Wo1, bo1) + x
        h = _ln(x, g2, be2)
        x = _attn(h, context, Wq2, Wk2, Wv2, Wo2, bo2) + x
        h = _ln(x, g3, be3)
        y = h @ Wp + bp
        a, gate = (y[..., :FF_HID], y[..., FF_HID:])
        x = a * jax.nn.gelu(gate, approximate=False) @ W2 + b2 + x
        return x

    def _L2_xattn_ref(hidden_states, context, wq1, wk1, wv1, wo1, bo1, wq2, wk2, wv2, wo2, bo2, w_geglu, b_geglu, w_ffout, b_ffout, ln1_g, ln1_b, ln2_g, ln2_b, ln3_g, ln3_b):
        import jax, jax.numpy as jnp
        import numpy as np
        B, N, D = (1, 256, 128)
        H, DH = (16, 64)
        CN, CD = (77, 96)
        FF = 4 * D
        EPS = 1e-05
        SCALE = DH ** (-0.5)

        def layer_norm(x, g, b):
            mu = jnp.mean(x, axis=-1, keepdims=True)
            var = jnp.var(x, axis=-1, keepdims=True)
            return (x - mu) * jax.lax.rsqrt(var + EPS) * g + b

        def cross_attention(x, ctx, wq, wk, wv, wo, bo):
            b, n, _ = x.shape
            m = ctx.shape[1]
            q = (x @ wq.T).reshape(b, n, H, DH)
            k = (ctx @ wk.T).reshape(b, m, H, DH)
            v = (ctx @ wv.T).reshape(b, m, H, DH)
            sim = jnp.einsum('bihd,bjhd->bhij', q, k) * SCALE
            attn = jax.nn.softmax(sim, axis=-1)
            out = jnp.einsum('bhij,bjhd->bihd', attn, v).reshape(b, n, H * DH)
            return out @ wo.T + bo

        def geglu_ffn(x, w_geglu, b_geglu, w_ffout, b_ffout):
            proj = x @ w_geglu.T + b_geglu
            h, gate = (proj[..., :FF], proj[..., FF:])
            h = h * jax.nn.gelu(gate, approximate=False)
            return h @ w_ffout.T + b_ffout
        x = hidden_states
        x = cross_attention(layer_norm(x, ln1_g, ln1_b), layer_norm(x, ln1_g, ln1_b), wq1, wk1, wv1, wo1, bo1) + x
        x = cross_attention(layer_norm(x, ln2_g, ln2_b), context, wq2, wk2, wv2, wo2, bo2) + x
        x = geglu_ffn(layer_norm(x, ln3_g, ln3_b), w_geglu, b_geglu, w_ffout, b_ffout) + x
        return x

    def _L3_xattn_ref(x, context, n1_w, n1_b, n2_w, n2_b, n3_w, n3_b, q1_w, k1_w, v1_w, o1_w, o1_b, q2_w, k2_w, v2_w, o2_w, o2_b, ff1_w, ff1_b, ff2_w, ff2_b):
        import jax, jax.numpy as jnp
        import numpy as np
        DIM = 128
        HEADS = 16
        D_HEAD = 64
        INNER = HEADS * D_HEAD
        CTX_DIM = 96
        FF_INNER = 4 * DIM
        SCALE = D_HEAD ** (-0.5)

        def _layer_norm(x, w, b, eps=1e-05):
            mu = jnp.mean(x, axis=-1, keepdims=True)
            var = jnp.var(x, axis=-1, keepdims=True)
            return (x - mu) * jax.lax.rsqrt(var + eps) * w + b

        def _attention(x, ctx, wq, wk, wv, wo, wob):

            def split_heads(t):
                b, n, _ = t.shape
                return t.reshape(b, n, HEADS, D_HEAD).transpose(0, 2, 1, 3)
            q = split_heads(x @ wq)
            k = split_heads(ctx @ wk)
            v = split_heads(ctx @ wv)
            sim = jnp.einsum('bhid,bhjd->bhij', q, k) * SCALE
            attn = jax.nn.softmax(sim, axis=-1)
            out = jnp.einsum('bhij,bhjd->bhid', attn, v)
            b, h, n, d = out.shape
            out = out.transpose(0, 2, 1, 3).reshape(b, n, h * d)
            return out @ wo + wob
        h = _layer_norm(x, n1_w, n1_b)
        x = _attention(h, h, q1_w, k1_w, v1_w, o1_w, o1_b) + x
        h = _layer_norm(x, n2_w, n2_b)
        x = _attention(h, context, q2_w, k2_w, v2_w, o2_w, o2_b) + x
        h = _layer_norm(x, n3_w, n3_b)
        proj = h @ ff1_w + ff1_b
        a, gate = jnp.split(proj, 2, axis=-1)
        h = a * jax.nn.gelu(gate, approximate=False)
        x = h @ ff2_w + ff2_b + x
        return x
    x = _L0_xattn_ref(x, ctx_768, mask_BxS_bf0, mask_BxS2_bf0, L0_xattn_ln1_w, L0_xattn_ln1_b, L0_xattn_qkv_w, L0_xattn_qkv_b, L0_xattn_proj_w, L0_xattn_proj_b, L0_xattn_ln2_w, L0_xattn_ln2_b, L0_xattn_q_w, L0_xattn_q_b, L0_xattn_k_w, L0_xattn_k_b, L0_xattn_v_w, L0_xattn_v_b, L0_xattn_out_w, L0_xattn_out_b, L0_xattn_ln3_w, L0_xattn_ln3_b, L0_xattn_mlp1_w, L0_xattn_mlp1_b, L0_xattn_mlp2_w, L0_xattn_mlp2_b)
    x = _L1_xattn_ref(x, ctx_768, L1_xattn_Wq1, L1_xattn_Wk1, L1_xattn_Wv1, L1_xattn_Wo1, L1_xattn_bo1, L1_xattn_Wq2, L1_xattn_Wk2, L1_xattn_Wv2, L1_xattn_Wo2, L1_xattn_bo2, L1_xattn_Wp, L1_xattn_bp, L1_xattn_W2, L1_xattn_b2, L1_xattn_g1, L1_xattn_be1, L1_xattn_g2, L1_xattn_be2, L1_xattn_g3, L1_xattn_be3)
    x = _L2_xattn_ref(x, ctx_768, L2_xattn_wq1, L2_xattn_wk1, L2_xattn_wv1, L2_xattn_wo1, L2_xattn_bo1, L2_xattn_wq2, L2_xattn_wk2, L2_xattn_wv2, L2_xattn_wo2, L2_xattn_bo2, L2_xattn_w_geglu, L2_xattn_b_geglu, L2_xattn_w_ffout, L2_xattn_b_ffout, L2_xattn_ln1_g, L2_xattn_ln1_b, L2_xattn_ln2_g, L2_xattn_ln2_b, L2_xattn_ln3_g, L2_xattn_ln3_b)
    x = _L3_xattn_ref(x, ctx_768, L3_xattn_n1_w, L3_xattn_n1_b, L3_xattn_n2_w, L3_xattn_n2_b, L3_xattn_n3_w, L3_xattn_n3_b, L3_xattn_q1_w, L3_xattn_k1_w, L3_xattn_v1_w, L3_xattn_o1_w, L3_xattn_o1_b, L3_xattn_q2_w, L3_xattn_k2_w, L3_xattn_v2_w, L3_xattn_o2_w, L3_xattn_o2_b, L3_xattn_ff1_w, L3_xattn_ff1_b, L3_xattn_ff2_w, L3_xattn_ff2_b)
    return x

_drawn_inputs = setup_inputs


def setup_inputs(seed=0):
    import zlib

    import numpy as np

    out = dict(_drawn_inputs(seed))
    spreads = {'L0_xattn_ln1_w': (1.0, 0.6),
     'L0_xattn_ln1_b': (0.0, 0.1),
     'L0_xattn_ln2_w': (1.0, 0.6),
     'L0_xattn_ln2_b': (0.0, 0.8),
     'L0_xattn_ln3_w': (1.0, 0.2),
     'L0_xattn_ln3_b': (0.0, 0.309),
     'L1_xattn_bo1': (0.0, 0.1),
     'L1_xattn_bo2': (0.0, 0.1),
     'L1_xattn_bp': (0.0, 0.1),
     'L1_xattn_b2': (0.0, 0.1),
     'L1_xattn_g1': (1.0, 0.2),
     'L1_xattn_be1': (0.0, 0.1),
     'L1_xattn_g2': (1.0, 0.2),
     'L1_xattn_be2': (0.0, 0.341),
     'L1_xattn_g3': (1.0, 0.2),
     'L1_xattn_be3': (0.0, 0.1),
     'L2_xattn_bo1': (0.0, 0.1),
     'L2_xattn_bo2': (0.0, 0.1),
     'L2_xattn_b_geglu': (0.0, 0.8),
     'L2_xattn_b_ffout': (0.0, 0.547),
     'L2_xattn_ln1_g': (1.0, 0.6),
     'L2_xattn_ln1_b': (0.0, 0.799),
     'L2_xattn_ln2_g': (1.0, 0.6),
     'L2_xattn_ln2_b': (0.0, 0.8),
     'L2_xattn_ln3_g': (1.0, 0.6),
     'L2_xattn_ln3_b': (0.0, 0.8),
     'L3_xattn_n1_w': (1.0, 0.6),
     'L3_xattn_n1_b': (0.0, 2.0),
     'L3_xattn_n2_w': (1.0, 0.6),
     'L3_xattn_n2_b': (0.0, 2.0),
     'L3_xattn_n3_w': (1.0, 0.6),
     'L3_xattn_n3_b': (0.0, 0.8),
     'L3_xattn_o1_b': (0.0, 0.481),
     'L3_xattn_o2_b': (0.0, 0.433),
     'L3_xattn_ff1_b': (0.0, 0.8),
     'L3_xattn_ff2_b': (0.0, 0.8)}
    factors = {'L0_xattn_q_b': 8.0,
     'L0_xattn_k_b': 64.0,
     'L2_xattn_wq1': 8.0,
     'L2_xattn_wk1': 8.0,
     'L2_xattn_wq2': 8.0,
     'L2_xattn_wk2': 8.0,
     'L2_xattn_w_geglu': 5.248,
     'L2_xattn_w_ffout': 5.059,
     'L3_xattn_q1_w': 21.718,
     'L3_xattn_k1_w': 8.0,
     'L3_xattn_q2_w': 31.926,
     'L3_xattn_k2_w': 30.527,
     'L3_xattn_ff1_w': 5.434,
     'L3_xattn_ff2_w': 5.461,
     'L3_xattn_v2_w': 3.357,
     'L3_xattn_o2_w': 3.36}
    for name, (base, spread) in spreads.items():
        noise = np.random.default_rng([zlib.crc32(name.encode()), seed]).standard_normal(out[name].shape)
        drawn = base * np.exp(spread * noise) if base else spread * noise
        out[name] = jnp.asarray(drawn.astype(out[name].dtype))
    for name, factor in factors.items():
        out[name] = (out[name] * factor).astype(out[name].dtype)
    return out
```

```python
import concourse.bass as bass
from concourse import mybir
from contextlib import ExitStack


B, T, C = 2, 512, 128
NT = B * T // 128
TB = T // 128
S, CE = 32, 96
H = 16
D0 = C // H
D = 64
HID = 512
FC = HID // 128
G0 = 4
NG = H // G0
LOOP_LAYERS = 3
ROW_MASK, ROW_MAX = 3 * D0, 3 * D0 + 1
BIG = 1e30


class Steps:

    def __init__(self, engine, semaphore):
        self.engine, self.semaphore, self.base, self.n = engine, semaphore, 0, 0

    def add(self, instruction):
        instruction.then_inc(self.semaphore, 1)
        self.n += 1

    def wait(self):
        self.engine.wait_ge(self.semaphore, self.base + self.n)

    def enter(self, index, per_turn):
        kept = (self.base, self.n, per_turn)
        self.base, self.n = self.base + self.n + index * per_turn, 0
        return kept

    def leave(self, kept, turns):
        base, n, per_turn = kept
        assert self.n == per_turn, (self.n, per_turn)
        self.base, self.n = base, n + turns * per_turn


def decoder_stack_kernel(nc, x_in, ctx_t, tgt_mask, enc_mask, consts, w0_qk, w0, wk0, vec0, rows0,
                         w_attn, w_ctx, w_cross, w_ff, vec, rows, out):
    f32, f32r, bf16, u8 = mybir.dt.float32, mybir.dt.float32r, mybir.dt.bfloat16, mybir.dt.uint8
    ALU = mybir.AluOpType
    ACT = mybir.ActivationFunctionType
    X = mybir.AxisListType.X
    EPS = 1e-5
    SCALE0 = float(D0) ** -0.5
    SCALE = float(D) ** -0.5

    x_dram = x_in.rearrange("b (t p) c -> p (b t) c", p=128)
    out_dram = out.rearrange("b (t p) c -> p (b t) c", p=128)

    ctx = ExitStack()
    with ctx:
        def sb(name, shape, dt=f32):
            return ctx.enter_context(nc.sbuf_tensor(name, shape, dt))

        def sem(name):
            return ctx.enter_context(nc.semaphore(name))

        x = sb("x", [128, NT, C])
        xhat = sb("xhat", [128, NT, C])
        hT = sb("hT", [128, NT * 128])
        hTh = sb("hTh", [128, NT * 128], f32r)
        hTl = sb("hTl", [128, NT * 128], f32r)
        stats = sb("stats", [128, NT, 6])
        mv = sb("mv", [128, NT, 2])
        veps = sb("veps", [128, NT])
        rstd = sb("rstd", [128, NT])
        mhalf = sb("mhalf", [128, NT])
        cst = sb("cst", [128, 128 + 128 + 4 + H])
        ident, tri = cst[:, 0:128], cst[:, 128:256]
        sQ, tQ, sK, tK = (cst[:, 256 + n:257 + n] for n in range(4))
        head_mask = cst[:, 260:260 + H]
        ident_bf = sb("ident_bf", [128, 128], bf16)
        tri_bf = sb("tri_bf", [128, 128], bf16)
        ones_row = sb("ones_row", [1, 128])
        spread = sb("spread", [128, 128], f32r)
        ctxT = sb("ctxT", [CE, B * S])

        wqk = sb("wqk", [128, 2 * 128 + 2])
        wl0 = sb("wl0", [128, 4 * C + HID + FC * C])
        w0_v, w0_proj, w0_qT, w0_out = (wl0[:, n * C:(n + 1) * C] for n in range(4))
        w0_m1 = wl0[:, 4 * C:4 * C + HID]
        w0_m2 = wl0[:, 4 * C + HID:4 * C + 2 * HID].rearrange("p (j c) -> p j c", j=FC)
        wkv0 = sb("wkv0", [CE, 2 * C])
        v0 = sb("v0", [128, 13])
        r0 = sb("r0", [128, 4, C])

        wa = sb("wa", [D, 2, 4 * C])
        wc = sb("wc", [CE, 2, H * D])
        wx = sb("wx", [128, H // 2, 2 * C])
        wf = sb("wf", [128, 2 * HID + FC * C])
        w_p, w_2 = wf[:, 0:2 * HID], wf[:, 2 * HID:].rearrange("p (j c) -> p j c", j=FC)
        vl = sb("vl", [128, 14])
        rl = sb("rl", [128, 3, C])

        A_hi = sb("A_hi", [128, 2, C], f32r)
        A_lo = sb("A_lo", [128, 2, C], f32r)
        Bm = sb("Bm", [128, 2, C])
        T_hi = sb("T_hi", [128, 2, T], f32r)
        T_lo = sb("T_lo", [128, 2, T], f32r)
        V1 = sb("V1", [128, 4, TB, C + 1])
        mcol = sb("mcol", [128, TB])
        mrow = sb("mrow", [128, T], f32r)
        rden = sb("rden", [128, 2, TB])

        K2T = sb("K2T", [128, H // 2, B * S])
        V2T = sb("V2T", [128, H // 2, B * S])
        Gm = sb("Gm", [128, B, H * S])
        Um = sb("Um", [128, B, 4, C])
        cross_bias = sb("cross_bias", [1, B, H * S])
        em8 = sb("em8", [1, B, S], u8)
        em = sb("em", [1, B, S])
        keepn = sb("keepn", [1, B, S])
        poison = sb("poison", [1, 3 * B])
        cmax = sb("cmax", [128, 2, H])
        csum = sb("csum", [128, 2, H])
        crec = sb("crec", [128, 2, H])
        Ec = sb("Ec", [128, 2, H * S])
        Pc = sb("Pc", [128, 2, H * S])

        Vaug = sb("Vaug", [128, NT, H, D0 + 1])
        Vg = sb("Vg", [128, 2, TB, G0, 32])
        OS = K2T[:, :, :].rearrange("p j k -> p (j k)")
        QH = sb("QH", [128, T], f32r)
        KH = sb("KH", [128, T], f32r)
        Qt = sb("Qt", [128, T])
        Kt = sb("Kt", [128, T])
        QX = sb("QX", [128, T], f32r)
        QM = sb("QM", [128, 2, T], f32r)
        KX = sb("KX", [128, 2, T], f32r)
        mcol0 = sb("mcol0", [128, TB, 128])
        room = sb("room", [128, 2 * G0 * TB * T])
        P0 = room[:, :].rearrange("p (u j k) -> p u j k", u=2, j=G0)
        Pt = room[:, 0:2 * TB * T].rearrange("p (u k q) -> p u k q", u=2, k=TB)
        uT = room[:, 4096:4096 + B * FC * T].rearrange("p (b j t) -> p b j t", b=B, j=FC)
        gl = room[:, 8192:8192 + 2 * T].rearrange("p (u t) -> p u t", u=2)
        P2T = room[:, 9216:9216 + 2 * 512].rearrange("p (u j t) -> p u j t", u=2, j=4)
        rden0 = sb("rden0", [128, 2, TB * G0])
        O0 = sb("O0", [128, NT, C])
        OT0 = room[:, 10240:10240 + NT * 128]
        tm8 = sb("tm8", [1, B, T], u8)
        eps = sb("eps", [128, NT])
        pool_pad, dve_pad = sb("pool_pad", [128, 1]), sb("dve_pad", [128, 1])
        tmr = sb("tmr", [1, B, T], bf16)
        onehot = sb("onehot", [1, 128], bf16)
        km8 = sb("km8", [128, NT], u8)
        keep = sb("keep", [128, NT])

        ps = ctx.enter_context(nc.psum_tensor("ps", [128, 8, 512], f32))

        consts_loaded, x_loaded, masks_loaded = sem("consts_loaded"), sem("x_loaded"), sem("masks_loaded")
        w0_loaded, wqk_loaded = sem("w0_loaded"), sem("wqk_loaded")
        wa_loaded = [sem("wa_loaded_even"), sem("wa_loaded_odd")]
        cross_loaded, ff_loaded, vec_loaded = sem("cross_loaded"), sem("ff_loaded"), sem("vec_loaded")
        zeroed, setup_done = sem("zeroed"), sem("setup_done")
        dve_step, pool_step, pad_written = sem("dve_step"), sem("pool_step"), sem("pad_written")
        ln_var, ln_rstd, ln_xhat = sem("ln_var"), sem("ln_rstd"), sem("ln_xhat")
        ln_turned, ln_hT, ln_hi, ln_lo = sem("ln_turned"), sem("ln_hT"), sem("ln_hi"), sem("ln_lo")
        bias_added = sem("bias_added")
        bf_done, masks_done = sem("bf_done"), sem("masks_done")
        v0_ready, v0_done = sem("v0_ready"), sem("v0_done")
        blocks_done, qb_ready, cross_bias_done = sem("blocks_done"), sem("qb_ready"), sem("cross_bias_done")
        q0_ready, q0_hi, q0_done = sem("q0_ready"), sem("q0_hi"), sem("q0_done")
        k0_ready, k0_hi, k0_done = sem("k0_ready"), sem("k0_hi"), sem("k0_done")
        d0_ready, d0_max = sem("d0_ready"), sem("d0_max")
        m0_ready, m0_done = sem("m0_ready"), sem("m0_done")
        s0_ready, s0_exp, s0_masked = sem("s0_ready"), sem("s0_exp"), sem("s0_masked")
        vg_done, o0_ready, o0_copied = sem("vg_done"), sem("o0_ready"), sem("o0_copied")
        o0_turned, o0_done = sem("o0_turned"), sem("o0_done")
        ot0_ready, ot0_done, proj_ready, proj_added = sem("ot0_ready"), sem("ot0_done"), sem("proj_ready"), sem("proj_added")
        ab_ready, a_hi_done, a_lo_done, b_done = sem("ab_ready"), sem("a_hi_done"), sem("a_lo_done"), sem("b_done")
        t_ready, t_hi_done, t_lo_done = sem("t_ready"), sem("t_hi_done"), sem("t_lo_done")
        v_ready, v_done = sem("v_ready"), sem("v_done")
        d_ready, d_max, m_ready, m_done = sem("d_ready"), sem("d_max"), sem("m_ready"), sem("m_done")
        s_ready, s_exp = sem("s_ready"), sem("s_exp")
        o_ready, r_done, o_done = sem("o_ready"), sem("r_done"), sem("o_done")
        kv2_ready, kv2_done = sem("kv2_ready"), sem("kv2_done")
        g_ready, g_done, u_ready, u_done = sem("g_ready"), sem("g_done"), sem("u_ready"), sem("u_done")
        c_ready, c_sub, c_exp, c_rec, c_norm = sem("c_ready"), sem("c_sub"), sem("c_exp"), sem("c_rec"), sem("c_norm")
        ct_ready, ct_done, co_ready, c_added = sem("ct_ready"), sem("ct_done"), sem("co_ready"), sem("c_added")
        f_ready, f_gelu, f_u = sem("f_ready"), sem("f_gelu"), sem("f_u")
        fo_ready, ff_added = sem("fo_ready"), sem("ff_added")
        stored = sem("stored")

        block = ctx.enter_context(nc.Block())

        ATTN, CROSS, FF = range(3)
        UNITS = H * B
        TURNS = H // 2
        UNITS0 = NG * B
        LAST = TURNS - 1

        def half_nth(L, part, b):
            return (L * 3 + part) * B + b + 1

        def nth(l, i, k, per, e):
            return (l * UNITS + i * 4 + k) * per + e + 1

        def rows_of(b):
            return slice(b * TB, (b + 1) * TB)

        def cols_of(b):
            return slice(b * T, (b + 1) * T)


        @block.sync
        def _(sp):
            sp.dma_start(cst[:, :], consts).then_inc(consts_loaded, 16)
            sp.dma_start(v0[:, :], vec0).then_inc(consts_loaded, 16)
            sp.dma_start(ctxT[:, :], ctx_t).then_inc(w0_loaded, 16)
            sp.dma_start(wkv0[:, :], wk0).then_inc(w0_loaded, 16)
            sp.dma_start(wl0[:, :], w0).then_inc(w0_loaded, 16)
            sp.dma_start(r0[:, :, :], rows0.partition_broadcast(128)).then_inc(w0_loaded, 16)
            sp.dma_start(wqk[:, :], w0_qk[0, :, :]).then_inc(wqk_loaded, 16)

            def layer_loads(l, first):
                layer = bass.ds(l, 1)
                if not first:
                    sp.wait_ge(u_done, (l + 1) * 2)
                sp.dma_start(wc[:, :, :], w_ctx[layer, :, :].rearrange("a p (k n) -> (a p) k n", k=2))\
                  .then_inc(cross_loaded, 16)
                sp.dma_start(wx[:, :, :], w_cross[layer, :, :].rearrange("a p (k n) -> (a p) k n", k=H // 2))\
                  .then_inc(cross_loaded, 16)
                for h in range(2):
                    if not first:
                        sp.wait_ge(ab_ready, l * H)
                    sp.dma_start(wa[:, h, :], w_attn[layer, h, :, :].rearrange("a d n -> (a d) n"))\
                      .then_inc(wa_loaded[h], 16)
                if not first:
                    sp.wait_ge(ff_added, (l + 1) * B)
                sp.dma_start(vl[:, :], vec[layer, :, :].rearrange("a p n -> (a p) n")).then_inc(vec_loaded, 16)
                sp.dma_start(rl[:, :, :], rows[layer, :, :].rearrange("a r c -> (a r) c").partition_broadcast(128))\
                  .then_inc(vec_loaded, 16)
                sp.dma_start(wf[:, :], w_ff[layer, :, :].rearrange("a p n -> (a p) n")).then_inc(ff_loaded, 16)
                with sp.Fori(1, TURNS) as i:
                    for h in range(2):
                        sp.wait_ge(ab_ready, l * H + i * 2 + h - 1)
                        sp.dma_start(wa[:, h, :],
                                     w_attn[layer, bass.ds(i * 2 + h, 1), :, :].rearrange("a b d n -> (a b d) n"))\
                          .then_inc(wa_loaded[h], 16)

            with sp.Fori(1, NG) as g:
                sp.wait_ge(k0_done, g * B)
                sp.dma_start(wqk[:, :], w0_qk[bass.ds(g, 1), :, :].rearrange("a p n -> (a p) n"))\
                  .then_inc(wqk_loaded, 16)
            layer_loads(0, True)
            with sp.Fori(1, LOOP_LAYERS) as l:
                layer_loads(l, False)
            for b in range(B):
                sp.wait_ge(ff_added, LOOP_LAYERS * B + b + 1)
                sp.dma_start(out_dram[:, rows_of(b), :], x[:, rows_of(b), :]).then_inc(stored, 16)
            sp.wait_ge(stored, 16 * B)

        @block.gpsimd
        def _(pool):
            steps = Steps(pool, pool_step)
            with nc.allow_non_contiguous_dma(reason="a mask of one byte per token, tokens onto partitions"):
                pool.dma_start(km8[:, :], tgt_mask.rearrange("b (t p) -> p (b t)", p=128)).then_inc(masks_loaded, 16)
            pool.dma_start(tm8[:, :, :], tgt_mask.rearrange("(a b) t -> a b t", a=1)).then_inc(masks_loaded, 16)
            pool.dma_start(em8[:, :, :], enc_mask.rearrange("(a b) s -> a b s", a=1)).then_inc(masks_loaded, 16)
            pool.memset(mhalf[:, :], -0.5).then_inc(zeroed, 1)
            pool.memset(eps[:, :], EPS).then_inc(zeroed, 1)
            pool.memset(pool_pad[:, :], 0.0).then_inc(pad_written, 1)
            pool.memset(spread[:, :].bitcast(f32), 0.0).then_inc(zeroed, 1)
            pool.memset(onehot[:, :], 0.0).then_inc(zeroed, 1)
            pool.wait_ge(zeroed, 4)
            pool.memset(mcol0[:, :, :], 0.0).then_inc(setup_done, 1)
            pool.memset(Vg[:, :, :, :, :], 0.0).then_inc(setup_done, 1)
            pool.memset(mrow[:, :].bitcast(f32), 0.0).then_inc(setup_done, 1)
            pool.memset(V1[:, :, :, C:C + 1], 1.0).then_inc(setup_done, 1)
            pool.memset(ones_row[:, :], 1.0).then_inc(setup_done, 1)
            pool.memset(spread[0:TB, :].bitcast(f32), 1.0).then_inc(setup_done, 1)
            pool.memset(onehot[:, :].rearrange("p (j r) -> p j r", r=32)[:, :, ROW_MASK:ROW_MASK + 1], 1.0)\
                .then_inc(setup_done, 1)

            def inverse_std(L, part):
                for b in range(B):
                    pool.wait_ge(ln_var, half_nth(L, part, b))
                    steps.add(pool.tensor_tensor(veps[:, rows_of(b)], mv[:, rows_of(b), 1], eps[:, rows_of(b)],
                                                 ALU.add))
                    steps.wait()
                    pool.tensor_tensor(rstd[:, rows_of(b)], veps[:, rows_of(b)], mhalf[:, rows_of(b)], ALU.pow)\
                        .then_inc(ln_rstd, 1)

            def add_bias(L, part, row):
                for b in range(B):
                    pool.wait_ge(ln_xhat, half_nth(L, part, b))
                    pool.tensor_tensor(x[:, rows_of(b), :], x[:, rows_of(b), :],
                                       row.unsqueeze(1).to_broadcast([128, TB, C]), ALU.add).then_inc(bias_added, 1)

            def normalise_cross(L):
                for n in range(NT):
                    pool.wait_ge(c_rec, L * NT + n + 1)
                    p = Pc[:, n % 2, :].rearrange("p (h s) -> p h s", s=S)
                    pool.tensor_tensor(p, p, crec[:, n % 2, :].unsqueeze(2).to_broadcast([128, H, S]),
                                       ALU.mult).then_inc(c_norm, 1)

            def zero_diagonal(u, b):
                for t in range(TB):
                    pool.wait_ge(s0_exp, (u * TB + t) * 2 + 2)
                    pool.wait_ge(pad_written, u * TB + t + 1)
                    pool.tensor_tensor(pool_pad[:, :], mhalf[:, 0:1], mhalf[:, 0:1], ALU.add)\
                        .then_inc(pad_written, 1)
                    blk = P0[:, b, :, t * T + t * 128:t * T + (t + 1) * 128]
                    pool.affine_select(out=blk, in_=blk, compare_op=ALU.is_ge, fill=0.0, base=0,
                                       pattern=[[0, G0], [1, 128]], channel_multiplier=-1).then_inc(s0_masked, 1)

            inverse_std(0, ATTN)
            pool.wait_ge(w0_loaded, 64)
            add_bias(0, ATTN, r0[:, 1, :])
            with pool.Fori(0, NG) as g:
                for b in range(B):
                    zero_diagonal(g * B + b, b)
            inverse_std(0, CROSS)
            add_bias(0, CROSS, r0[:, 2, :])
            normalise_cross(0)
            inverse_std(0, FF)
            add_bias(0, FF, r0[:, 3, :])
            with pool.Fori(0, LOOP_LAYERS) as l:
                kept = steps.enter(l, 3 * B)
                for part in (ATTN, CROSS, FF):
                    inverse_std(l + 1, part)
                    if part == ATTN:
                        pool.wait_ge(vec_loaded, l * 32 + 32)
                    add_bias(l + 1, part, rl[:, part, :])
                    if part == CROSS:
                        normalise_cross(l + 1)
                steps.leave(kept, LOOP_LAYERS)

        @block.scalar
        def _(act):
            for b in range(B):
                act.dma_start(x[:, rows_of(b), :], x_dram[:, rows_of(b), :]).then_inc(x_loaded, 16)

            def finish_ln(L, part, scale, bias, l=None):
                for b in range(B):
                    act.wait_ge(ln_turned, half_nth(L, part, b))
                    act.activation(hT[:, cols_of(b)], ps[:, 6 + b, :], ACT.Identity, bias=bias, scale=scale)\
                       .then_inc(ln_hT, 1)
                    if l is not None:
                        act.activation(hTh[:, cols_of(b)], ps[:, 6 + b, :], ACT.Identity, bias=bias, scale=scale)\
                           .then_inc(ln_hi, 1)

            def turn_out(L, n):
                act.wait_ge(ct_ready, L * NT + n + 1)
                if n >= 2:
                    act.wait_ge(co_ready, L * NT + n - 1)
                act.activation(P2T[:, n % 2, :, :].rearrange("p j t -> p (j t)"), ps[:, 2 + n % 2, :],
                               ACT.Copy).then_inc(ct_done, 1)

            def cross_act(L, scale):
                for n in range(NT):
                    act.wait_ge(c_sub, L * NT + n + 1)
                    if n >= 2:
                        act.wait_ge(ct_ready, L * NT + n - 1)
                    act.activation(Pc[:, n % 2, :], Ec[:, n % 2, :], ACT.Exp, scale=scale).then_inc(c_exp, 1)
                    if n >= 1:
                        turn_out(L, n - 1)
                turn_out(L, NT - 1)

            act.wait_ge(consts_loaded, 32)
            act.wait_ge(kv2_ready, 1)
            act.activation(K2T[:, 0, :], ps[:, 4, 0:B * S], ACT.Identity, bias=v0[:, 10:11]).then_inc(kv2_done, 1)
            act.activation(V2T[:, 0, :], ps[:, 4, B * S:2 * B * S], ACT.Identity, bias=v0[:, 11:12])\
               .then_inc(kv2_done, 1)
            finish_ln(0, ATTN, v0[:, 0:1], v0[:, 1:2])
            for b in range(B):
                act.wait_ge(g_ready, b + 1)
                act.activation(Gm[:, b, :], ps[:, b, :], ACT.Copy).then_inc(g_done, 1)
            for b in range(B):
                act.wait_ge(u_ready, b + 1)
                act.activation(Um[:, b, :, :].rearrange("p j c -> p (j c)"), ps[:, 4 + b, :], ACT.Copy)\
                   .then_inc(u_done, 1)

            def q_hi(u):
                act.wait_ge(q0_ready, u + 1)
                act.activation(QH[:, :], ps[:, 6, :], ACT.Identity, bias=wqk[:, 256:257]).then_inc(q0_hi, 1)

            def k_hi(u):
                act.wait_ge(k0_ready, u + 1)
                act.activation(KH[:, :], ps[:, 6, :], ACT.Identity, bias=wqk[:, 257:258]).then_inc(k0_hi, 1)

            def exps0(u, b, t):
                for j2 in range(2):
                    act.wait_ge(s0_ready, (u * TB + t) * 2 + j2 + 1)
                    act.activation(P0[:, b, 2 * j2:2 * j2 + 2, t * T + t * 128:(t + 1) * T],
                                   ps[:, 2 + 2 * j2:4 + 2 * j2, 0:T - t * 128], ACT.Exp, scale=SCALE0)\
                       .then_inc(s0_exp, 1)

            def sums_out(u):
                act.wait_ge(o0_ready, u + 1)
                act.activation(OS, ps[:, 7, :], ACT.Copy).then_inc(o0_copied, 1)

            def unit0_act(u, b, first=False, last=False):
                if not last:
                    q_hi(u + 1)
                exps0(u, b, 0)
                if not last:
                    k_hi(u + 1)
                for t in range(1, TB):
                    exps0(u, b, t)
                if not first:
                    sums_out(u - 1)

            q_hi(0)
            k_hi(0)
            unit0_act(0, 0, first=True)
            unit0_act(1, 1)
            with act.Fori(1, NG - 1) as g:
                for b in range(B):
                    unit0_act(g * B + b, b)
            for b in range(B):
                unit0_act(UNITS0 - B + b, b, last=b == B - 1)
            sums_out(UNITS0 - 1)
            for b in range(B):
                act.wait_ge(ot0_ready, b + 1)
                act.activation(OT0[:, cols_of(b)], ps[:, b, :], ACT.Copy).then_inc(ot0_done, 1)
            finish_ln(0, CROSS, v0[:, 2:3], v0[:, 3:4])
            cross_act(0, SCALE0)
            finish_ln(0, FF, v0[:, 4:5], v0[:, 5:6])
            for b in range(B):
                for j in range(FC):
                    n = b * FC + j
                    act.wait_ge(f_ready, n + 1)
                    act.activation(uT[:, b, j, :], ps[:, 2 * (n % 2), :], ACT.Gelu, bias=v0[:, 6 + j:7 + j])\
                       .then_inc(f_gelu, 1)

            with act.Fori(0, LOOP_LAYERS) as l:
                for n, dst in enumerate((K2T, V2T)):
                    act.wait_ge(kv2_ready, 1 + l * 2 + n + 1)
                    act.activation(dst[:, :, :].rearrange("p j k -> p (j k)"), ps[:, n, :], ACT.Copy)\
                       .then_inc(kv2_done, 1)
                for r in range(2):
                    act.wait_ge(g_ready, B + l * 2 + r + 1)
                    for b in range(B):
                        src = ps[:, 2 + r, :].rearrange("p (j b s) -> p j b s", b=B, s=S)[:, :, b, :]
                        half = Gm[:, b, r * 256:(r + 1) * 256].rearrange("p (j s) -> p j s", s=S)
                        act.activation(half, src, ACT.Copy).then_inc(g_done, 1)
                for r in range(2):
                    act.wait_ge(u_ready, B + l * 2 + r + 1)
                    act.activation(Um[:, :, 2 * r:2 * r + 2, :],
                                   ps[:, 4 + r, :].rearrange("p (b j c) -> p b j c", b=B, j=2), ACT.Copy)\
                       .then_inc(u_done, 1)
                act.wait_ge(vec_loaded, l * 32 + 32)
                finish_ln(l + 1, ATTN, vl[:, 0:1], vl[:, 1:2], l)

                def fold(h, e):
                    act.wait_ge(ab_ready, h + 1)
                    act.activation(A_hi[:, e, :], ps[:, 6, 0:C], ACT.Copy).then_inc(a_hi_done, 1)
                    act.activation(Bm[:, e, :], ps[:, 6, C:2 * C], ACT.Copy).then_inc(b_done, 1)

                def t_hi(i, k):
                    act.wait_ge(t_ready, nth(l, i, k, 1, 0))
                    act.activation(T_hi[:, k % 2, :], ps[:, 6, :], ACT.Copy).then_inc(t_hi_done, 1)

                def v_out(i, k):
                    act.wait_ge(v_ready, nth(l, i, k, 1, 0))
                    act.activation(V1[:, k % 4, :, 0:C], ps[:, 6, :].rearrange("p (t c) -> p t c", c=C),
                                   ACT.Copy).then_inc(v_done, 1)

                def exps(i, k, e):
                    act.wait_ge(s_ready, nth(l, i, k, 2, e))
                    act.activation(Pt[:, k % 2, 2 * e:2 * e + 2, :], ps[:, 2 * e:2 * e + 2, :], ACT.Exp,
                                   scale=SCALE).then_inc(s_exp, 1)

                def unit(i, k, last=False):
                    if not last:
                        t_hi(i, k + 1)
                    exps(i, k, 0)
                    if k % 2 == 0 and not (k == 2 and i is LAST):
                        fold(l * H + i * 2 + k // 2 + 1, (k // 2 + 1) % 2)
                    exps(i, k, 1)
                    if not last:
                        v_out(i, k + 1)

                fold(l * H, 0)
                t_hi(0, 0)
                v_out(0, 0)
                with act.Fori(0, LAST) as i:
                    for k in range(4):
                        unit(i, k)
                for k in range(4):
                    unit(LAST, k, last=k == 3)
                finish_ln(l + 1, CROSS, vl[:, 2:3], vl[:, 3:4])
                cross_act(l + 1, SCALE)
                finish_ln(l + 1, FF, vl[:, 4:5], vl[:, 5:6])
                for b in range(B):
                    for j in range(FC):
                        n = b * FC + j
                        act.wait_ge(f_ready, (l + 1) * B * FC + n + 1)
                        act.activation(gl[:, n % 2, :], ps[:, 2 * (n % 2), :], ACT.Gelu, bias=vl[:, 10 + j:11 + j])\
                           .then_inc(f_gelu, 1)

        @block.vector
        def _(dve):
            steps = Steps(dve, dve_step)

            def layer_norm(L, part, x_ready, x_nth, l=None):
                for b in range(B):
                    dve.wait_ge(x_ready, x_nth(b))
                    for n in range(b * TB, (b + 1) * TB):
                        ins = dve.bn_stats(stats[:, n, :], x[:, n, :])
                    steps.add(ins)
                    steps.wait()
                    dve.memset(dve_pad[:, :], 0.0)
                    for n in range(b * TB, (b + 1) * TB):
                        ins = dve.bn_aggr(mv[:, n, :], stats[:, n, :])
                    ins.then_inc(ln_var, 1)
                for b in range(B):
                    dve.wait_ge(ln_rstd, half_nth(L, part, b))
                    for n in range(b * TB, (b + 1) * TB):
                        ins = dve.tensor_scalar(xhat[:, n, :], x[:, n, :], mv[:, n, 0:1], rstd[:, n:n + 1],
                                                ALU.subtract, ALU.mult)
                    ins.then_inc(ln_xhat, 1)
                if l is not None:
                    for b in range(B):
                        dve.wait_ge(ln_hT, half_nth(L, part, b))
                        dve.wait_ge(ln_hi, l * B + b + 1)
                        dve.tensor_tensor(hTl[:, cols_of(b)], hT[:, cols_of(b)], hTh[:, cols_of(b)].bitcast(f32),
                                          ALU.subtract).then_inc(ln_lo, 1)

            def cross_dve(L):
                def softmax(n):
                    dve.wait_ge(c_ready, L * NT + n + 1)
                    sc = ps[:, n % 2, :].rearrange("p (h s) -> p h s", s=S)
                    steps.add(dve.tensor_reduce(cmax[:, n % 2, :], sc, X, ALU.max))
                    steps.wait()
                    if n >= 2:
                        dve.wait_ge(c_exp, L * NT + n - 1)
                    dve.tensor_tensor(Ec[:, n % 2, :].rearrange("p (h s) -> p h s", s=S), sc,
                                      cmax[:, n % 2, :].unsqueeze(2).to_broadcast([128, H, S]),
                                      ALU.subtract).then_inc(c_sub, 1)

                def sums(n):
                    dve.wait_ge(c_exp, L * NT + n + 1)
                    steps.add(dve.tensor_reduce(csum[:, n % 2, :],
                                                Pc[:, n % 2, :].rearrange("p (h s) -> p h s", s=S), X, ALU.add))
                    steps.wait()
                    if n >= 2:
                        dve.wait_ge(c_norm, L * NT + n - 1)
                    dve.reciprocal(crec[:, n % 2, :], csum[:, n % 2, :]).then_inc(c_rec, 1)

                def add_out(n):
                    dve.wait_ge(bias_added, half_nth(L, CROSS, n // TB))
                    dve.wait_ge(co_ready, L * NT + n + 1)
                    dve.tensor_tensor(x[:, n, :], ps[:, 4 + n % 2, 0:C], x[:, n, :], ALU.add).then_inc(c_added, 1)

                for n in range(NT):
                    softmax(n)
                    if n >= 1:
                        sums(n - 1)
                    if n >= 3:
                        add_out(n - 3)
                sums(NT - 1)
                for n in range(NT - 3, NT):
                    add_out(n)

            def ff_out(L):
                for b in range(B):
                    dve.wait_ge(bias_added, half_nth(L, FF, b))
                    dve.wait_ge(fo_ready, L * B + b + 1)
                    dve.tensor_tensor(x[:, rows_of(b), :], ps[:, 4 + b, :].rearrange("p (t c) -> p t c", c=C),
                                      x[:, rows_of(b), :], ALU.add).then_inc(ff_added, 1)

            dve.wait_ge(consts_loaded, 32)
            dve.tensor_copy(ident_bf[:, :], ident).then_inc(bf_done, 1)
            dve.tensor_copy(tri_bf[:, :], tri).then_inc(bf_done, 1)
            layer_norm(0, ATTN, x_loaded, lambda b: 32)
            dve.wait_ge(masks_loaded, 48)
            dve.tensor_scalar(tmr[:, :, :], tm8[:, :, :], -BIG, None, ALU.mult).then_inc(masks_done, 1)
            steps.add(dve.tensor_scalar(keep[:, :], km8[:, :], -1.0, 1.0, ALU.mult, ALU.add))
            steps.add(dve.tensor_scalar(em[:, :, :], em8[:, :, :], -BIG, None, ALU.mult))
            steps.add(dve.tensor_scalar(keepn[:, :, :], em8[:, :, :], -1.0, 1.0, ALU.mult, ALU.add))
            steps.wait()
            steps.add(dve.tensor_reduce(poison[:, 0:B], keepn[:, :, :], X, ALU.add))
            steps.wait()
            steps.add(dve.reciprocal(poison[:, B:2 * B], poison[:, 0:B]))
            steps.wait()
            steps.add(dve.tensor_scalar(poison[:, 2 * B:3 * B], poison[:, B:2 * B], 0.0, None, ALU.mult))
            dve.wait_ge(kv2_done, 2)
            for b in range(B):
                for src, dst in ((K2T, Ec), (V2T, Pc)):
                    ins = dve.tensor_tensor(dst[:, b, :].rearrange("p (h s) -> p h s", s=S),
                                            src[:, 0, b * S:(b + 1) * S].unsqueeze(1).to_broadcast([128, H, S]),
                                            head_mask.unsqueeze(2).to_broadcast([128, H, S]), ALU.mult)
                ins.then_inc(blocks_done, 1)
            dve.wait_ge(w0_loaded, 64)
            for b in range(B):
                dve.wait_ge(v0_ready, b + 1)
                for t in range(TB):
                    ins = dve.tensor_tensor(Vaug[:, b * TB + t, :, 0:D0],
                                            ps[:, 2 + b, t * C:(t + 1) * C].rearrange("p (h d) -> p h d", d=D0),
                                            r0[:, 0, :].rearrange("p (h d) -> p h d", d=D0), ALU.add)
                steps.add(ins)
                steps.wait()
                for t in range(TB):
                    n = b * TB + t
                    dve.tensor_scalar(Vaug[:, n, :, 0:D0], Vaug[:, n, :, 0:D0], keep[:, n:n + 1], None, ALU.mult)
                    ins = dve.tensor_copy(Vaug[:, n, :, D0], keep[:, n:n + 1].to_broadcast([128, H]))
                ins.then_inc(v0_done, 1)
            for b in range(B):
                dve.wait_ge(qb_ready, b + 1)
                steps.add(dve.tensor_tensor(cross_bias[:, b, :].rearrange("p (h s) -> p h s", s=S),
                                            ps[0:1, 6 + b, :].rearrange("p (h s) -> p h s", s=S),
                                            em[:, b, :].unsqueeze(1).to_broadcast([1, H, S]), ALU.add))
                steps.wait()
                dve.tensor_scalar(cross_bias[:, b, :], cross_bias[:, b, :], poison[:, 2 * B + b:2 * B + b + 1], None,
                                  ALU.add).then_inc(cross_bias_done, 1)

            def q_part(u):
                dve.wait_ge(q0_hi, u + 1)
                steps.add(dve.tensor_scalar(Qt[:, :], ps[:, 6, :], wqk[:, 256:257], tQ, ALU.add, ALU.mult))
                steps.wait()
                dve.scalar_tensor_tensor(out=QX[:, :], in0=QH[:, :].bitcast(f32), scalar=sQ, in1=Qt[:, :],
                                         op0=ALU.mult, op1=ALU.add).then_inc(q0_done, 1)

            def k_part(u, parity):
                dve.wait_ge(k0_hi, u + 1)
                steps.add(dve.tensor_scalar(Kt[:, :], ps[:, 6, :], wqk[:, 257:258], tK, ALU.add, ALU.mult))
                steps.wait()
                dve.scalar_tensor_tensor(out=KX[:, parity, :], in0=KH[:, :].bitcast(f32), scalar=sK, in1=Kt[:, :],
                                         op0=ALU.mult, op1=ALU.add).then_inc(k0_done, 1)

            mcol0_heads = mcol0[:, :, :].rearrange("p t (j r) -> p t j r", r=32)

            def maxima0(u):
                for t in range(TB):
                    for j2 in range(2):
                        dve.wait_ge(d0_ready, (u * TB + t) * 2 + j2 + 1)
                        dve.tensor_reduce(mcol0_heads[:, t, 2 * j2:2 * j2 + 2, ROW_MAX], ps[:, 0:2, 0:(t + 1) * 128],
                                          X, ALU.max, negate=True).then_inc(d0_max, 1)

            def outputs0(u, heads, cols, b):
                dve.wait_ge(o0_turned, u + 1)
                o = ps[:, 7, :].rearrange("p (t j d) -> p t j d", j=G0, d=32)
                r = rden0[:, b, :].rearrange("p (t j) -> p t j", j=G0)
                steps.add(dve.reciprocal(r, o[:, :, :, D0]))
                steps.wait()
                for t in range(TB):
                    ins = dve.tensor_tensor(O0[:, b * TB + t, cols].rearrange("p (j d) -> p j d", d=D0),
                                            o[:, t, :, 0:D0], r[:, t, :].unsqueeze(2).to_broadcast([128, G0, D0]),
                                            ALU.mult)
                ins.then_inc(o0_done, 1)

            def values_of(u, g, b):
                if isinstance(u, int) and u < 2:
                    pass
                else:
                    dve.wait_ge(o0_ready, u - 1)
                for t in range(TB):
                    ins = dve.tensor_copy(Vg[:, b, t, :, 0:D0 + 1], Vaug[:, b * TB + t, heads_at(g), :])
                ins.then_inc(vg_done, 1)

            def heads_at(g):
                return bass.ds(g * G0, G0)

            def cols_at(g):
                return bass.ds(g * (G0 * D0), G0 * D0)

            def unit0(g, b, first=False, last=False, normalise=True):
                u = g * B + b
                dve.wait_ge(m0_ready, u + 1)
                dve.tensor_tensor(QM[:, b, :], ps[:, 6, :], QX[:, :].bitcast(f32), ALU.add).then_inc(m0_done, 1)
                if normalise:
                    outputs0(u - 2, heads_at(g - 1), cols_at(g - 1), b)
                if not last:
                    dve.wait_ge(m0_done, u + 1)
                    q_part(u + 1)
                    k_part(u + 1, (b + 1) % 2)
                values_of(u, g, b)
                if not last:
                    maxima0(u + 1)

            dve.wait_ge(setup_done, 7)
            dve.wait_ge(wqk_loaded, 16)
            q_part(0)
            k_part(0, 0)
            maxima0(0)
            unit0(0, 0, first=True, normalise=False)
            unit0(0, 1, normalise=False)
            with dve.Fori(1, NG - 1) as g:
                kept = steps.enter(g - 1, 6)
                unit0(g, 0)
                unit0(g, 1)
                steps.leave(kept, NG - 2)
            unit0(NG - 1, 0)
            unit0(NG - 1, 1, last=True)
            for b in range(B):
                outputs0(UNITS0 - B + b, heads_at(NG - 1), cols_at(NG - 1), b)
            for b in range(B):
                dve.wait_ge(bias_added, half_nth(0, ATTN, b))
                dve.wait_ge(proj_ready, b + 1)
                dve.tensor_tensor(x[:, rows_of(b), :], ps[:, 2 + b, :].rearrange("p (t c) -> p t c", c=C),
                                  x[:, rows_of(b), :], ALU.add).then_inc(proj_added, 1)
            layer_norm(0, CROSS, proj_added, lambda b: b + 1)
            cross_dve(0)
            layer_norm(0, FF, c_added, lambda b: (b + 1) * TB)
            ff_out(0)

            with dve.Fori(0, LOOP_LAYERS) as l:
                kept_l = steps.enter(l, 3 * B + 2 * NT)
                layer_norm(l + 1, ATTN, ff_added, lambda b: l * B + b + 1, l)

                def fold(h, e):
                    dve.wait_ge(b_done, h + 1)
                    dve.tensor_tensor(A_lo[:, e, :], ps[:, 6, 0:C], A_hi[:, e, :].bitcast(f32),
                                      ALU.subtract).then_inc(a_lo_done, 1)

                def t_lo(i, k):
                    dve.wait_ge(t_hi_done, nth(l, i, k, 1, 0))
                    dve.tensor_tensor(T_lo[:, k % 2, :], ps[:, 6, :], T_hi[:, k % 2, :].bitcast(f32),
                                      ALU.subtract).then_inc(t_lo_done, 1)

                def maximum(i, k, t):
                    dve.wait_ge(d_ready, nth(l, i, k, TB, t))
                    dve.tensor_reduce(mcol[:, t:t + 1], ps[:, 4 + t % 2, :], X, ALU.max, negate=True)\
                       .then_inc(d_max, 1)

                def output(i, k, pair):
                    o = ps[:, 7, :].rearrange("p (t n) -> p t n", t=2)
                    dve.wait_ge(o_ready, nth(l, i, k, 2, pair))
                    dve.reciprocal(rden[:, k % 2, 2 * pair:2 * pair + 2], o[:, :, C]).then_inc(r_done, 1)
                    dve.wait_ge(r_done, nth(l, i, k, 2, pair))
                    for t in range(2 * pair, 2 * pair + 2):
                        n = (k % 2) * TB + t
                        ins = dve.scalar_tensor_tensor(out=x[:, n, :], in0=o[:, t % 2, 0:C],
                                                       scalar=rden[:, k % 2, t:t + 1], in1=x[:, n, :],
                                                       op0=ALU.mult, op1=ALU.add)
                    ins.then_inc(o_done, 1)

                def unit(i, k, first=False, last=False):
                    before = (i, k - 1)
                    dve.wait_ge(m_ready, nth(l, i, k, 1, 0))
                    dve.tensor_tensor(mrow[0:TB, :].rearrange("p (t q) -> p t q", t=TB),
                                      ps[0:TB, 4, 0:128].unsqueeze(1).to_broadcast([TB, TB, 128]),
                                      ident[0:TB, 0:TB].unsqueeze(2).to_broadcast([TB, TB, 128]), ALU.mult)\
                       .then_inc(m_done, 1)
                    if not first:
                        output(*before, 0)
                    if not last:
                        t_lo(i, k + 1)
                        maximum(i, k + 1, 0)
                        maximum(i, k + 1, 1)
                        if k % 2 == 0 and not (k == 2 and i is LAST):
                            fold(l * H + i * 2 + k // 2 + 1, (k // 2 + 1) % 2)
                        maximum(i, k + 1, 2)
                        maximum(i, k + 1, 3)
                    if not first:
                        output(*before, 1)

                dve.wait_ge(bias_added, half_nth(l + 1, ATTN, B - 1))
                fold(l * H, 0)
                t_lo(0, 0)
                for t in range(TB):
                    maximum(0, 0, t)
                for k in range(4):
                    unit(0, k, first=k == 0)
                with dve.Fori(1, LAST) as i:
                    for k in range(4):
                        unit(i, k)
                for k in range(4):
                    unit(LAST, k, last=k == 3)
                for pair in range(2):
                    output(LAST, 3, pair)
                layer_norm(l + 1, CROSS, o_done, lambda b: nth(l, LAST, 2 + b, 2, 1))
                cross_dve(l + 1)
                layer_norm(l + 1, FF, c_added, lambda b: (l + 1) * NT + (b + 1) * TB)
                for b in range(B):
                    for j in range(FC):
                        n = b * FC + j
                        dve.wait_ge(f_gelu, (l + 1) * B * FC + n + 1)
                        dve.scalar_tensor_tensor(out=uT[:, b, j, :], in0=ps[:, 2 * (n % 2) + 1, :],
                                                 scalar=vl[:, 6 + j:7 + j], in1=gl[:, n % 2, :],
                                                 op0=ALU.add, op1=ALU.mult).then_inc(f_u, 1)
                ff_out(l + 1)
                steps.leave(kept_l, LOOP_LAYERS)

        @block.tensor
        def _(pe):
            def turn_ln(L, part):
                for b in range(B):
                    pe.wait_ge(ln_xhat, half_nth(L, part, b))
                    for t in range(TB):
                        mm = pe.transpose(ps[:, 6 + b, t * 128:(t + 1) * 128], xhat[:, b * TB + t, :], ident)
                    mm.then_inc(ln_turned, 1)

            def cross_pe(L, with_bias):
                def scores(n):
                    b = n // TB
                    if n % TB == 0:
                        pe.wait_ge(ln_hT, half_nth(L, CROSS, b))
                    if n >= 2:
                        pe.wait_ge(c_sub, L * NT + n - 1)
                    mm = pe.matmul(ps[:, n % 2, :], hT[:, n * 128:(n + 1) * 128], Gm[:, b, :], start=True,
                                   stop=not with_bias)
                    if with_bias:
                        mm = pe.matmul(ps[:, n % 2, :], ones_row[:, :], cross_bias[:, b, :], start=False, stop=True)
                    mm.then_inc(c_ready, 1)

                def turn(n):
                    pe.wait_ge(c_norm, L * NT + n + 1)
                    if n >= 2:
                        pe.wait_ge(ct_done, L * NT + n - 1)
                    for j in range(4):
                        mm = pe.transpose(ps[:, 2 + n % 2, j * 128:(j + 1) * 128], Pc[:, n % 2, j * 128:(j + 1) * 128],
                                          ident)
                    mm.then_inc(ct_ready, 1)

                def outs(n):
                    pe.wait_ge(ct_done, L * NT + n + 1)
                    if n >= 2:
                        pe.wait_ge(c_added, L * NT + n - 1)
                    for j in range(4):
                        mm = pe.matmul(ps[:, 4 + n % 2, 0:C], P2T[:, n % 2, j, :], Um[:, n // TB, j, :],
                                       start=j == 0, stop=j == 3)
                    mm.then_inc(co_ready, 1)

                scores(0)
                scores(1)
                for n in range(NT):
                    turn(n)
                    if n + 2 < NT:
                        scores(n + 2)
                    if n >= 1:
                        outs(n - 1)
                outs(NT - 1)

            def ff_pe(L, hidden, w_out, used):
                def outs(b):
                    pe.wait_ge(*used(b * FC + FC - 1))
                    for t in range(TB):
                        for j in range(FC):
                            mm = pe.matmul(ps[:, 4 + b, t * C:(t + 1) * C], uT[:, b, j, t * 128:(t + 1) * 128],
                                           w_out[:, j, :], start=j == 0, stop=j == FC - 1)
                    mm.then_inc(fo_ready, 1)

                def hid(n):
                    b, j = n // FC, n % FC
                    if j == 0:
                        pe.wait_ge(ln_hT, half_nth(L, FF, b))
                    if n >= 2:
                        pe.wait_ge(*used(n - 2))
                    for bank, w in hidden(n, j):
                        mm = pe.matmul(ps[:, bank, :], w, hT[:, cols_of(b)], start=True, stop=True)
                    mm.then_inc(f_ready, 1)

                for n in range(FC + 2):
                    hid(n)
                outs(0)
                for n in range(FC + 2, 2 * FC):
                    hid(n)
                outs(1)

            pe.wait_ge(w0_loaded, 64)
            pe.matmul(ps[:, 4, 0:B * S], wkv0[:, 0:C], ctxT[:, :], start=True, stop=True)
            pe.matmul(ps[:, 4, B * S:2 * B * S], wkv0[:, C:2 * C], ctxT[:, :], start=True, stop=True)\
              .then_inc(kv2_ready, 1)
            pe.wait_ge(consts_loaded, 32)
            turn_ln(0, ATTN)
            for b in range(B):
                pe.wait_ge(ln_hT, b + 1)
                for t in range(TB):
                    n = b * TB + t
                    mm = pe.matmul(ps[:, 2 + b, t * C:(t + 1) * C], hT[:, n * 128:(n + 1) * 128], w0_v, start=True,
                                   stop=True)
                mm.then_inc(v0_ready, 1)
            for b in range(B):
                pe.wait_ge(blocks_done, b + 1)
                pe.matmul(ps[:, b, :], w0_qT, Ec[:, b, :], start=True, stop=True).then_inc(g_ready, 1)
                pe.matmul(ps[0:1, 6 + b, :], v0[:, 12:13], Ec[:, b, :], start=True, stop=True).then_inc(qb_ready, 1)
            for b in range(B):
                for j in range(4):
                    mm = pe.matmul(ps[:, 4 + b, j * C:(j + 1) * C], Pc[:, b, j * 128:(j + 1) * 128], w0_out,
                                   start=True, stop=True)
                mm.then_inc(u_ready, 1)

            def q_proj(u, b):
                pe.matmul(ps[:, 6, :], wqk[:, 0:128], hT[:, cols_of(b)], start=True, stop=True).then_inc(q0_ready, 1)

            def k_proj(u, b):
                pe.wait_ge(q0_done, u + 1)
                pe.matmul(ps[:, 6, :], wqk[:, 128:256], hT[:, cols_of(b)], start=True, stop=False)
                pe.matmul(ps[:, 6, :], onehot[:, :], tmr[:, b, :], start=False, stop=True).then_inc(k0_ready, 1)

            def row_max_scores(u, b, t, j2, fresh):
                if t == 0 and j2 == 0:
                    pe.wait_ge(k0_done, u + 1)
                if not fresh:
                    pe.wait_ge(d0_max, (u * TB + t) * 2 + j2)
                w = (t + 1) * 128
                for jj in range(2):
                    rows_j = slice(32 * (2 * j2 + jj), 32 * (2 * j2 + jj) + 32)
                    pe.matmul(ps[:, jj, 0:w], QX[rows_j, t * 128:w], KX[rows_j, b, 0:w], start=True, stop=False)
                for jj in range(2):
                    mm = pe.matmul(ps[:, jj, w - 128:w], ident_bf[:, :], tri_bf[:, :], start=False, stop=True)
                mm.then_inc(d0_ready, 1)

            def turned_scores(u, b, t, fresh):
                for j2 in range(2):
                    if not (fresh and t == 0):
                        pe.wait_ge(s0_exp, (u * TB + t) * 2 + j2 - 1)
                    for jj in range(2):
                        rows_j = slice(32 * (2 * j2 + jj), 32 * (2 * j2 + jj) + 32)
                        mm = pe.matmul(ps[:, 2 + 2 * j2 + jj, 0:T - t * 128], KX[rows_j, b, t * 128:(t + 1) * 128],
                                       QM[rows_j, b, t * 128:T], start=True, stop=True)
                    mm.then_inc(s0_ready, 1)

            pieces0 = [(j, s) for j in range(G0) for s in range(TB)]

            def weighted0(b, pieces):
                for j, s in pieces:
                    mm = pe.matmul(ps[32 * j:32 * j + 32, 7, s * 128:T], Vg[:, b, s, j, :],
                                   P0[:, b, j, s * T + s * 128:(s + 1) * T], start=s == 0, stop=s == TB - 1)
                return mm

            def turn_sums(u):
                pe.wait_ge(o0_copied, u + 1)
                for t in range(TB):
                    mm = pe.transpose(ps[:, 7, t * 128:(t + 1) * 128], OS[:, t * 128:(t + 1) * 128], ident)
                mm.then_inc(o0_turned, 1)

            def unit0(u, b, first=False, last=False, next_group=None, turns=True):
                pe.wait_ge(d0_max, (u + 1) * TB * 2)
                for t in range(TB):
                    mm = pe.transpose(ps[:, 6, t * 128:(t + 1) * 128], mcol0[:, t, :], ident)
                mm.then_inc(m0_ready, 1)
                if turns:
                    turn_sums(u - 2)
                pe.wait_ge(m0_done, u + 1)
                if not last:
                    if next_group is not None:
                        pe.wait_ge(wqk_loaded, next_group * 16 + 16)
                    q_proj(u + 1, (b + 1) % 2)
                turned_scores(u, b, 0, first)
                if not last:
                    k_proj(u + 1, (b + 1) % 2)
                if not first:
                    pe.wait_ge(s0_masked, u * TB)
                    pe.wait_ge(vg_done, u)
                    if turns:
                        pe.wait_ge(o0_done, u - 1)
                for t in range(1, TB):
                    turned_scores(u, b, t, False)
                    if not first:
                        weighted0((b + 1) % 2, pieces0[t - 1:t])
                if not first:
                    weighted0((b + 1) % 2, pieces0[3:4])
                for e in range(8):
                    if not last:
                        row_max_scores(u + 1, (b + 1) % 2, e // 2, e % 2, False)
                    if not first:
                        mm = weighted0((b + 1) % 2, pieces0[4 + e * 12 // 8:4 + (e + 1) * 12 // 8])
                if not first:
                    mm.then_inc(o0_ready, 1)

            pe.wait_ge(bf_done, 2)
            pe.wait_ge(masks_done, 1)
            pe.wait_ge(setup_done, 7)
            pe.wait_ge(cross_bias_done, B)
            pe.wait_ge(g_done, B)
            pe.wait_ge(v0_done, B)
            pe.wait_ge(u_done, B)
            pe.wait_ge(wqk_loaded, 16)
            q_proj(0, 0)
            k_proj(0, 0)
            for e in range(8):
                row_max_scores(0, 0, e // 2, e % 2, e == 0)
            unit0(0, 0, first=True, turns=False)
            unit0(1, 1, next_group=1, turns=False)
            with pe.Fori(1, NG - 1) as g:
                unit0(g * B, 0)
                unit0(g * B + 1, 1, next_group=g + 1)
            unit0(UNITS0 - 2, 0)
            unit0(UNITS0 - 1, 1, last=True)
            turn_sums(UNITS0 - 2)
            pe.wait_ge(s0_masked, UNITS0 * TB)
            pe.wait_ge(vg_done, UNITS0)
            pe.wait_ge(o0_done, UNITS0 - 1)
            weighted0(1, pieces0).then_inc(o0_ready, 1)
            turn_sums(UNITS0 - 1)
            for b in range(B):
                pe.wait_ge(o0_done, UNITS0 - B + b + 1)
                for t in range(TB):
                    mm = pe.transpose(ps[:, b, t * 128:(t + 1) * 128], O0[:, b * TB + t, :], ident)
                mm.then_inc(ot0_ready, 1)
            for b in range(B):
                pe.wait_ge(ot0_done, b + 1)
                for t in range(TB):
                    n = b * TB + t
                    mm = pe.matmul(ps[:, 2 + b, t * C:(t + 1) * C], OT0[:, n * 128:(n + 1) * 128], w0_proj,
                                   start=True, stop=True)
                mm.then_inc(proj_ready, 1)
            turn_ln(0, CROSS)
            cross_pe(0, True)
            turn_ln(0, FF)
            ff_pe(0, lambda n, j: [(2 * (n % 2), w0_m1[:, j * 128:(j + 1) * 128])], w0_m2, lambda n: (f_gelu, n + 1))

            with pe.Fori(0, LOOP_LAYERS) as l:
                pe.wait_ge(cross_loaded, l * 32 + 32)
                for n in range(2):
                    for j in range(H // 2):
                        mm = pe.matmul(ps[:, n, j * B * S:(j + 1) * B * S], wc[:, n, j * 128:(j + 1) * 128],
                                       ctxT[:, :], start=True, stop=True)
                    mm.then_inc(kv2_ready, 1)
                pe.wait_ge(kv2_done, 2 + l * 2 + 1)
                for r in range(2):
                    half = slice(64 * r, 64 * r + 64)
                    if r == 1:
                        pe.wait_ge(kv2_done, 2 + l * 2 + 2)
                        pe.wait_ge(ff_added, (l + 1) * B)
                    for j in range(H // 2):
                        mm = pe.matmul(ps[:, 2 + r, j * B * S:(j + 1) * B * S], wx[half, j, 0:C], K2T[half, j, :],
                                       start=True, stop=True)
                    mm.then_inc(g_ready, 1)
                for r in range(2):
                    half = slice(64 * r, 64 * r + 64)
                    for b in range(B):
                        for j in range(H // 2):
                            c = (b * 2 + j // 4) * C
                            mm = pe.matmul(ps[32 * (j % 4):32 * (j % 4) + 32, 4 + r, c:c + C],
                                           V2T[half, j, b * S:(b + 1) * S], wx[half, j, C:2 * C], start=True,
                                           stop=True)
                    mm.then_inc(u_ready, 1)
                turn_ln(l + 1, ATTN)

                def fold(h, e, turn_nth):
                    pe.wait_ge(wa_loaded[e], turn_nth * 16)
                    pe.matmul(ps[:, 6, 0:C], wa[:, e, 0:C], wa[:, e, C:2 * C], start=True, stop=True)
                    pe.matmul(ps[:, 6, C:2 * C], wa[:, e, 2 * C:3 * C], wa[:, e, 3 * C:4 * C], start=True, stop=True)\
                      .then_inc(ab_ready, 1)

                def t_rows(i, k):
                    e, cols = (k // 2) % 2, cols_of(k % 2)
                    pe.matmul(ps[:, 6, :], A_hi[:, e, :], hTh[:, cols], start=True, stop=False)
                    pe.matmul(ps[:, 6, :], A_lo[:, e, :], hTh[:, cols], start=False, stop=False)
                    pe.matmul(ps[:, 6, :], A_hi[:, e, :], hTl[:, cols], start=False, stop=True).then_inc(t_ready, 1)

                def values(i, k):
                    e = (k // 2) % 2
                    pe.wait_ge(t_lo_done, nth(l, i, k, 1, 0))
                    for t in range(TB):
                        n = (k % 2) * TB + t
                        mm = pe.matmul(ps[:, 6, t * C:(t + 1) * C], hT[:, n * 128:(n + 1) * 128], Bm[:, e, :],
                                       start=True, stop=True)
                    mm.then_inc(v_ready, 1)

                def row_max_scores(i, k, t, fresh=False):
                    if not fresh:
                        pe.wait_ge(d_max, nth(l, i, k, TB, t) - 2)
                    pe.matmul(ps[:, 4 + t % 2, :], T_hi[:, k % 2, t * 128:(t + 1) * 128], hTh[:, cols_of(k % 2)],
                              start=True, stop=True).then_inc(d_ready, 1)

                def turned_scores(i, k, e, fresh):
                    if e == 0:
                        pe.wait_ge(m_done, nth(l, i, k, 1, 0))
                    if not fresh:
                        pe.wait_ge(s_exp, nth(l, i, k, 2, e) - 2)
                    for s in range(2 * e, 2 * e + 2):
                        n = (k % 2) * TB + s
                        keys = slice(n * 128, (n + 1) * 128)
                        pe.matmul(ps[:, s, :], hTh[:, keys], T_hi[:, k % 2, :], start=True, stop=False)
                        pe.matmul(ps[:, s, :], hTh[:, keys], T_lo[:, k % 2, :], start=False, stop=False)
                        pe.matmul(ps[:, s, :], hTl[:, keys], T_hi[:, k % 2, :], start=False, stop=False)
                        mm = pe.matmul(ps[:, s, :], spread[:, :], mrow[:, :], start=False, stop=True)
                    mm.then_inc(s_ready, 1)

                def weighted(i, k, pair, fresh=False):
                    if not (fresh and pair == 0):
                        pe.wait_ge(o_done, nth(l, i, k, 2, pair) - 1)
                    for t in range(2 * pair, 2 * pair + 2):
                        o = ps[:, 7, 256 * (t % 2):256 * (t % 2) + C + 1]
                        for s in range(TB):
                            mm = pe.matmul(o, Pt[:, k % 2, s, t * 128:(t + 1) * 128], V1[:, k % 4, s, :],
                                           start=s == 0, stop=s == TB - 1)
                    mm.then_inc(o_ready, 1)

                def unit(i, k, first=False, last=False):
                    before = (i, k - 1)
                    none_before = first and k == 0
                    fresh = first and k == 1
                    folds = k % 2 == 0 and not (k == 2 and i is LAST)
                    pe.wait_ge(d_max, nth(l, i, k, TB, TB - 1))
                    pe.transpose(ps[0:TB, 4, 0:128], mcol[:, 0:TB], ident).then_inc(m_ready, 1)
                    if not none_before:
                        pe.wait_ge(s_exp, nth(l, i, k - 1, 2, 1))
                        weighted(*before, 0, fresh)
                    pe.wait_ge(v_done, nth(l, i, k, 1, 0))
                    if not last:
                        t_rows(i, k + 1)
                    turned_scores(i, k, 0, none_before)
                    if not last:
                        pe.wait_ge(t_lo_done, nth(l, i, k + 1, 1, 0))
                        row_max_scores(i, k + 1, 0)
                        row_max_scores(i, k + 1, 1)
                    if folds:
                        fold(l * H + i * 2 + k // 2 + 1, (k // 2 + 1) % 2, l * TURNS + i + (1 if k == 0 else 2))
                    turned_scores(i, k, 1, none_before)
                    if not last:
                        row_max_scores(i, k + 1, 2)
                        row_max_scores(i, k + 1, 3)
                    if not none_before:
                        weighted(*before, 1, fresh)
                    if folds:
                        pe.wait_ge(a_lo_done, l * H + i * 2 + k // 2 + 2)
                    if not last:
                        values(i, k + 1)

                pe.wait_ge(setup_done, 7)
                pe.wait_ge(ln_hT, half_nth(l + 1, ATTN, B - 1))
                pe.wait_ge(ln_lo, (l + 1) * B)
                fold(l * H, 0, l * TURNS + 1)
                pe.wait_ge(a_lo_done, l * H + 1)
                pe.wait_ge(b_done, l * H + 1)
                t_rows(0, 0)
                values(0, 0)
                pe.wait_ge(u_done, B + (l + 1) * 2)
                for t in range(TB):
                    row_max_scores(0, 0, t, fresh=t < 2)
                for k in range(4):
                    unit(0, k, first=True)
                with pe.Fori(1, LAST) as i:
                    for k in range(4):
                        unit(i, k)
                for k in range(4):
                    unit(LAST, k, last=k == 3)
                pe.wait_ge(s_exp, nth(l, LAST, 3, 2, 1))
                for pair in range(2):
                    weighted(LAST, 3, pair)
                turn_ln(l + 1, CROSS)
                cross_pe(l + 1, False)
                turn_ln(l + 1, FF)
                pe.wait_ge(ff_loaded, l * 16 + 16)
                ff_pe(l + 1, lambda n, j: [(2 * (n % 2), w_p[:, HID + j * 128:HID + (j + 1) * 128]),
                                           (2 * (n % 2) + 1, w_p[:, j * 128:(j + 1) * 128])], w_2,
                      lambda n: (f_u, l * B * FC + n + 1))


def kernel(**inputs):
    import numpy as _np
    import concourse.bacc as _bacc
    from concourse import mybir as _mybir
    from concourse.bass_utils import run_bass_kernel_spmd as _run

    a = {k: _np.asarray(v) for k, v in inputs.items()}
    f = a["x"].dtype
    l0 = {k[len("L0_xattn_"):]: v for k, v in a.items() if k.startswith("L0_")}

    consts = _np.zeros((128, 260 + H), f)
    consts[:, 0:128] = _np.eye(128)
    consts[:, 128:256] = _np.triu(_np.full((128, 128), -BIG), 1)
    row = _np.arange(128) % 32
    consts[:, 256] = _np.where((row < D0) | ((row >= 2 * D0) & (row <= ROW_MASK)), 1, 0) - _np.where((row >= D0) & (row < 2 * D0), 1, 0)
    consts[:, 257] = (row >= D0) & (row < 2 * D0)
    consts[:, 258] = _np.where((row < 2 * D0) | (row == ROW_MASK) | (row == ROW_MAX), 1, 0) - _np.where((row >= 2 * D0) & (row < 3 * D0), 1, 0)
    consts[:, 259] = (row >= 2 * D0) & (row < 3 * D0)
    for h in range(H):
        consts[h * D0:(h + 1) * D0, 260 + h] = 1

    w0_qk = _np.zeros((NG, 128, 258), f)
    for g in range(NG):
        for j in range(G0):
            cols = slice((g * G0 + j) * D0, (g * G0 + j + 1) * D0)
            for copy in range(3):
                at = 32 * j + copy * D0
                for n in range(2):
                    w0_qk[g, :, 128 * n + at:128 * n + at + D0] = l0["qkv_w"][:, n * C:(n + 1) * C][:, cols]
                    w0_qk[g, at:at + D0, 256 + n] = l0["qkv_b"][n * C:(n + 1) * C][cols]
            w0_qk[g, 32 * j + ROW_MASK, 256] = 1
            w0_qk[g, 32 * j + ROW_MAX, 257] = 1

    def chunks(w):
        return w.reshape(-1, 128, w.shape[1]).transpose(1, 0, 2).reshape(128, -1)

    w0 = _np.concatenate([l0["qkv_w"][:, 2 * C:], l0["proj_w"], l0["q_w"].T, l0["out_w"], l0["mlp1_w"],
                          chunks(l0["mlp2_w"])], axis=1)
    wk0 = _np.concatenate([l0["k_w"], l0["v_w"]], axis=1)
    vec0 = _np.stack([l0["ln1_w"], l0["ln1_b"], l0["ln2_w"], l0["ln2_b"], l0["ln3_w"], l0["ln3_b"],
                      *l0["mlp1_b"].reshape(FC, 128), l0["k_b"], l0["v_b"], l0["q_b"]], axis=1)
    rows0 = _np.stack([l0["qkv_b"][2 * C:], l0["proj_b"], l0["out_b"], l0["mlp2_b"]])

    n1, n2, n3 = "L1_xattn_", "L2_xattn_", "L3_xattn_"

    def three(first, second, third, turned=True):
        second = a[n2 + second]
        return a[n1 + first], second.T if turned else second, a[n3 + third]

    def stack(*parts):
        return _np.stack([_np.concatenate(layer, axis=-1) for layer in zip(*parts)])

    def by_head(ws):
        return [w.T.reshape(H, D, C) for w in ws]

    def out_by_head(ws):
        return [w.reshape(H, D, C) for w in ws]

    def by_pair(ws):
        return [w.reshape(H // 2, 128, C).transpose(1, 0, 2) for w in ws]

    w_attn = stack(by_head(three("Wq1", "wq1", "q1_w")), by_head(three("Wk1", "wk1", "k1_w")),
                   by_head(three("Wv1", "wv1", "v1_w")), out_by_head(three("Wo1", "wo1", "o1_w")))
    w_ctx = stack(three("Wk2", "wk2", "k2_w"), three("Wv2", "wv2", "v2_w"))
    w_cross = stack(by_pair(by_head(three("Wq2", "wq2", "q2_w"))), by_pair(out_by_head(three("Wo2", "wo2", "o2_w"))))
    w_cross = w_cross.reshape(LOOP_LAYERS, 128, -1)
    w_ff = stack(three("Wp", "w_geglu", "ff1_w"), [chunks(w) for w in three("W2", "w_ffout", "ff2_w")])

    def col(ws):
        return [w.reshape(-1, 128).T for w in ws]

    vec = stack(*(col(three(*names, turned=False)) for names in (
        ("g1", "ln1_g", "n1_w"), ("be1", "ln1_b", "n1_b"), ("g2", "ln2_g", "n2_w"), ("be2", "ln2_b", "n2_b"),
        ("g3", "ln3_g", "n3_w"), ("be3", "ln3_b", "n3_b"), ("bp", "b_geglu", "ff1_b"))))
    rows = _np.stack([_np.stack(three(*names, turned=False)) for names in (
        ("bo1", "bo1", "o1_b"), ("bo2", "bo2", "o2_b"), ("b2", "b_ffout", "ff2_b"))], axis=1)
    ctx_t = a["ctx_768"].reshape(B * S, CE).T

    arrays, args = {}, []
    for name, v in (("x", a["x"]), ("ctx_t", ctx_t), ("tgt_mask", a["mask_BxS_bf0"]), ("enc_mask", a["mask_BxS2_bf0"]),
                    ("consts", consts), ("w0_qk", w0_qk), ("w0", w0), ("wk0", wk0), ("vec0", vec0), ("rows0", rows0),
                    ("w_attn", w_attn), ("w_ctx", w_ctx), ("w_cross", w_cross), ("w_ff", w_ff), ("vec", vec),
                    ("rows", rows)):
        arrays["in_" + name] = _np.ascontiguousarray(v)
    nc = _bacc.Bacc("TRN2", target_bir_lowering=False, num_devices=1)
    for name, v in arrays.items():
        args.append(nc.dram_tensor(name, v.shape, _mybir.dt.from_np(v.dtype), kind="ExternalInput").ap())
    out = nc.dram_tensor("out", (B, T, C), _mybir.dt.float32, kind="ExternalOutput").ap()
    decoder_stack_kernel(nc, *args, out)
    r = _run(nc, [arrays], core_ids=[0])
    return r.results[0]["out"]
```

```python
import concourse.bass as bass
from concourse import mybir
from contextlib import ExitStack


B, T, C = 2, 512, 128
NT = B * T // 128
TB = T // 128
S, CE = 32, 96
H = 16
D0 = C // H
D = 64
HID = 512
FC = HID // 128
G0 = 4
NG = H // G0
TURNS = H // 2
LOOP_LAYERS = 3
ROW_MASK, ROW_MAX = 3 * D0, 3 * D0 + 1
BIG = 1e30


class Steps:

    def __init__(self, engine, semaphore):
        self.engine, self.semaphore, self.base, self.n = engine, semaphore, 0, 0

    def add(self, instruction):
        instruction.then_inc(self.semaphore, 1)
        self.n += 1

    def wait(self):
        self.engine.wait_ge(self.semaphore, self.base + self.n)

    def enter(self, index, per_turn):
        kept = (self.base, self.n, per_turn)
        self.base, self.n = self.base + self.n + index * per_turn, 0
        return kept

    def leave(self, kept, turns):
        base, n, per_turn = kept
        assert self.n == per_turn, (self.n, per_turn)
        self.base, self.n = base, n + turns * per_turn


def decoder_stack_kernel(nc, x_in, ctx_t, tgt_mask, enc_mask, consts, w0_qk, w0, wk0, vec0, rows0,
                         w_attn, w_ctx, w_cross, w_ff, vec, rows, out):
    f32, f32r, bf16, u8 = mybir.dt.float32, mybir.dt.float32r, mybir.dt.bfloat16, mybir.dt.uint8
    ALU = mybir.AluOpType
    ACT = mybir.ActivationFunctionType
    X = mybir.AxisListType.X
    EPS = 1e-5
    SCALE0 = float(D0) ** -0.5
    SCALE = float(D) ** -0.5

    x_dram = x_in.rearrange("b (t p) c -> p (b t) c", p=128)
    out_dram = out.rearrange("b (t p) c -> p (b t) c", p=128)

    ctx = ExitStack()
    with ctx:
        def sb(name, shape, dt=f32):
            return ctx.enter_context(nc.sbuf_tensor(name, shape, dt))

        def sem(name):
            return ctx.enter_context(nc.semaphore(name))

        x = sb("x", [128, NT, C])
        xhat = sb("xhat", [128, NT, C])
        hT = sb("hT", [128, NT * 128])
        hTh = sb("hTh", [128, NT * 128], f32r)
        hTl = sb("hTl", [128, NT * 128], f32r)
        stats = sb("stats", [128, NT, 6])
        mv = sb("mv", [128, NT, 2])
        veps = sb("veps", [128, NT])
        rstd = sb("rstd", [128, NT])
        mhalf = sb("mhalf", [128, NT])
        cst = sb("cst", [128, 128 + 128 + 4 + H])
        ident, tri = cst[:, 0:128], cst[:, 128:256]
        sQ, tQ, sK, tK = (cst[:, 256 + n:257 + n] for n in range(4))
        head_mask = cst[:, 260:260 + H]
        ident_bf = sb("ident_bf", [128, 128], bf16)
        tri_bf = sb("tri_bf", [128, 128], bf16)
        ones_row = sb("ones_row", [1, 128])
        ctxT = sb("ctxT", [CE, B * S])

        wqk = sb("wqk", [128, 2 * 128 + 2])
        wl0 = sb("wl0", [128, 4 * C + HID + FC * C])
        w0_v, w0_proj, w0_qT, w0_out = (wl0[:, n * C:(n + 1) * C] for n in range(4))
        w0_m1 = wl0[:, 4 * C:4 * C + HID]
        w0_m2 = wl0[:, 4 * C + HID:4 * C + 2 * HID].rearrange("p (j c) -> p j c", j=FC)
        wkv0 = sb("wkv0", [CE, 2 * C])
        v0 = sb("v0", [128, 13])
        r0 = sb("r0", [128, 4, C])

        wc = sb("wc", [CE, 2, H * D])
        wx = sb("wx", [128, H // 2, 2 * C])
        wf = sb("wf", [128, 2 * HID + FC * C])
        w_p, w_2 = wf[:, 0:2 * HID], wf[:, 2 * HID:].rearrange("p (j c) -> p j c", j=FC)
        vl = sb("vl", [128, 14])
        rl = sb("rl", [128, 3, C])

        Wh = sb("Wh", [128, 2, C], f32r)
        Wl = sb("Wl", [128, 2, C], f32r)
        QX = sb("QX", [128, 4, T], f32r)
        KX = sb("KX", [128, 4, T], f32r)
        KB = sb("KB", [128, 4, T], f32r)
        QB = sb("QB", [128, 4, T], f32r)
        V = sb("V", [128, B, TB, C])
        ones = sb("ones", [128, 32])
        pick = sb("pick", [128, TB, D])
        mcol = sb("mcol", [128, TB])

        K2T = sb("K2T", [128, B * S])
        V2T = sb("V2T", [128, B * S])
        K2b = sb("K2b", [128, H // 2, B, 2 * S])
        V2b = sb("V2b", [128, H // 2, B, 2 * S])
        Gm = sb("Gm", [128, B, H * S])
        Um = sb("Um", [128, B, 4, C])
        cross_bias = sb("cross_bias", [1, B, H * S])
        em8 = sb("em8", [1, B, S], u8)
        em = sb("em", [1, B, S])
        keepn = sb("keepn", [1, B, S])
        poison = sb("poison", [1, 3 * B])
        cmax = sb("cmax", [128, 2, H])
        csum = sb("csum", [128, 2, H])
        crec = sb("crec", [128, 2, H])
        Ec = sb("Ec", [128, 2, H * S])

        Vaug = sb("Vaug", [128, NT, H, D0 + 1])
        Vg = sb("Vg", [128, 2, TB, G0, 32])
        OS = V[:, 0, :, :].rearrange("p t c -> p (t c)")
        QH, KH, QX0 = QX[:, 0, :], QX[:, 1, :], QX[:, 2, :]
        KX0, QM = KX[:, 0:2, :], KX[:, 2:4, :]
        Qt = sb("Qt", [128, T])
        Kt = sb("Kt", [128, T])
        mcol0 = sb("mcol0", [128, TB, 128])
        room = sb("room", [128, 2 * G0 * TB * T])
        P0 = room[:, :].rearrange("p (u j k) -> p u j k", u=2, j=G0)
        Pt = room[:, 0:4 * TB * T].rearrange("p (u k q) -> p u k q", u=4, k=TB)
        Psum = room[:, 8192:8192 + 4 * T].rearrange("p (u q) -> p u q", u=4)
        On = room[:, 10240:10240 + T]
        Os = room[:, 10240 + T:10240 + 2 * T]
        Lr = room[:, 10240 + 2 * T:10240 + 2 * T + 2 * 128]
        wa = room[:, 12288:12288 + TURNS * 4 * C].rearrange("p (i n) -> p i n", i=TURNS)
        Pc = room[:, 11264:11264 + 2 * H * S].rearrange("p (u n) -> p u n", u=2)
        uT = room[:, 4096:4096 + B * FC * T].rearrange("p (b j t) -> p b j t", b=B, j=FC)
        gl = room[:, 8192:8192 + 2 * T].rearrange("p (u t) -> p u t", u=2)
        P2T = room[:, 9216:9216 + 2 * 512].rearrange("p (u j t) -> p u j t", u=2, j=4)
        rden0 = sb("rden0", [128, 2, TB * G0])
        O0 = sb("O0", [128, NT, C])
        OT0 = room[:, 10240:10240 + NT * 128]
        tm8 = sb("tm8", [1, B, T], u8)
        eps = sb("eps", [128, NT])
        pool_pad, dve_pad = sb("pool_pad", [128, 1]), sb("dve_pad", [128, 1])
        tmr = sb("tmr", [1, B, T], bf16)
        onehot = sb("onehot", [1, 128], bf16)
        km8 = sb("km8", [128, NT], u8)
        keep = sb("keep", [128, NT])

        ps = ctx.enter_context(nc.psum_tensor("ps", [128, 8, 512], f32))

        consts_loaded, x_loaded, masks_loaded = sem("consts_loaded"), sem("x_loaded"), sem("masks_loaded")
        w0_loaded, wqk_loaded = sem("w0_loaded"), sem("wqk_loaded")
        wa_loaded = sem("wa_loaded")
        cross_loaded, ff_loaded, vec_loaded = sem("cross_loaded"), sem("ff_loaded"), sem("vec_loaded")
        zeroed, setup_done = sem("zeroed"), sem("setup_done")
        dve_step, pool_step, pad_written = sem("dve_step"), sem("pool_step"), sem("pad_written")
        ln_var, ln_rstd, ln_xhat = sem("ln_var"), sem("ln_rstd"), sem("ln_xhat")
        ln_turned, ln_hT, ln_hi, ln_lo = sem("ln_turned"), sem("ln_hT"), sem("ln_hi"), sem("ln_lo")
        bias_added = sem("bias_added")
        bf_done, masks_done = sem("bf_done"), sem("masks_done")
        v0_ready, v0_done = sem("v0_ready"), sem("v0_done")
        blocks_done, qb_ready, cross_bias_done = sem("blocks_done"), sem("qb_ready"), sem("cross_bias_done")
        q0_ready, q0_hi, q0_done = sem("q0_ready"), sem("q0_hi"), sem("q0_done")
        k0_ready, k0_hi, k0_done = sem("k0_ready"), sem("k0_hi"), sem("k0_done")
        d0_ready, d0_max = sem("d0_ready"), sem("d0_max")
        m0_ready, m0_done = sem("m0_ready"), sem("m0_done")
        s0_ready, s0_exp, s0_masked = sem("s0_ready"), sem("s0_exp"), sem("s0_masked")
        vg_done, o0_ready, o0_copied = sem("vg_done"), sem("o0_ready"), sem("o0_copied")
        o0_turned, o0_done = sem("o0_turned"), sem("o0_done")
        ot0_ready, ot0_done, proj_ready, proj_added = sem("ot0_ready"), sem("ot0_done"), sem("proj_ready"), sem("proj_added")
        w_hi, w_lo = sem("w_hi"), sem("w_lo")
        qk_ready, qk_hi, qk_lo = sem("qk_ready"), sem("qk_hi"), sem("qk_lo")
        v_ready, v_done = sem("v_ready"), sem("v_done")
        d_ready, d_max, m_ready, m_done = sem("d_ready"), sem("d_max"), sem("m_ready"), sem("m_done")
        s_ready, s_exp = sem("s_ready"), sem("s_exp")
        p_sum, l_ready, l_rec, o_norm = sem("p_sum"), sem("l_ready"), sem("l_rec"), sem("o_norm")
        o_ready, o_copied, l_spread = sem("o_ready"), sem("o_copied"), sem("l_spread")
        op_ready, o_done = sem("op_ready"), sem("o_done")
        kv2_ready, kv2_done = sem("kv2_ready"), sem("kv2_done")
        g_ready, g_done, u_ready, u_done = sem("g_ready"), sem("g_done"), sem("u_ready"), sem("u_done")
        c_ready, c_sub, c_exp, c_rec, c_norm = sem("c_ready"), sem("c_sub"), sem("c_exp"), sem("c_rec"), sem("c_norm")
        ct_ready, ct_done, co_ready, c_added = sem("ct_ready"), sem("ct_done"), sem("co_ready"), sem("c_added")
        f_ready, f_gelu, f_u = sem("f_ready"), sem("f_gelu"), sem("f_u")
        fo_ready, ff_added = sem("fo_ready"), sem("ff_added")
        stored = sem("stored")

        block = ctx.enter_context(nc.Block())

        ATTN, CROSS, FF = range(3)
        UNITS = H * B
        UNITS0 = NG * B
        LAST = TURNS - 1

        def half_nth(L, part, b):
            return (L * 3 + part) * B + b + 1

        def nth(l, i, k, per, e):
            return (l * UNITS + i * 4 + k) * per + e + 1

        def qk_nth(l, i, k, per=1, e=0):
            return nth(l, i, k, per, e) + 2 * per

        def couple_nth(l, i, b):
            return (l * TURNS + i) * B + b + 1

        def pairs_nth(l, i):
            return (l * TURNS + i) * 2 + 2

        def of_pair(i, n):
            if isinstance(i, int):
                return wa[:, i, n * C:(n + 1) * C]
            return wa[:, bass.ds(i, 1), n * C:(n + 1) * C].rearrange("p a n -> p (a n)")

        def score_bank(n):
            return (0, 1, 6, 7)[n % 4]

        def rows_of(b):
            return slice(b * TB, (b + 1) * TB)

        def cols_of(b):
            return slice(b * T, (b + 1) * T)


        @block.sync
        def _(sp):
            sp.dma_start(cst[:, :], consts).then_inc(consts_loaded, 16)
            sp.dma_start(v0[:, :], vec0).then_inc(consts_loaded, 16)
            sp.dma_start(ctxT[:, :], ctx_t).then_inc(w0_loaded, 16)
            sp.dma_start(wkv0[:, :], wk0).then_inc(w0_loaded, 16)
            sp.dma_start(wl0[:, :], w0).then_inc(w0_loaded, 16)
            sp.dma_start(r0[:, :, :], rows0.partition_broadcast(128)).then_inc(w0_loaded, 16)
            sp.dma_start(wqk[:, :], w0_qk[0, :, :]).then_inc(wqk_loaded, 16)

            def layer_loads(l, first):
                layer = bass.ds(l, 1)
                if not first:
                    sp.wait_ge(u_done, (l + 1) * 2)
                sp.dma_start(wc[:, :, :], w_ctx[layer, :, :].rearrange("a p (k n) -> (a p) k n", k=2))\
                  .then_inc(cross_loaded, 16)
                sp.dma_start(wx[:, :, :], w_cross[layer, :, :].rearrange("a p (k n) -> (a p) k n", k=H // 2))\
                  .then_inc(cross_loaded, 16)
                if first:
                    sp.wait_ge(o0_ready, UNITS0)
                else:
                    sp.wait_ge(op_ready, l * TURNS * B)
                sp.dma_start(wa[:, :, :], w_attn[layer, :, :].rearrange("a p (i n) -> (a p) i n", i=TURNS))\
                  .then_inc(wa_loaded, 16)
                if not first:
                    sp.wait_ge(ff_added, (l + 1) * B)
                sp.dma_start(vl[:, :], vec[layer, :, :].rearrange("a p n -> (a p) n")).then_inc(vec_loaded, 16)
                sp.dma_start(rl[:, :, :], rows[layer, :, :].rearrange("a r c -> (a r) c").partition_broadcast(128))\
                  .then_inc(vec_loaded, 16)
                sp.dma_start(wf[:, :], w_ff[layer, :, :].rearrange("a p n -> (a p) n")).then_inc(ff_loaded, 16)

            with sp.Fori(1, NG) as g:
                sp.wait_ge(k0_done, g * B)
                sp.dma_start(wqk[:, :], w0_qk[bass.ds(g, 1), :, :].rearrange("a p n -> (a p) n"))\
                  .then_inc(wqk_loaded, 16)
            layer_loads(0, True)
            with sp.Fori(1, LOOP_LAYERS) as l:
                layer_loads(l, False)
            for b in range(B):
                sp.wait_ge(ff_added, LOOP_LAYERS * B + b + 1)
                sp.dma_start(out_dram[:, rows_of(b), :], x[:, rows_of(b), :]).then_inc(stored, 16)
            sp.wait_ge(stored, 16 * B)

        @block.gpsimd
        def _(pool):
            steps = Steps(pool, pool_step)
            with nc.allow_non_contiguous_dma(reason="a mask of one byte per token, tokens onto partitions"):
                pool.dma_start(km8[:, :], tgt_mask.rearrange("b (t p) -> p (b t)", p=128)).then_inc(masks_loaded, 16)
            pool.dma_start(tm8[:, :, :], tgt_mask.rearrange("(a b) t -> a b t", a=1)).then_inc(masks_loaded, 16)
            pool.dma_start(em8[:, :, :], enc_mask.rearrange("(a b) s -> a b s", a=1)).then_inc(masks_loaded, 16)
            pool.memset(mhalf[:, :], -0.5).then_inc(zeroed, 1)
            pool.memset(eps[:, :], EPS).then_inc(zeroed, 1)
            pool.memset(pool_pad[:, :], 0.0).then_inc(pad_written, 1)
            pool.memset(QB[:, :, :].bitcast(f32), 0.0).then_inc(zeroed, 1)
            pool.memset(onehot[:, :], 0.0).then_inc(zeroed, 1)
            pool.memset(pick[:, :, :], 0.0).then_inc(zeroed, 1)
            pool.wait_ge(zeroed, 5)
            pool.memset(mcol0[:, :, :], 0.0).then_inc(setup_done, 1)
            pool.memset(Vg[:, :, :, :, :], 0.0).then_inc(setup_done, 1)
            pool.memset(KB[:, :, :].bitcast(f32), 1.0).then_inc(setup_done, 1)
            pool.memset(ones[:, :], 1.0).then_inc(setup_done, 1)
            pool.memset(K2b[:, :, :, :], 0.0).then_inc(setup_done, 1)
            pool.memset(V2b[:, :, :, :], 0.0).then_inc(setup_done, 1)
            pool.memset(ones_row[:, :], 1.0).then_inc(setup_done, 1)
            pool.memset(onehot[:, :].rearrange("p (j r) -> p j r", r=32)[:, :, ROW_MASK:ROW_MASK + 1], 1.0)\
                .then_inc(setup_done, 1)

            def inverse_std(L, part, halves=range(B)):
                for b in halves:
                    pool.wait_ge(ln_var, half_nth(L, part, b))
                    steps.add(pool.tensor_tensor(veps[:, rows_of(b)], mv[:, rows_of(b), 1], eps[:, rows_of(b)],
                                                 ALU.add))
                    steps.wait()
                    pool.tensor_tensor(rstd[:, rows_of(b)], veps[:, rows_of(b)], mhalf[:, rows_of(b)], ALU.pow)\
                        .then_inc(ln_rstd, 1)

            def add_bias(L, part, row):
                for b in range(B):
                    pool.wait_ge(ln_xhat, half_nth(L, part, b))
                    pool.tensor_tensor(x[:, rows_of(b), :], x[:, rows_of(b), :],
                                       row.unsqueeze(1).to_broadcast([128, TB, C]), ALU.add).then_inc(bias_added, 1)

            def normalise_cross(L):
                for n in range(NT):
                    pool.wait_ge(c_rec, L * NT + n + 1)
                    p = Pc[:, n % 2, :].rearrange("p (h s) -> p h s", s=S)
                    pool.tensor_tensor(p, p, crec[:, n % 2, :].unsqueeze(2).to_broadcast([128, H, S]),
                                       ALU.mult).then_inc(c_norm, 1)
                    if n == NT - 2:
                        inverse_std(L, FF, (0,))
                inverse_std(L, FF, (1,))

            def zero_diagonal(u, b):
                for t in range(TB):
                    pool.wait_ge(s0_exp, (u * TB + t) * 2 + 2)
                    pool.wait_ge(pad_written, u * TB + t + 1)
                    pool.tensor_tensor(pool_pad[:, :], mhalf[:, 0:1], mhalf[:, 0:1], ALU.add)\
                        .then_inc(pad_written, 1)
                    blk = P0[:, b, :, t * T + t * 128:t * T + (t + 1) * 128]
                    pool.affine_select(out=blk, in_=blk, compare_op=ALU.is_ge, fill=0.0, base=0,
                                       pattern=[[0, G0], [1, 128]], channel_multiplier=-1).then_inc(s0_masked, 1)

            inverse_std(0, ATTN)
            pool.wait_ge(w0_loaded, 64)
            add_bias(0, ATTN, r0[:, 1, :])
            with pool.Fori(0, NG) as g:
                for b in range(B):
                    zero_diagonal(g * B + b, b)
            inverse_std(0, CROSS)
            add_bias(0, CROSS, r0[:, 2, :])
            normalise_cross(0)
            add_bias(0, FF, r0[:, 3, :])
            with pool.Fori(0, LOOP_LAYERS) as l:
                kept = steps.enter(l, 3 * B + 2 * UNITS)
                for part in (ATTN, CROSS, FF):
                    if part != FF:
                        inverse_std(l + 1, part)
                    if part == ATTN:
                        pool.wait_ge(vec_loaded, l * 32 + 32)
                    add_bias(l + 1, part, rl[:, part, :])
                    if part == ATTN:
                        with pool.Fori(0, TURNS) as i:
                            kept_i = steps.enter(i, 8)
                            for k in range(4):
                                pool.wait_ge(s_exp, nth(l, i, k, 2, 1))
                                steps.add(pool.tensor_tensor(Psum[:, k, :], Pt[:, k, 0, :], Pt[:, k, 1, :], ALU.add))
                                steps.wait()
                                steps.add(pool.tensor_tensor(Psum[:, k, :], Psum[:, k, :], Pt[:, k, 2, :], ALU.add))
                                steps.wait()
                                pool.tensor_tensor(Psum[:, k, :], Psum[:, k, :], Pt[:, k, 3, :], ALU.add)\
                                    .then_inc(p_sum, 1)
                            steps.leave(kept_i, TURNS)
                    if part == CROSS:
                        normalise_cross(l + 1)
                steps.leave(kept, LOOP_LAYERS)

        @block.scalar
        def _(act):
            for b in range(B):
                act.dma_start(x[:, rows_of(b), :], x_dram[:, rows_of(b), :]).then_inc(x_loaded, 16)

            def finish_ln(L, part, scale, bias, l=None, halves=range(B)):
                for b in halves:
                    act.wait_ge(ln_turned, half_nth(L, part, b))
                    act.activation(hT[:, cols_of(b)], ps[:, 6 + b, :], ACT.Identity, bias=bias, scale=scale)\
                       .then_inc(ln_hT, 1)
                    if l is not None:
                        act.activation(hTh[:, cols_of(b)], ps[:, 6 + b, :], ACT.Identity, bias=bias, scale=scale)\
                           .then_inc(ln_hi, 1)

            def turn_out(L, n):
                act.wait_ge(ct_ready, L * NT + n + 1)
                if n >= 2:
                    act.wait_ge(co_ready, L * NT + n - 1)
                act.activation(P2T[:, n % 2, :, :].rearrange("p j t -> p (j t)"), ps[:, 2 + n % 2, :],
                               ACT.Copy).then_inc(ct_done, 1)

            def cross_act(L, scale, ff_scale, ff_bias):
                for n in range(NT):
                    act.wait_ge(c_sub, L * NT + n + 1)
                    if n >= 2:
                        act.wait_ge(ct_ready, L * NT + n - 1)
                    act.activation(Pc[:, n % 2, :], Ec[:, n % 2, :], ACT.Exp, scale=scale).then_inc(c_exp, 1)
                    if n >= 1:
                        turn_out(L, n - 1)
                turn_out(L, NT - 1)
                finish_ln(L, FF, ff_scale, ff_bias, halves=(0,))

            act.wait_ge(consts_loaded, 32)
            act.wait_ge(kv2_ready, 1)
            act.activation(K2T[:, :], ps[:, 4, 0:B * S], ACT.Identity, bias=v0[:, 10:11]).then_inc(kv2_done, 1)
            act.activation(V2T[:, :], ps[:, 4, B * S:2 * B * S], ACT.Identity, bias=v0[:, 11:12])\
               .then_inc(kv2_done, 1)
            finish_ln(0, ATTN, v0[:, 0:1], v0[:, 1:2])
            for b in range(B):
                act.wait_ge(g_ready, b + 1)
                act.activation(Gm[:, b, :], ps[:, b, :], ACT.Copy).then_inc(g_done, 1)
            for b in range(B):
                act.wait_ge(u_ready, b + 1)
                act.activation(Um[:, b, :, :].rearrange("p j c -> p (j c)"), ps[:, 4 + b, :], ACT.Copy)\
                   .then_inc(u_done, 1)

            def q_hi(u):
                act.wait_ge(q0_ready, u + 1)
                act.activation(QH[:, :], ps[:, 0, :], ACT.Identity, bias=wqk[:, 256:257]).then_inc(q0_hi, 1)

            def k_hi(u):
                act.wait_ge(k0_ready, u + 1)
                act.activation(KH[:, :], ps[:, 1, :], ACT.Identity, bias=wqk[:, 257:258]).then_inc(k0_hi, 1)

            def exps0(u, b, t):
                for j2 in range(2):
                    act.wait_ge(s0_ready, (u * TB + t) * 2 + j2 + 1)
                    act.activation(P0[:, b, 2 * j2:2 * j2 + 2, t * T + t * 128:(t + 1) * T],
                                   ps[:, 2 + 2 * j2:4 + 2 * j2, 0:T - t * 128], ACT.Exp, scale=SCALE0)\
                       .then_inc(s0_exp, 1)

            def sums_out(u):
                act.wait_ge(o0_ready, u + 1)
                act.activation(OS, ps[:, 7, :], ACT.Copy).then_inc(o0_copied, 1)

            def unit0_act(u, b, first=False, last=False):
                if not last:
                    q_hi(u + 1)
                    k_hi(u + 1)
                for t in range(TB):
                    exps0(u, b, t)
                if not first:
                    sums_out(u - 1)

            q_hi(0)
            k_hi(0)
            unit0_act(0, 0, first=True)
            unit0_act(1, 1)
            with act.Fori(1, NG - 1) as g:
                for b in range(B):
                    unit0_act(g * B + b, b)
            for b in range(B):
                unit0_act(UNITS0 - B + b, b, last=b == B - 1)
            sums_out(UNITS0 - 1)
            for b in range(B):
                act.wait_ge(ot0_ready, b + 1)
                act.activation(OT0[:, cols_of(b)], ps[:, b, :], ACT.Copy).then_inc(ot0_done, 1)
            finish_ln(0, CROSS, v0[:, 2:3], v0[:, 3:4])
            cross_act(0, SCALE0, v0[:, 4:5], v0[:, 5:6])
            for b in range(B):
                for j in range(FC):
                    n = b * FC + j
                    if n == 2:
                        finish_ln(0, FF, v0[:, 4:5], v0[:, 5:6], halves=(1,))
                    act.wait_ge(f_ready, n + 1)
                    act.activation(uT[:, b, j, :], ps[:, 2 * (n % 2), :], ACT.Gelu, bias=v0[:, 6 + j:7 + j])\
                       .then_inc(f_gelu, 1)

            act.wait_ge(setup_done, 12)
            with act.Fori(0, LOOP_LAYERS) as l:
                def weights_hi(i, n):
                    act.activation(Wh[:, n, :], of_pair(i, n), ACT.Copy).then_inc(w_hi, 1)

                act.wait_ge(wa_loaded, l * 16 + 16)
                for n in range(2):
                    weights_hi(0, n)
                for n, dst in enumerate((K2b, V2b)):
                    act.wait_ge(kv2_ready, 1 + l * 2 + n + 1)
                    for e in range(2):
                        half = slice(64 * e, 64 * e + 64)
                        ins = act.activation(
                            dst[half, :, :, e * S:(e + 1) * S].rearrange("p j b s -> p (j b) s"),
                            ps[half, n, :].rearrange("p (k s) -> p k s", s=S), ACT.Copy)
                    ins.then_inc(kv2_done, 1)
                act.wait_ge(vec_loaded, l * 32 + 32)
                finish_ln(l + 1, ATTN, vl[:, 0:1], vl[:, 1:2], l, halves=(0,))
                for r in range(2):
                    act.wait_ge(g_ready, B + l * 2 + r + 1)
                    for b in range(B):
                        src = ps[:, 2 + r, :].rearrange("p (j b n) -> p j b n", b=B, n=2 * S)[:, :, b, :]
                        half = Gm[:, b, r * 256:(r + 1) * 256].rearrange("p (j n) -> p j n", n=2 * S)
                        act.activation(half, src, ACT.Copy).then_inc(g_done, 1)
                finish_ln(l + 1, ATTN, vl[:, 0:1], vl[:, 1:2], l, halves=(1,))
                for b in range(B):
                    act.wait_ge(u_ready, B + l * 2 + b + 1)
                    act.activation(Um[:, b, :, :].rearrange("p j c -> p (j c)"), ps[:, 4 + b, :], ACT.Copy)\
                       .then_inc(u_done, 1)

                def halves(e):
                    return slice(64 * e, 64 * e + 64), slice(64 - 64 * e, 128 - 64 * e)

                def q_hi_parts(i, k, slot):
                    act.wait_ge(qk_ready, qk_nth(l, i, k))
                    for e in range(2):
                        own = halves(e)[0]
                        act.activation(QX[own, slot + e, :], ps[own, 6, :], ACT.Copy)
                        act.activation(QB[own, slot + e, :], ps[own, 6, :], ACT.Copy).then_inc(qk_hi, 1)

                def k_hi_parts(i, k, slot):
                    act.wait_ge(qk_ready, qk_nth(l, i, k))
                    for e in range(2):
                        own, other = halves(e)
                        act.activation(KX[own, slot + e, :], ps[own, 6, :], ACT.Copy)
                        act.activation(KX[other, slot + e, :], ps[own, 6, :], ACT.Copy).then_inc(qk_hi, 1)

                def v_out(i, b):
                    act.wait_ge(v_ready, couple_nth(l, i, b))
                    act.activation(V[:, b, :, :].rearrange("p t c -> p (t c)"), ps[:, 6, :], ACT.Copy)\
                       .then_inc(v_done, 1)

                def exps(i, k, e):
                    act.wait_ge(s_ready, nth(l, i, k, 2, e))
                    act.activation(Pt[:, k, 2 * e:2 * e + 2, :], ps[:, 2 * e:2 * e + 2, :], ACT.Exp,
                                   scale=SCALE).then_inc(s_exp, 1)

                def sums_out(i, b):
                    act.wait_ge(o_ready, couple_nth(l, i, b))
                    act.activation(Os, ps[:, 7, :], ACT.Copy).then_inc(o_copied, 1)

                def unit(i, k, first=False):
                    more = not (i is LAST and k >= 2)
                    if k == 3:
                        sums_out(i, 0)
                    if k == 1 and not first:
                        sums_out(i - 1, 1)
                    slot = (k // 2 * 2 + 2) % 4
                    if more and k % 2 == 0:
                        q_hi_parts(i, k, slot)
                    exps(i, k, 0)
                    exps(i, k, 1)
                    if more and k % 2 == 0:
                        k_hi_parts(i, k + 1, slot)
                    if i is not LAST and k == 1:
                        for n in range(2):
                            weights_hi(i + 1, n)
                    if more and k % 2 == 1:
                        v_out(*((i, 1) if k == 1 else (i + 1, 0)))

                q_hi_parts(0, -2, 0)
                k_hi_parts(0, -1, 0)
                v_out(0, 0)
                for k in range(4):
                    unit(0, k, first=True)
                with act.Fori(1, LAST) as i:
                    for k in range(4):
                        unit(i, k)
                for k in range(4):
                    unit(LAST, k)
                sums_out(LAST, 1)
                finish_ln(l + 1, CROSS, vl[:, 2:3], vl[:, 3:4])
                cross_act(l + 1, SCALE, vl[:, 4:5], vl[:, 5:6])
                for b in range(B):
                    for j in range(FC):
                        n = b * FC + j
                        if n == 2:
                            finish_ln(l + 1, FF, vl[:, 4:5], vl[:, 5:6], halves=(1,))
                        act.wait_ge(f_ready, (l + 1) * B * FC + n + 1)
                        act.activation(gl[:, n % 2, :], ps[:, 2 * (n % 2), :], ACT.Gelu, bias=vl[:, 10 + j:11 + j])\
                           .then_inc(f_gelu, 1)

        @block.vector
        def _(dve):
            steps = Steps(dve, dve_step)

            def ln_stats(L, part, b, x_ready, x_nth):
                dve.wait_ge(x_ready, x_nth)
                for n in range(b * TB, (b + 1) * TB):
                    ins = dve.bn_stats(stats[:, n, :], x[:, n, :])
                steps.add(ins)
                steps.wait()
                dve.memset(dve_pad[:, :], 0.0)
                for n in range(b * TB, (b + 1) * TB):
                    ins = dve.bn_aggr(mv[:, n, :], stats[:, n, :])
                ins.then_inc(ln_var, 1)

            def ln_normalise(L, part, b):
                dve.wait_ge(ln_rstd, half_nth(L, part, b))
                for n in range(b * TB, (b + 1) * TB):
                    ins = dve.tensor_scalar(xhat[:, n, :], x[:, n, :], mv[:, n, 0:1], rstd[:, n:n + 1],
                                            ALU.subtract, ALU.mult)
                ins.then_inc(ln_xhat, 1)

            def layer_norm(L, part, x_ready, x_nth):
                for b in range(B):
                    ln_stats(L, part, b, x_ready, x_nth(b))
                for b in range(B):
                    ln_normalise(L, part, b)

            def cross_dve(L):
                def softmax(n):
                    dve.wait_ge(c_ready, L * NT + n + 1)
                    sc = ps[:, score_bank(n), :].rearrange("p (h s) -> p h s", s=S)
                    steps.add(dve.tensor_reduce(cmax[:, n % 2, :], sc, X, ALU.max))
                    steps.wait()
                    if n >= 2:
                        dve.wait_ge(c_exp, L * NT + n - 1)
                    dve.tensor_tensor(Ec[:, n % 2, :].rearrange("p (h s) -> p h s", s=S), sc,
                                      cmax[:, n % 2, :].unsqueeze(2).to_broadcast([128, H, S]),
                                      ALU.subtract).then_inc(c_sub, 1)

                def sums(n):
                    dve.wait_ge(c_exp, L * NT + n + 1)
                    steps.add(dve.tensor_reduce(csum[:, n % 2, :],
                                                Pc[:, n % 2, :].rearrange("p (h s) -> p h s", s=S), X, ALU.add))
                    steps.wait()
                    if n >= 2:
                        dve.wait_ge(c_norm, L * NT + n - 1)
                    dve.reciprocal(crec[:, n % 2, :], csum[:, n % 2, :]).then_inc(c_rec, 1)

                def add_out(n):
                    dve.wait_ge(bias_added, half_nth(L, CROSS, n // TB))
                    dve.wait_ge(co_ready, L * NT + n + 1)
                    dve.tensor_tensor(x[:, n, :], ps[:, 4 + n % 2, 0:C], x[:, n, :], ALU.add).then_inc(c_added, 1)

                for n in range(NT):
                    softmax(n)
                    if n >= 1:
                        sums(n - 1)
                    if n >= 4:
                        add_out(n - 4)
                    if n == NT - 1:
                        ln_stats(L, FF, 0, c_added, L * NT + TB)
                sums(NT - 1)
                add_out(NT - 4)
                ln_normalise(L, FF, 0)
                for n in range(NT - 3, NT):
                    add_out(n)
                ln_stats(L, FF, 1, c_added, L * NT + NT)
                ln_normalise(L, FF, 1)

            def ff_out(L):
                for b in range(B):
                    dve.wait_ge(bias_added, half_nth(L, FF, b))
                    dve.wait_ge(fo_ready, L * B + b + 1)
                    dve.tensor_tensor(x[:, rows_of(b), :], ps[:, 4 + b, :].rearrange("p (t c) -> p t c", c=C),
                                      x[:, rows_of(b), :], ALU.add).then_inc(ff_added, 1)
                    ln_stats(L + 1, ATTN, b, ff_added, L * B + b + 1)

            dve.wait_ge(consts_loaded, 32)
            dve.tensor_copy(ident_bf[:, :], ident).then_inc(bf_done, 1)
            dve.tensor_copy(tri_bf[:, :], tri).then_inc(bf_done, 1)
            layer_norm(0, ATTN, x_loaded, lambda b: 32)
            dve.wait_ge(zeroed, 5)
            for t in range(TB):
                dve.memset(pick[32 * t:32 * t + 1, t, :], 1.0).then_inc(setup_done, 1)
            dve.wait_ge(masks_loaded, 48)
            dve.tensor_scalar(tmr[:, :, :], tm8[:, :, :], -BIG, None, ALU.mult).then_inc(masks_done, 1)
            steps.add(dve.tensor_scalar(keep[:, :], km8[:, :], -1.0, 1.0, ALU.mult, ALU.add))
            steps.add(dve.tensor_scalar(em[:, :, :], em8[:, :, :], -BIG, None, ALU.mult))
            steps.add(dve.tensor_scalar(keepn[:, :, :], em8[:, :, :], -1.0, 1.0, ALU.mult, ALU.add))
            steps.wait()
            steps.add(dve.tensor_reduce(poison[:, 0:B], keepn[:, :, :], X, ALU.add))
            steps.wait()
            steps.add(dve.reciprocal(poison[:, B:2 * B], poison[:, 0:B]))
            steps.wait()
            steps.add(dve.tensor_scalar(poison[:, 2 * B:3 * B], poison[:, B:2 * B], 0.0, None, ALU.mult))
            dve.wait_ge(kv2_done, 2)
            for b in range(B):
                for src, dst in ((K2T, Ec), (V2T, Pc)):
                    ins = dve.tensor_tensor(dst[:, b, :].rearrange("p (h s) -> p h s", s=S),
                                            src[:, b * S:(b + 1) * S].unsqueeze(1).to_broadcast([128, H, S]),
                                            head_mask.unsqueeze(2).to_broadcast([128, H, S]), ALU.mult)
                ins.then_inc(blocks_done, 1)
            dve.wait_ge(w0_loaded, 64)
            for b in range(B):
                dve.wait_ge(v0_ready, b + 1)
                for t in range(TB):
                    ins = dve.tensor_tensor(Vaug[:, b * TB + t, :, 0:D0],
                                            ps[:, 2 + b, t * C:(t + 1) * C].rearrange("p (h d) -> p h d", d=D0),
                                            r0[:, 0, :].rearrange("p (h d) -> p h d", d=D0), ALU.add)
                steps.add(ins)
                steps.wait()
                for t in range(TB):
                    n = b * TB + t
                    dve.tensor_scalar(Vaug[:, n, :, 0:D0], Vaug[:, n, :, 0:D0], keep[:, n:n + 1], None, ALU.mult)
                    ins = dve.tensor_copy(Vaug[:, n, :, D0], keep[:, n:n + 1].to_broadcast([128, H]))
                ins.then_inc(v0_done, 1)
            for b in range(B):
                dve.wait_ge(qb_ready, b + 1)
                steps.add(dve.tensor_tensor(cross_bias[:, b, :].rearrange("p (h s) -> p h s", s=S),
                                            ps[0:1, 6 + b, :].rearrange("p (h s) -> p h s", s=S),
                                            em[:, b, :].unsqueeze(1).to_broadcast([1, H, S]), ALU.add))
                steps.wait()
                dve.tensor_scalar(cross_bias[:, b, :], cross_bias[:, b, :], poison[:, 2 * B + b:2 * B + b + 1], None,
                                  ALU.add).then_inc(cross_bias_done, 1)

            def q_part(u):
                dve.wait_ge(q0_hi, u + 1)
                steps.add(dve.tensor_scalar(Qt[:, :], ps[:, 0, :], wqk[:, 256:257], tQ, ALU.add, ALU.mult))
                steps.wait()
                dve.scalar_tensor_tensor(out=QX0[:, :], in0=QH[:, :].bitcast(f32), scalar=sQ, in1=Qt[:, :],
                                         op0=ALU.mult, op1=ALU.add).then_inc(q0_done, 1)

            def k_part(u, parity):
                dve.wait_ge(k0_hi, u + 1)
                steps.add(dve.tensor_scalar(Kt[:, :], ps[:, 1, :], wqk[:, 257:258], tK, ALU.add, ALU.mult))
                steps.wait()
                dve.scalar_tensor_tensor(out=KX0[:, parity, :], in0=KH[:, :].bitcast(f32), scalar=sK, in1=Kt[:, :],
                                         op0=ALU.mult, op1=ALU.add).then_inc(k0_done, 1)

            mcol0_heads = mcol0[:, :, :].rearrange("p t (j r) -> p t j r", r=32)

            def maxima0(u):
                for t in range(TB):
                    for j2 in range(2):
                        dve.wait_ge(d0_ready, (u * TB + t) * 2 + j2 + 1)
                        dve.tensor_reduce(mcol0_heads[:, t, 2 * j2:2 * j2 + 2, ROW_MAX],
                                          ps[:, 2 * j2:2 * j2 + 2, 0:(t + 1) * 128],
                                          X, ALU.max, negate=True).then_inc(d0_max, 1)

            def outputs0(u, heads, cols, b):
                dve.wait_ge(o0_turned, u + 1)
                o = ps[:, 7, :].rearrange("p (t j d) -> p t j d", j=G0, d=32)
                r = rden0[:, b, :].rearrange("p (t j) -> p t j", j=G0)
                steps.add(dve.reciprocal(r, o[:, :, :, D0]))
                steps.wait()
                for t in range(TB):
                    ins = dve.tensor_tensor(O0[:, b * TB + t, cols].rearrange("p (j d) -> p j d", d=D0),
                                            o[:, t, :, 0:D0], r[:, t, :].unsqueeze(2).to_broadcast([128, G0, D0]),
                                            ALU.mult)
                ins.then_inc(o0_done, 1)

            def values_of(u, g, b):
                if isinstance(u, int) and u < 2:
                    pass
                else:
                    dve.wait_ge(o0_ready, u - 1)
                for t in range(TB):
                    ins = dve.tensor_copy(Vg[:, b, t, :, 0:D0 + 1], Vaug[:, b * TB + t, heads_at(g), :])
                ins.then_inc(vg_done, 1)

            def heads_at(g):
                return bass.ds(g * G0, G0)

            def cols_at(g):
                return bass.ds(g * (G0 * D0), G0 * D0)

            def unit0(g, b, first=False, last=False, normalise=True):
                u = g * B + b
                dve.wait_ge(m0_ready, u + 1)
                dve.tensor_tensor(QM[:, b, :], ps[:, 6, :], QX0[:, :].bitcast(f32), ALU.add).then_inc(m0_done, 1)
                if normalise:
                    outputs0(u - 2, heads_at(g - 1), cols_at(g - 1), b)
                if not last:
                    dve.wait_ge(m0_done, u + 1)
                    q_part(u + 1)
                    k_part(u + 1, (b + 1) % 2)
                values_of(u, g, b)
                if not last:
                    maxima0(u + 1)

            dve.wait_ge(setup_done, 12)
            dve.wait_ge(wqk_loaded, 16)
            q_part(0)
            k_part(0, 0)
            maxima0(0)
            unit0(0, 0, first=True, normalise=False)
            unit0(0, 1, normalise=False)
            with dve.Fori(1, NG - 1) as g:
                kept = steps.enter(g - 1, 6)
                unit0(g, 0)
                unit0(g, 1)
                steps.leave(kept, NG - 2)
            unit0(NG - 1, 0)
            unit0(NG - 1, 1, last=True)
            for b in range(B):
                outputs0(UNITS0 - B + b, heads_at(NG - 1), cols_at(NG - 1), b)
            for b in range(B):
                dve.wait_ge(bias_added, half_nth(0, ATTN, b))
                dve.wait_ge(proj_ready, b + 1)
                dve.tensor_tensor(x[:, rows_of(b), :], ps[:, 2 + b, :].rearrange("p (t c) -> p t c", c=C),
                                  x[:, rows_of(b), :], ALU.add).then_inc(proj_added, 1)
            layer_norm(0, CROSS, proj_added, lambda b: b + 1)
            cross_dve(0)
            ff_out(0)

            with dve.Fori(0, LOOP_LAYERS) as l:
                kept_l = steps.enter(l, 3 * B + 2 * NT)

                def weights_lo(i, n):
                    dve.wait_ge(w_hi, pairs_nth(l, i) - 1 + n)
                    dve.tensor_tensor(Wl[:, n, :], of_pair(i, n), Wh[:, n, :].bitcast(f32),
                                      ALU.subtract).then_inc(w_lo, 1)

                for b in range(B):
                    ln_normalise(l + 1, ATTN, b)
                for n in range(2):
                    weights_lo(0, n)
                for b in range(B):
                    dve.wait_ge(ln_hT, half_nth(l + 1, ATTN, b))
                    dve.wait_ge(ln_hi, l * B + b + 1)
                    dve.tensor_tensor(hTl[:, cols_of(b)], hT[:, cols_of(b)], hTh[:, cols_of(b)].bitcast(f32),
                                      ALU.subtract).then_inc(ln_lo, 1)

                def lo_parts(i, k, slot):
                    dve.wait_ge(qk_hi, qk_nth(l, i, k, 2, 1))
                    for e in range(2):
                        own, other = slice(64 * e, 64 * e + 64), slice(64 - 64 * e, 128 - 64 * e)
                        if k % 2 == 0:
                            ins = dve.tensor_tensor(QX[other, slot + e, :], ps[own, 6, :],
                                                    QX[own, slot + e, :].bitcast(f32), ALU.subtract)
                        else:
                            ins = dve.tensor_tensor(KB[own, slot + e, :], ps[own, 6, :],
                                                    KX[own, slot + e, :].bitcast(f32), ALU.subtract)
                    ins.then_inc(qk_lo, 1)

                def maximum(i, k, t):
                    dve.wait_ge(d_ready, nth(l, i, k, TB, t))
                    dve.tensor_reduce(mcol[:, t:t + 1], ps[:, 4 + t % 2, :], X, ALU.max, negate=True)\
                       .then_inc(d_max, 1)

                def inverse_sums(i, b):
                    dve.wait_ge(l_ready, couple_nth(l, i, b))
                    dve.reciprocal(Lr, ps[:, 5, 0:2 * 128]).then_inc(l_rec, 1)

                def normalise(i, b):
                    dve.wait_ge(o_copied, couple_nth(l, i, b))
                    dve.wait_ge(l_spread, couple_nth(l, i, b))
                    dve.tensor_tensor(On, ps[:, 7, :], Os, ALU.mult).then_inc(o_norm, 1)

                def add_output(i, b):
                    dve.wait_ge(op_ready, couple_nth(l, i, b))
                    dve.tensor_tensor(x[:, rows_of(b), :], ps[:, 7, :].rearrange("p (t c) -> p t c", c=C),
                                      x[:, rows_of(b), :], ALU.add).then_inc(o_done, 1)

                def unit(i, k, first=False, last=False):
                    e = k % 2
                    before = (i, 0) if k >= 2 else None if first else (i - 1, 1)
                    more = not (i is LAST and k >= 2)
                    dve.wait_ge(m_ready, nth(l, i, k, 1, 0))
                    dve.tensor_tensor(QB[64 - 64 * e:64 - 64 * e + TB, k, :].rearrange("p (t q) -> p t q", t=TB),
                                      ps[0:TB, 5, 0:128].unsqueeze(1).to_broadcast([TB, TB, 128]),
                                      ident[0:TB, 0:TB].unsqueeze(2).to_broadcast([TB, TB, 128]), ALU.mult)\
                       .then_inc(m_done, 1)
                    if not last:
                        maximum(i, k + 1, 0)
                        maximum(i, k + 1, 1)
                    if e == 0:
                        if not first:
                            add_output(i - 1, k // 2)
                        if before:
                            inverse_sums(*before)
                    if more:
                        lo_parts(i, k, (k // 2 * 2 + 2) % 4)
                    if not last:
                        maximum(i, k + 1, 2)
                        maximum(i, k + 1, 3)
                    if e == 1 and before:
                        normalise(*before)
                    if i is not LAST and k == 1:
                        for n in range(2):
                            weights_lo(i + 1, n)

                dve.wait_ge(bias_added, half_nth(l + 1, ATTN, B - 1))
                lo_parts(0, -2, 0)
                lo_parts(0, -1, 0)
                for t in range(TB):
                    maximum(0, 0, t)
                for k in range(4):
                    unit(0, k, first=True)
                with dve.Fori(1, LAST) as i:
                    for k in range(4):
                        unit(i, k)
                for k in range(4):
                    unit(LAST, k, last=k == 3)
                add_output(LAST, 0)
                ln_stats(l + 1, CROSS, 0, o_done, couple_nth(l, LAST, 0))
                inverse_sums(LAST, 1)
                ln_normalise(l + 1, CROSS, 0)
                normalise(LAST, 1)
                add_output(LAST, 1)
                ln_stats(l + 1, CROSS, 1, o_done, couple_nth(l, LAST, 1))
                ln_normalise(l + 1, CROSS, 1)
                cross_dve(l + 1)
                for b in range(B):
                    for j in range(FC):
                        n = b * FC + j
                        dve.wait_ge(f_gelu, (l + 1) * B * FC + n + 1)
                        dve.scalar_tensor_tensor(out=uT[:, b, j, :], in0=ps[:, 2 * (n % 2) + 1, :],
                                                 scalar=vl[:, 6 + j:7 + j], in1=gl[:, n % 2, :],
                                                 op0=ALU.add, op1=ALU.mult).then_inc(f_u, 1)
                ff_out(l + 1)
                steps.leave(kept_l, LOOP_LAYERS)

        @block.tensor
        def _(pe):
            def turn_ln(L, part, halves=range(B)):
                for b in halves:
                    pe.wait_ge(ln_xhat, half_nth(L, part, b))
                    for t in range(TB):
                        mm = pe.transpose(ps[:, 6 + b, t * 128:(t + 1) * 128], xhat[:, b * TB + t, :], ident)
                    mm.then_inc(ln_turned, 1)

            def cross_pe(L, with_bias):
                def scores(n):
                    b = n // TB
                    if n == 0:
                        pe.wait_ge(ln_hT, half_nth(L, CROSS, 0))
                    if n == 3:
                        pe.wait_ge(ln_hT, half_nth(L, CROSS, 1))
                    if n >= 4:
                        pe.wait_ge(c_sub, L * NT + n - 3)
                    mm = pe.matmul(ps[:, score_bank(n), :], hT[:, n * 128:(n + 1) * 128], Gm[:, b, :], start=True,
                                   stop=not with_bias)
                    if with_bias:
                        mm = pe.matmul(ps[:, score_bank(n), :], ones_row[:, :], cross_bias[:, b, :], start=False, stop=True)
                    mm.then_inc(c_ready, 1)

                def turn(n):
                    pe.wait_ge(c_norm, L * NT + n + 1)
                    if n >= 2:
                        pe.wait_ge(ct_done, L * NT + n - 1)
                    for j in range(4):
                        mm = pe.transpose(ps[:, 2 + n % 2, j * 128:(j + 1) * 128], Pc[:, n % 2, j * 128:(j + 1) * 128],
                                          ident)
                    mm.then_inc(ct_ready, 1)

                def outs(n):
                    pe.wait_ge(ct_done, L * NT + n + 1)
                    if n >= 2:
                        pe.wait_ge(c_added, L * NT + n - 1)
                    for j in range(4):
                        mm = pe.matmul(ps[:, 4 + n % 2, 0:C], P2T[:, n % 2, j, :], Um[:, n // TB, j, :],
                                       start=j == 0, stop=j == 3)
                    mm.then_inc(co_ready, 1)

                scores(0)
                scores(1)
                turn_ln(L, CROSS, (1,))
                scores(2)
                scores(3)
                for n in range(NT):
                    turn(n)
                    if n >= 1:
                        outs(n - 1)
                    if n + 4 < NT:
                        scores(n + 4)
                outs(NT - 1)
                turn_ln(L, FF, (0,))

            def ff_pe(L, hidden, w_out, used):
                def outs(b):
                    pe.wait_ge(*used(b * FC + FC - 1))
                    for t in range(TB):
                        for j in range(FC):
                            mm = pe.matmul(ps[:, 4 + b, t * C:(t + 1) * C], uT[:, b, j, t * 128:(t + 1) * 128],
                                           w_out[:, j, :], start=j == 0, stop=j == FC - 1)
                    mm.then_inc(fo_ready, 1)

                def hid(n):
                    b, j = n // FC, n % FC
                    if j == 0:
                        pe.wait_ge(ln_hT, half_nth(L, FF, b))
                    if n >= 2:
                        pe.wait_ge(*used(n - 2))
                    for bank, w in hidden(n, j):
                        mm = pe.matmul(ps[:, bank, :], w, hT[:, cols_of(b)], start=True, stop=True)
                    mm.then_inc(f_ready, 1)

                for n in range(FC + 2):
                    if n == 2:
                        turn_ln(L, FF, (1,))
                    hid(n)
                outs(0)
                for n in range(FC + 2, 2 * FC):
                    hid(n)
                outs(1)

            pe.wait_ge(w0_loaded, 64)
            pe.matmul(ps[:, 4, 0:B * S], wkv0[:, 0:C], ctxT[:, :], start=True, stop=True)
            pe.matmul(ps[:, 4, B * S:2 * B * S], wkv0[:, C:2 * C], ctxT[:, :], start=True, stop=True)\
              .then_inc(kv2_ready, 1)
            pe.wait_ge(consts_loaded, 32)
            turn_ln(0, ATTN)
            for b in range(B):
                pe.wait_ge(ln_hT, b + 1)
                for t in range(TB):
                    n = b * TB + t
                    mm = pe.matmul(ps[:, 2 + b, t * C:(t + 1) * C], hT[:, n * 128:(n + 1) * 128], w0_v, start=True,
                                   stop=True)
                mm.then_inc(v0_ready, 1)
            for b in range(B):
                pe.wait_ge(blocks_done, b + 1)
                pe.matmul(ps[:, b, :], w0_qT, Ec[:, b, :], start=True, stop=True).then_inc(g_ready, 1)
                pe.matmul(ps[0:1, 6 + b, :], v0[:, 12:13], Ec[:, b, :], start=True, stop=True).then_inc(qb_ready, 1)
            for b in range(B):
                for j in range(4):
                    mm = pe.matmul(ps[:, 4 + b, j * C:(j + 1) * C], Pc[:, b, j * 128:(j + 1) * 128], w0_out,
                                   start=True, stop=True)
                mm.then_inc(u_ready, 1)

            def q_proj(u, b):
                pe.matmul(ps[:, 0, :], wqk[:, 0:128], hT[:, cols_of(b)], start=True, stop=True).then_inc(q0_ready, 1)

            def k_proj(u, b):
                pe.matmul(ps[:, 1, :], wqk[:, 128:256], hT[:, cols_of(b)], start=True, stop=False)
                pe.matmul(ps[:, 1, :], onehot[:, :], tmr[:, b, :], start=False, stop=True).then_inc(k0_ready, 1)

            def row_max_scores(u, b, t, j2, first=False):
                if t == 0 and j2 == 0:
                    pe.wait_ge(k0_done, u + 1)
                elif t == 0:
                    if not first:
                        pe.wait_ge(s0_exp, u * TB * 2 - 1)
                else:
                    pe.wait_ge(d0_max, (u * TB + t) * 2 + j2 - 1)
                w = (t + 1) * 128
                for j in (2 * j2, 2 * j2 + 1):
                    rows_j = slice(32 * j, 32 * j + 32)
                    pe.matmul(ps[:, j, 0:w], QX0[rows_j, t * 128:w], KX0[rows_j, b, 0:w], start=True, stop=False)
                    mm = pe.matmul(ps[:, j, w - 128:w], ident_bf[:, :], tri_bf[:, :], start=False, stop=True)
                mm.then_inc(d0_ready, 1)

            def turn_maxima(u, t):
                if t < TB - 1:
                    pe.wait_ge(d0_max, (u * TB + t) * 2 + 2)
                mm = pe.transpose(ps[:, 6, t * 128:(t + 1) * 128], mcol0[:, t, :], ident)
                if t == TB - 1:
                    mm.then_inc(m0_ready, 1)

            def maxima_and_scores(u, b, first=False, between=()):
                for n in range(2 * TB):
                    t, j2 = n // 2, n % 2
                    row_max_scores(u, b, t, j2, first)
                    if j2 == 1 and t > 0:
                        turn_maxima(u, t - 1)
                    if between:
                        mm = weighted0(b, between[n])
                        if n == 2 * TB - 1:
                            mm.then_inc(o0_ready, 1)

            def turned_scores(u, b, t, fresh):
                for j2 in range(2):
                    if not (fresh and t == 0):
                        pe.wait_ge(s0_exp, (u * TB + t) * 2 + j2 - 1)
                    for jj in range(2):
                        rows_j = slice(32 * (2 * j2 + jj), 32 * (2 * j2 + jj) + 32)
                        mm = pe.matmul(ps[:, 2 + 2 * j2 + jj, 0:T - t * 128], KX0[rows_j, b, t * 128:(t + 1) * 128],
                                       QM[rows_j, b, t * 128:T], start=True, stop=True)
                    mm.then_inc(s0_ready, 1)

            pieces0 = [(j, s) for s in range(TB) for j in range(G0)]

            def weighted0(b, pieces):
                for j, s in pieces:
                    mm = pe.matmul(ps[32 * j:32 * j + 32, 7, s * 128:T], Vg[:, b, s, j, :],
                                   P0[:, b, j, s * T + s * 128:(s + 1) * T], start=s == 0, stop=s == TB - 1)
                return mm

            def turn_sums(u):
                pe.wait_ge(o0_copied, u + 1)
                for t in range(TB):
                    mm = pe.transpose(ps[:, 7, t * 128:(t + 1) * 128], OS[:, t * 128:(t + 1) * 128], ident)
                mm.then_inc(o0_turned, 1)

            def unit0(u, b, first=False, last=False, next_group=None, turns=True):
                if not last:
                    pe.wait_ge(d0_max, (u + 1) * TB * 2 - 1)
                    if next_group is not None:
                        pe.wait_ge(wqk_loaded, next_group * 16 + 16)
                    q_proj(u + 1, (b + 1) % 2)
                    k_proj(u + 1, (b + 1) % 2)
                pe.wait_ge(d0_max, (u + 1) * TB * 2)
                turn_maxima(u, TB - 1)
                if turns:
                    turn_sums(u - 2)
                pe.wait_ge(m0_done, u + 1)
                turned_scores(u, b, 0, first)
                if not first:
                    pe.wait_ge(s0_masked, u * TB)
                    pe.wait_ge(vg_done, u)
                    if turns:
                        pe.wait_ge(o0_done, u - 1)
                for t in range(1, TB):
                    turned_scores(u, b, t, False)
                    if not first:
                        weighted0((b + 1) % 2, pieces0[(t - 1) * 1:t * 1])
                if not last:
                    rest = pieces0[3 * 1:]
                    maxima_and_scores(u + 1, (b + 1) % 2,
                                      between=() if first else [rest[13 * n // 8:13 * (n + 1) // 8] for n in range(8)])
                elif not first:
                    weighted0((b + 1) % 2, pieces0[3 * 1:]).then_inc(o0_ready, 1)

            pe.wait_ge(bf_done, 2)
            pe.wait_ge(masks_done, 1)
            pe.wait_ge(setup_done, 12)
            pe.wait_ge(cross_bias_done, B)
            pe.wait_ge(g_done, B)
            pe.wait_ge(v0_done, B)
            pe.wait_ge(u_done, B)
            pe.wait_ge(wqk_loaded, 16)
            q_proj(0, 0)
            k_proj(0, 0)
            maxima_and_scores(0, 0, first=True)
            unit0(0, 0, first=True, turns=False)
            unit0(1, 1, next_group=1, turns=False)
            with pe.Fori(1, NG - 1) as g:
                unit0(g * B, 0)
                unit0(g * B + 1, 1, next_group=g + 1)
            unit0(UNITS0 - 2, 0)
            unit0(UNITS0 - 1, 1, last=True)
            turn_sums(UNITS0 - 2)
            pe.wait_ge(s0_masked, UNITS0 * TB)
            pe.wait_ge(vg_done, UNITS0)
            pe.wait_ge(o0_done, UNITS0 - 1)
            weighted0(1, pieces0).then_inc(o0_ready, 1)
            turn_sums(UNITS0 - 1)
            for b in range(B):
                pe.wait_ge(o0_done, UNITS0 - B + b + 1)
                for t in range(TB):
                    mm = pe.transpose(ps[:, b, t * 128:(t + 1) * 128], O0[:, b * TB + t, :], ident)
                mm.then_inc(ot0_ready, 1)
            for b in range(B):
                pe.wait_ge(ot0_done, b + 1)
                for t in range(TB):
                    n = b * TB + t
                    mm = pe.matmul(ps[:, 2 + b, t * C:(t + 1) * C], OT0[:, n * 128:(n + 1) * 128], w0_proj,
                                   start=True, stop=True)
                mm.then_inc(proj_ready, 1)
            turn_ln(0, CROSS, (0,))
            cross_pe(0, True)
            ff_pe(0, lambda n, j: [(2 * (n % 2), w0_m1[:, j * 128:(j + 1) * 128])], w0_m2, lambda n: (f_gelu, n + 1))

            with pe.Fori(0, LOOP_LAYERS) as l:
                pe.wait_ge(cross_loaded, l * 32 + 32)
                for n in range(2):
                    for j in range(H // 2):
                        mm = pe.matmul(ps[:, n, j * B * S:(j + 1) * B * S], wc[:, n, j * 128:(j + 1) * 128],
                                       ctxT[:, :], start=True, stop=True)
                    mm.then_inc(kv2_ready, 1)
                turn_ln(l + 1, ATTN, (0,))
                pe.wait_ge(kv2_done, 2 + l * 2 + 2)
                for r in range(2):
                    for j in range(4 * r, 4 * r + 4):
                        mm = pe.matmul(ps[:, 2 + r, (j % 4) * 128:(j % 4 + 1) * 128], wx[:, j, 0:C],
                                       K2b[:, j, :, :].rearrange("p b n -> p (b n)"), start=True, stop=True)
                    mm.then_inc(g_ready, 1)
                turn_ln(l + 1, ATTN, (1,))
                for b in range(B):
                    for j in range(H // 2):
                        mm = pe.matmul(ps[64 * (j % 2):64 * (j % 2) + 64, 4 + b, (j // 2) * C:(j // 2 + 1) * C],
                                       V2b[:, j, b, :], wx[:, j, C:2 * C], start=True, stop=True)
                    mm.then_inc(u_ready, 1)

                def project(i, k):
                    n, cols = k % 2, cols_of((k // 2 + 1) % 2)
                    if k // 2 != 0:
                        pe.wait_ge(w_lo, pairs_nth(l, 0 if k < 0 else i + 1) - 1 + n)
                    pe.matmul(ps[:, 6, :], Wh[:, n, :], hTh[:, cols], start=True, stop=False)
                    pe.matmul(ps[:, 6, :], Wl[:, n, :], hTh[:, cols], start=False, stop=False)
                    pe.matmul(ps[:, 6, :], Wh[:, n, :], hTl[:, cols], start=False, stop=True).then_inc(qk_ready, 1)

                def values(i, b):
                    for t in range(TB):
                        n = b * TB + t
                        mm = pe.matmul(ps[:, 6, t * C:(t + 1) * C], hT[:, n * 128:(n + 1) * 128], of_pair(i, 2),
                                       start=True, stop=True)
                    mm.then_inc(v_ready, 1)

                def row_max_scores(i, k, t, fresh=False):
                    if not fresh:
                        pe.wait_ge(d_max, nth(l, i, k, TB, t) - 2)
                    pe.matmul(ps[:, 4 + t % 2, :], QX[:, k % 4, t * 128:(t + 1) * 128], KX[:, k % 4, :],
                              start=True, stop=True).then_inc(d_ready, 1)

                def turned_scores(i, k, e, fresh):
                    if not fresh:
                        pe.wait_ge(s_exp, nth(l, i, k, 2, e) - 2)
                    for s in range(2 * e, 2 * e + 2):
                        keys = slice(s * 128, (s + 1) * 128)
                        pe.matmul(ps[:, s, :], KX[:, k, keys], QX[:, k, :], start=True, stop=False)
                        mm = pe.matmul(ps[:, s, :], KB[:, k, keys], QB[:, k, :], start=False, stop=True)
                    mm.then_inc(s_ready, 1)

                def weighted(b, s):
                    for e in range(2):
                        mm = pe.matmul(ps[64 * e:64 * e + 64, 7, :], V[:, b, s, 64 * e:64 * e + 64],
                                       Pt[:, 2 * b + e, s, :], start=s == 0, stop=s == TB - 1)
                    if s == TB - 1:
                        mm.then_inc(o_ready, 1)

                def denominators(i, b):
                    pe.wait_ge(p_sum, nth(l, i, 2 * b + 1, 1, 0))
                    for e in range(2):
                        for t in range(TB):
                            mm = pe.matmul(ps[32 * t:32 * t + 32, 5, e * 128:(e + 1) * 128], ones[:, :],
                                           Psum[:, 2 * b + e, t * 128:(t + 1) * 128], start=True, stop=True)
                    mm.then_inc(l_ready, 1)

                def spread_inverse(i, b):
                    pe.wait_ge(l_rec, couple_nth(l, i, b))
                    pe.wait_ge(o_copied, couple_nth(l, i, b))
                    for t in range(TB):
                        for e in range(2):
                            mm = pe.matmul(ps[64 * e:64 * e + 64, 7, t * 128:(t + 1) * 128], pick[:, t, :],
                                           Lr[:, e * 128:(e + 1) * 128], start=True, stop=True)
                    mm.then_inc(l_spread, 1)

                def out_rows(i, b):
                    pe.wait_ge(o_norm, couple_nth(l, i, b))
                    for t in range(TB):
                        mm = pe.matmul(ps[:, 7, t * C:(t + 1) * C], On[:, t * 128:(t + 1) * 128], of_pair(i, 3),
                                       start=True, stop=True)
                    mm.then_inc(op_ready, 1)

                def unit(i, k, first=False, last=False):
                    b, e = k // 2, k % 2
                    before = (i, 0) if b == 1 else None if first else (i - 1, 1)
                    none_before = first and k == 0
                    more = not (i is LAST and k >= 2)
                    pe.wait_ge(d_max, nth(l, i, k, TB, TB - 1))
                    pe.transpose(ps[0:TB, 5, 0:128], mcol[:, 0:TB], ident).then_inc(m_ready, 1)
                    if not last:
                        if e == 1 and more:
                            pe.wait_ge(qk_hi, qk_nth(l, i, k, 2, 0))
                        row_max_scores(i, k + 1, 0)
                    if e == 0:
                        if not first:
                            out_rows(i - 1, b)
                    elif before:
                        weighted(before[1], 3)
                    pe.wait_ge(m_done, nth(l, i, k, 1, 0))
                    if not last:
                        row_max_scores(i, k + 1, 1)
                    if e == 0:
                        pe.wait_ge(v_done, couple_nth(l, i, b))
                        if more:
                            project(i, k)
                    turned_scores(i, k, 0, none_before)
                    if e == 0 and before:
                        pe.wait_ge(d_max, nth(l, i, k + 1, TB, 1))
                        denominators(*before)
                        if not (first and b == 1):
                            pe.wait_ge(o_done, couple_nth(l, *before) - 1)
                        weighted(before[1], 0)
                        weighted(before[1], 1)
                    turned_scores(i, k, 1, none_before)
                    if not last:
                        row_max_scores(i, k + 1, 2)
                        if e == 0 and before:
                            pe.wait_ge(l_rec, couple_nth(l, *before))
                        row_max_scores(i, k + 1, 3)
                    if e == 0:
                        if more:
                            pe.wait_ge(qk_lo, qk_nth(l, i, k))
                            project(i, k + 1)
                        if before:
                            weighted(before[1], 2)
                    else:
                        if before:
                            spread_inverse(*before)
                        if more:
                            pe.wait_ge(qk_lo, qk_nth(l, i, k))
                            values(*((i, 1) if k == 1 else (i + 1, 0)))

                pe.wait_ge(setup_done, 12)
                pe.wait_ge(wa_loaded, l * 16 + 16)
                pe.wait_ge(ln_hT, half_nth(l + 1, ATTN, B - 1))
                pe.wait_ge(ln_lo, (l + 1) * B)
                project(0, -2)
                pe.wait_ge(qk_lo, qk_nth(l, 0, -2))
                project(0, -1)
                pe.wait_ge(qk_lo, qk_nth(l, 0, -1))
                values(0, 0)
                pe.wait_ge(u_done, B + (l + 1) * 2)
                for t in range(TB):
                    row_max_scores(0, 0, t, fresh=t < 2)
                for k in range(4):
                    unit(0, k, first=True)
                with pe.Fori(1, LAST) as i:
                    for k in range(4):
                        unit(i, k)
                for k in range(4):
                    unit(LAST, k, last=k == 3)
                pe.wait_ge(s_exp, nth(l, LAST, 3, 2, 1))
                out_rows(LAST, 0)
                pe.wait_ge(o_done, couple_nth(l, LAST, 0))
                for s in range(TB):
                    weighted(1, s)
                denominators(LAST, 1)
                spread_inverse(LAST, 1)
                turn_ln(l + 1, CROSS, (0,))
                out_rows(LAST, 1)
                cross_pe(l + 1, False)
                pe.wait_ge(ff_loaded, l * 16 + 16)
                ff_pe(l + 1, lambda n, j: [(2 * (n % 2), w_p[:, HID + j * 128:HID + (j + 1) * 128]),
                                           (2 * (n % 2) + 1, w_p[:, j * 128:(j + 1) * 128])], w_2,
                      lambda n: (f_u, l * B * FC + n + 1))


def kernel(**inputs):
    import numpy as _np
    import concourse.bacc as _bacc
    from concourse import mybir as _mybir
    from concourse.bass_utils import run_bass_kernel_spmd as _run

    a = {k: _np.asarray(v) for k, v in inputs.items()}
    f = a["x"].dtype
    l0 = {k[len("L0_xattn_"):]: v for k, v in a.items() if k.startswith("L0_")}

    consts = _np.zeros((128, 260 + H), f)
    consts[:, 0:128] = _np.eye(128)
    consts[:, 128:256] = _np.triu(_np.full((128, 128), -BIG), 1)
    row = _np.arange(128) % 32
    consts[:, 256] = _np.where((row < D0) | ((row >= 2 * D0) & (row <= ROW_MASK)), 1, 0) - _np.where((row >= D0) & (row < 2 * D0), 1, 0)
    consts[:, 257] = (row >= D0) & (row < 2 * D0)
    consts[:, 258] = _np.where((row < 2 * D0) | (row == ROW_MASK) | (row == ROW_MAX), 1, 0) - _np.where((row >= 2 * D0) & (row < 3 * D0), 1, 0)
    consts[:, 259] = (row >= 2 * D0) & (row < 3 * D0)
    for h in range(H):
        consts[h * D0:(h + 1) * D0, 260 + h] = 1

    w0_qk = _np.zeros((NG, 128, 258), f)
    for g in range(NG):
        for j in range(G0):
            cols = slice((g * G0 + j) * D0, (g * G0 + j + 1) * D0)
            for copy in range(3):
                at = 32 * j + copy * D0
                for n in range(2):
                    w0_qk[g, :, 128 * n + at:128 * n + at + D0] = l0["qkv_w"][:, n * C:(n + 1) * C][:, cols]
                    w0_qk[g, at:at + D0, 256 + n] = l0["qkv_b"][n * C:(n + 1) * C][cols]
            w0_qk[g, 32 * j + ROW_MASK, 256] = 1
            w0_qk[g, 32 * j + ROW_MAX, 257] = 1

    def chunks(w):
        return w.reshape(-1, 128, w.shape[1]).transpose(1, 0, 2).reshape(128, -1)

    w0 = _np.concatenate([l0["qkv_w"][:, 2 * C:], l0["proj_w"], l0["q_w"].T, l0["out_w"], l0["mlp1_w"],
                          chunks(l0["mlp2_w"])], axis=1)
    wk0 = _np.concatenate([l0["k_w"], l0["v_w"]], axis=1)
    vec0 = _np.stack([l0["ln1_w"], l0["ln1_b"], l0["ln2_w"], l0["ln2_b"], l0["ln3_w"], l0["ln3_b"],
                      *l0["mlp1_b"].reshape(FC, 128), l0["k_b"], l0["v_b"], l0["q_b"]], axis=1)
    rows0 = _np.stack([l0["qkv_b"][2 * C:], l0["proj_b"], l0["out_b"], l0["mlp2_b"]])

    n1, n2, n3 = "L1_xattn_", "L2_xattn_", "L3_xattn_"

    def three(first, second, third, turned=True):
        second = a[n2 + second]
        return a[n1 + first], second.T if turned else second, a[n3 + third]

    def stack(*parts):
        return _np.stack([_np.concatenate(layer, axis=-1) for layer in zip(*parts)])

    def by_head(ws):
        return [w.T.reshape(H, D, C) for w in ws]

    def out_by_head(ws):
        return [w.reshape(H, D, C) for w in ws]

    def pair_cols(ws):
        return [w.reshape(C, H // 2, 2 * D).transpose(1, 0, 2) for w in ws]

    def pair_rows(ws):
        return [w.reshape(H // 2, 2 * D, C) for w in ws]

    def by_pair(ws):
        return [w.reshape(H // 2, 128, C).transpose(1, 0, 2) for w in ws]

    w_attn = stack(pair_cols(three("Wq1", "wq1", "q1_w")), pair_cols(three("Wk1", "wk1", "k1_w")),
                   pair_cols(three("Wv1", "wv1", "v1_w")), pair_rows(three("Wo1", "wo1", "o1_w")))
    w_attn = w_attn.transpose(0, 2, 1, 3).reshape(LOOP_LAYERS, 128, -1)
    w_ctx = stack(three("Wk2", "wk2", "k2_w"), three("Wv2", "wv2", "v2_w"))
    w_cross = stack(by_pair(by_head(three("Wq2", "wq2", "q2_w"))), by_pair(out_by_head(three("Wo2", "wo2", "o2_w"))))
    w_cross = w_cross.reshape(LOOP_LAYERS, 128, -1)
    w_ff = stack(three("Wp", "w_geglu", "ff1_w"), [chunks(w) for w in three("W2", "w_ffout", "ff2_w")])

    def col(ws):
        return [w.reshape(-1, 128).T for w in ws]

    vec = stack(*(col(three(*names, turned=False)) for names in (
        ("g1", "ln1_g", "n1_w"), ("be1", "ln1_b", "n1_b"), ("g2", "ln2_g", "n2_w"), ("be2", "ln2_b", "n2_b"),
        ("g3", "ln3_g", "n3_w"), ("be3", "ln3_b", "n3_b"), ("bp", "b_geglu", "ff1_b"))))
    rows = _np.stack([_np.stack(three(*names, turned=False)) for names in (
        ("bo1", "bo1", "o1_b"), ("bo2", "bo2", "o2_b"), ("b2", "b_ffout", "ff2_b"))], axis=1)
    ctx_t = a["ctx_768"].reshape(B * S, CE).T

    arrays, args = {}, []
    for name, v in (("x", a["x"]), ("ctx_t", ctx_t), ("tgt_mask", a["mask_BxS_bf0"]), ("enc_mask", a["mask_BxS2_bf0"]),
                    ("consts", consts), ("w0_qk", w0_qk), ("w0", w0), ("wk0", wk0), ("vec0", vec0), ("rows0", rows0),
                    ("w_attn", w_attn), ("w_ctx", w_ctx), ("w_cross", w_cross), ("w_ff", w_ff), ("vec", vec),
                    ("rows", rows)):
        arrays["in_" + name] = _np.ascontiguousarray(v)
    nc = _bacc.Bacc("TRN2", target_bir_lowering=False, num_devices=1)
    for name, v in arrays.items():
        args.append(nc.dram_tensor(name, v.shape, _mybir.dt.from_np(v.dtype), kind="ExternalInput").ap())
    out = nc.dram_tensor("out", (B, T, C), _mybir.dt.float32, kind="ExternalOutput").ap()
    decoder_stack_kernel(nc, *args, out)
    r = _run(nc, [arrays], core_ids=[0])
    return r.results[0]["out"]
```

```python
import concourse.bass as bass
from concourse import mybir
from contextlib import ExitStack


B, T, C = 2, 512, 128
NT = B * T // 128
TB = T // 128
S, CE = 32, 96
H = 16
D0 = C // H
D = 64
HID = 512
FC = HID // 128
G0 = 4
NG = H // G0
TURNS = H // 2
LOOP_LAYERS = 3
ROW_MASK, ROW_MAX = 3 * D0, 3 * D0 + 1
BIG = 1e30


class Steps:

    def __init__(self, engine, semaphore):
        self.engine, self.semaphore, self.base, self.n = engine, semaphore, 0, 0

    def add(self, instruction):
        instruction.then_inc(self.semaphore, 1)
        self.n += 1

    def wait(self):
        self.engine.wait_ge(self.semaphore, self.base + self.n)

    def enter(self, index, per_turn):
        kept = (self.base, self.n, per_turn)
        self.base, self.n = self.base + self.n + index * per_turn, 0
        return kept

    def leave(self, kept, turns):
        base, n, per_turn = kept
        assert self.n == per_turn, (self.n, per_turn)
        self.base, self.n = base, n + turns * per_turn


def decoder_stack_kernel(nc, x_in, ctx_t, tgt_mask, enc_mask, consts, w0_qk, w0, wk0, vec0, rows0,
                         w_attn, w_ctx, w_cross, w_ff, vec, rows, out):
    f32, f32r, bf16, u8 = mybir.dt.float32, mybir.dt.float32r, mybir.dt.bfloat16, mybir.dt.uint8
    ALU = mybir.AluOpType
    ACT = mybir.ActivationFunctionType
    X = mybir.AxisListType.X
    EPS = 1e-5
    SCALE0 = float(D0) ** -0.5
    SCALE = float(D) ** -0.5

    x_dram = x_in.rearrange("b (t p) c -> p (b t) c", p=128)
    out_dram = out.rearrange("b (t p) c -> p (b t) c", p=128)

    ctx = ExitStack()
    with ctx:
        def sb(name, shape, dt=f32):
            return ctx.enter_context(nc.sbuf_tensor(name, shape, dt))

        def sem(name):
            return ctx.enter_context(nc.semaphore(name))

        x = sb("x", [128, NT, C])
        xhat = sb("xhat", [128, NT, C])
        hT = sb("hT", [128, NT * 128])
        hTh = sb("hTh", [128, NT * 128], f32r)
        hTl = sb("hTl", [128, NT * 128], f32r)
        stats = sb("stats", [128, NT, 6])
        mv = sb("mv", [128, NT, 2])
        veps = sb("veps", [128, NT])
        rstd = sb("rstd", [128, NT])
        mhalf = sb("mhalf", [128, NT])
        cst = sb("cst", [128, 128 + 128 + 4 + H])
        ident, tri = cst[:, 0:128], cst[:, 128:256]
        sQ, tQ, sK, tK = (cst[:, 256 + n:257 + n] for n in range(4))
        head_mask = cst[:, 260:260 + H]
        ident_bf = sb("ident_bf", [128, 128], bf16)
        tri_bf = sb("tri_bf", [128, 128], bf16)
        ones_row = sb("ones_row", [1, 128])
        ctxT = sb("ctxT", [CE, B * S])

        wqk = sb("wqk", [128, 2 * 128 + 2])
        wl0 = sb("wl0", [128, 4 * C + HID + FC * C])
        w0_v, w0_proj, w0_qT, w0_out = (wl0[:, n * C:(n + 1) * C] for n in range(4))
        w0_m1 = wl0[:, 4 * C:4 * C + HID]
        w0_m2 = wl0[:, 4 * C + HID:4 * C + 2 * HID].rearrange("p (j c) -> p j c", j=FC)
        wkv0 = sb("wkv0", [CE, 2 * C])
        v0 = sb("v0", [128, 13])
        r0 = sb("r0", [128, 4, C])

        wc = sb("wc", [CE, 2, H * D])
        wx = sb("wx", [128, H // 2, 2 * C])
        wf = sb("wf", [128, 2 * HID + FC * C])
        w_p, w_2 = wf[:, 0:2 * HID], wf[:, 2 * HID:].rearrange("p (j c) -> p j c", j=FC)
        vl = sb("vl", [128, 14])
        rl = sb("rl", [128, 3, C])

        Wh = sb("Wh", [128, 2, C], f32r)
        Wl = sb("Wl", [128, 2, C], f32r)
        QX = sb("QX", [128, 4, T], f32r)
        KX = sb("KX", [128, 4, T], f32r)
        KB = sb("KB", [128, 4, T], f32r)
        QB = sb("QB", [128, 4, T], f32r)
        V = sb("V", [128, B, TB, C])
        ones = sb("ones", [128, 32])
        pick = sb("pick", [128, TB, D])
        mcol = sb("mcol", [128, TB])

        K2T = sb("K2T", [128, B * S])
        V2T = sb("V2T", [128, B * S])
        K2b = sb("K2b", [128, H // 2, B, 2 * S])
        V2b = sb("V2b", [128, H // 2, B, 2 * S])
        Gm = sb("Gm", [128, B, H * S])
        Um = sb("Um", [128, B, 4, C])
        cross_bias = sb("cross_bias", [1, B, H * S])
        em8 = sb("em8", [1, B, S], u8)
        em = sb("em", [1, B, S])
        keepn = sb("keepn", [1, B, S])
        poison = sb("poison", [1, 3 * B])
        cmax = sb("cmax", [128, 2, H])
        csum = sb("csum", [128, 2, H])
        crec = sb("crec", [128, 2, H])
        Ec = sb("Ec", [128, 2, H * S])

        Vaug = sb("Vaug", [128, NT, H, D0 + 1])
        Vg = sb("Vg", [128, 2, TB, G0, 32])
        OS = V[:, 0, :, :].rearrange("p t c -> p (t c)")
        QH, KH, QX0 = QX[:, 0, :], QX[:, 1, :], QX[:, 2, :]
        KX0, QM = KX[:, 0:2, :], KX[:, 2:4, :]
        Qt = sb("Qt", [128, T])
        Kt = sb("Kt", [128, T])
        mcol0 = sb("mcol0", [128, TB, 128])
        room = sb("room", [128, 2 * G0 * TB * T])
        P0 = room[:, :].rearrange("p (u j k) -> p u j k", u=2, j=G0)
        Pt = room[:, 0:4 * TB * T].rearrange("p (u k q) -> p u k q", u=4, k=TB)
        Psum = room[:, 8192:8192 + 4 * T].rearrange("p (u q) -> p u q", u=4)
        On = room[:, 10240:10240 + T]
        Os = room[:, 10240 + T:10240 + 2 * T]
        Lr = room[:, 10240 + 2 * T:10240 + 2 * T + 2 * 128]
        wa = room[:, 12288:12288 + TURNS * 4 * C].rearrange("p (i n) -> p i n", i=TURNS)
        Pc = room[:, 11264:11264 + 2 * H * S].rearrange("p (u n) -> p u n", u=2)
        uT = room[:, 4096:4096 + B * FC * T].rearrange("p (b j t) -> p b j t", b=B, j=FC)
        gl = room[:, 8192:8192 + 2 * T].rearrange("p (u t) -> p u t", u=2)
        P2T = room[:, 9216:9216 + 2 * 512].rearrange("p (u j t) -> p u j t", u=2, j=4)
        rden0 = sb("rden0", [128, 2, TB * G0])
        O0 = sb("O0", [128, NT, C])
        OT0 = room[:, 10240:10240 + NT * 128]
        tm8 = sb("tm8", [1, B, T], u8)
        eps = sb("eps", [128, NT])
        pool_pad, dve_pad = sb("pool_pad", [128, 1]), sb("dve_pad", [128, 1])
        tmr = sb("tmr", [1, B, T], bf16)
        onehot = sb("onehot", [1, 128], bf16)
        km8 = sb("km8", [128, NT], u8)
        keep = sb("keep", [128, NT])

        ps = ctx.enter_context(nc.psum_tensor("ps", [128, 8, 512], f32))

        consts_loaded, x_loaded, masks_loaded = sem("consts_loaded"), sem("x_loaded"), sem("masks_loaded")
        w0_loaded, wqk_loaded = sem("w0_loaded"), sem("wqk_loaded")
        wa_loaded = sem("wa_loaded")
        cross_loaded, ff_loaded, vec_loaded = sem("cross_loaded"), sem("ff_loaded"), sem("vec_loaded")
        zeroed, setup_done = sem("zeroed"), sem("setup_done")
        dve_step, pool_step, pad_written = sem("dve_step"), sem("pool_step"), sem("pad_written")
        ln_var, ln_rstd, ln_xhat = sem("ln_var"), sem("ln_rstd"), sem("ln_xhat")
        ln_turned, ln_hT, ln_hi, ln_lo = sem("ln_turned"), sem("ln_hT"), sem("ln_hi"), sem("ln_lo")
        bias_added = sem("bias_added")
        bf_done, masks_done = sem("bf_done"), sem("masks_done")
        v0_ready, v0_done = sem("v0_ready"), sem("v0_done")
        blocks_done, qb_ready, cross_bias_done = sem("blocks_done"), sem("qb_ready"), sem("cross_bias_done")
        q0_ready, q0_hi, q0_done = sem("q0_ready"), sem("q0_hi"), sem("q0_done")
        k0_ready, k0_hi = sem("k0_ready"), sem("k0_hi")
        d0_ready, d0_max = sem("d0_ready"), sem("d0_max")
        m0_ready, m0_done = sem("m0_ready"), sem("m0_done")
        s0_ready, s0_exp, s0_masked = sem("s0_ready"), sem("s0_exp"), sem("s0_masked")
        vg_done, o0_ready, o0_copied = sem("vg_done"), sem("o0_ready"), sem("o0_copied")
        o0_turned, o0_done = sem("o0_turned"), sem("o0_done")
        ot0_ready, ot0_done = sem("ot0_ready"), sem("ot0_done")
        proj_ready, proj_added = sem("proj_ready"), sem("proj_added")
        w_hi, w_lo = sem("w_hi"), sem("w_lo")
        qk_ready, qk_hi, qk_lo = sem("qk_ready"), sem("qk_hi"), sem("qk_lo")
        v_ready, v_done = sem("v_ready"), sem("v_done")
        d_ready, d_max, m_ready, m_done = sem("d_ready"), sem("d_max"), sem("m_ready"), sem("m_done")
        s_ready, s_exp = sem("s_ready"), sem("s_exp")
        p_sum, l_ready, l_rec, o_norm = sem("p_sum"), sem("l_ready"), sem("l_rec"), sem("o_norm")
        o_ready, o_copied, l_spread = sem("o_ready"), sem("o_copied"), sem("l_spread")
        op_ready, o_done = sem("op_ready"), sem("o_done")
        kv2_ready, kv2_done = sem("kv2_ready"), sem("kv2_done")
        g_ready, g_done, u_ready, u_done = sem("g_ready"), sem("g_done"), sem("u_ready"), sem("u_done")
        c_ready, c_sub, c_exp, c_rec, c_norm = sem("c_ready"), sem("c_sub"), sem("c_exp"), sem("c_rec"), sem("c_norm")
        ct_ready, ct_done, co_ready, c_added = sem("ct_ready"), sem("ct_done"), sem("co_ready"), sem("c_added")
        f_ready, f_gelu, f_u = sem("f_ready"), sem("f_gelu"), sem("f_u")
        fo_ready, ff_added = sem("fo_ready"), sem("ff_added")
        stored = sem("stored")

        block = ctx.enter_context(nc.Block())

        ATTN, CROSS, FF = range(3)
        UNITS = H * B
        UNITS0 = NG * B
        LAST = TURNS - 1

        def half_nth(L, part, b):
            return (L * 3 + part) * B + b + 1

        def nth(l, i, k, per, e):
            return (l * UNITS + i * 4 + k) * per + e + 1

        def qk_nth(l, i, k, per=1, e=0):
            return nth(l, i, k, per, e) + 2 * per

        def couple_nth(l, i, b):
            return (l * TURNS + i) * B + b + 1

        def pairs_nth(l, i):
            return (l * TURNS + i) * 2 + 2

        def of_pair(i, n):
            if isinstance(i, int):
                return wa[:, i, n * C:(n + 1) * C]
            return wa[:, bass.ds(i, 1), n * C:(n + 1) * C].rearrange("p a n -> p (a n)")

        def score_bank(n):
            return (0, 1, 6, 7)[n % 4]

        NMAX = TB * G0

        def rows_of(b):
            return slice(b * TB, (b + 1) * TB)

        def cols_of(b):
            return slice(b * T, (b + 1) * T)


        @block.sync
        def _(sp):
            sp.dma_start(cst[:, :], consts).then_inc(consts_loaded, 16)
            sp.dma_start(v0[:, :], vec0).then_inc(consts_loaded, 16)
            sp.dma_start(ctxT[:, :], ctx_t).then_inc(w0_loaded, 16)
            sp.dma_start(wkv0[:, :], wk0).then_inc(w0_loaded, 16)
            sp.dma_start(wl0[:, :], w0).then_inc(w0_loaded, 16)
            sp.dma_start(r0[:, :, :], rows0.partition_broadcast(128)).then_inc(w0_loaded, 16)
            sp.dma_start(wqk[:, :], w0_qk[0, :, :]).then_inc(wqk_loaded, 16)

            def layer_loads(l, first):
                layer = bass.ds(l, 1)
                if not first:
                    sp.wait_ge(u_done, (l + 1) * 2)
                sp.dma_start(wc[:, :, :], w_ctx[layer, :, :].rearrange("a p (k n) -> (a p) k n", k=2))\
                  .then_inc(cross_loaded, 16)
                sp.dma_start(wx[:, :, :], w_cross[layer, :, :].rearrange("a p (k n) -> (a p) k n", k=H // 2))\
                  .then_inc(cross_loaded, 16)
                if first:
                    sp.wait_ge(o0_ready, UNITS0)
                else:
                    sp.wait_ge(op_ready, l * TURNS * B)
                sp.dma_start(wa[:, :, :], w_attn[layer, :, :].rearrange("a p (i n) -> (a p) i n", i=TURNS))\
                  .then_inc(wa_loaded, 16)
                if not first:
                    sp.wait_ge(ff_added, (l + 1) * B)
                sp.dma_start(vl[:, :], vec[layer, :, :].rearrange("a p n -> (a p) n")).then_inc(vec_loaded, 16)
                sp.dma_start(rl[:, :, :], rows[layer, :, :].rearrange("a r c -> (a r) c").partition_broadcast(128))\
                  .then_inc(vec_loaded, 16)
                sp.dma_start(wf[:, :], w_ff[layer, :, :].rearrange("a p n -> (a p) n")).then_inc(ff_loaded, 16)

            with sp.Fori(1, NG) as g:
                sp.wait_ge(q0_done, g * B)
                sp.dma_start(wqk[:, :], w0_qk[bass.ds(g, 1), :, :].rearrange("a p n -> (a p) n"))\
                  .then_inc(wqk_loaded, 16)
            layer_loads(0, True)
            with sp.Fori(1, LOOP_LAYERS) as l:
                layer_loads(l, False)
            for b in range(B):
                sp.wait_ge(ff_added, LOOP_LAYERS * B + b + 1)
                sp.dma_start(out_dram[:, rows_of(b), :], x[:, rows_of(b), :]).then_inc(stored, 16)
            sp.wait_ge(stored, 16 * B)

        @block.gpsimd
        def _(pool):
            steps = Steps(pool, pool_step)
            with nc.allow_non_contiguous_dma(reason="a mask of one byte per token, tokens onto partitions"):
                pool.dma_start(km8[:, :], tgt_mask.rearrange("b (t p) -> p (b t)", p=128)).then_inc(masks_loaded, 16)
            pool.dma_start(tm8[:, :, :], tgt_mask.rearrange("(a b) t -> a b t", a=1)).then_inc(masks_loaded, 16)
            pool.dma_start(em8[:, :, :], enc_mask.rearrange("(a b) s -> a b s", a=1)).then_inc(masks_loaded, 16)
            pool.memset(mhalf[:, :], -0.5).then_inc(zeroed, 1)
            pool.memset(eps[:, :], EPS).then_inc(zeroed, 1)
            pool.memset(pool_pad[:, :], 0.0).then_inc(pad_written, 1)
            pool.memset(onehot[:, :], 0.0).then_inc(zeroed, 1)
            pool.memset(pick[:, :, :], 0.0).then_inc(zeroed, 1)

            def inverse_std(L, part, halves=range(B)):
                for b in halves:
                    pool.wait_ge(ln_var, half_nth(L, part, b))
                    steps.add(pool.tensor_tensor(veps[:, rows_of(b)], mv[:, rows_of(b), 1], eps[:, rows_of(b)],
                                                 ALU.add))
                    steps.wait()
                    pool.tensor_tensor(rstd[:, rows_of(b)], veps[:, rows_of(b)], mhalf[:, rows_of(b)], ALU.pow)\
                        .then_inc(ln_rstd, 1)

            def add_bias(L, part, row):
                for b in range(B):
                    pool.wait_ge(ln_xhat, half_nth(L, part, b))
                    pool.tensor_tensor(x[:, rows_of(b), :], x[:, rows_of(b), :],
                                       row.unsqueeze(1).to_broadcast([128, TB, C]), ALU.add).then_inc(bias_added, 1)

            def normalise_cross(L):
                for n in range(NT):
                    pool.wait_ge(c_rec, L * NT + n + 1)
                    p = Pc[:, n % 2, :].rearrange("p (h s) -> p h s", s=S)
                    pool.tensor_tensor(p, p, crec[:, n % 2, :].unsqueeze(2).to_broadcast([128, H, S]),
                                       ALU.mult).then_inc(c_norm, 1)
                    if n == NT - 2:
                        inverse_std(L, FF, (0,))
                inverse_std(L, FF, (1,))

            def zero_diagonal(u, b):
                for t in range(TB):
                    pool.wait_ge(s0_exp, (u * TB + t) * 2 + 2)
                    pool.wait_ge(pad_written, u * TB + t + 1)
                    pool.tensor_tensor(pool_pad[:, :], mhalf[:, 0:1], mhalf[:, 0:1], ALU.add)\
                        .then_inc(pad_written, 1)
                    blk = P0[:, b, :, t * T + t * 128:t * T + (t + 1) * 128]
                    pool.affine_select(out=blk, in_=blk, compare_op=ALU.is_ge, fill=0.0, base=0,
                                       pattern=[[0, G0], [1, 128]], channel_multiplier=-1).then_inc(s0_masked, 1)

            pool.wait_ge(zeroed, 4)
            pool.memset(mcol0[:, :, :], 0.0).then_inc(setup_done, 1)
            inverse_std(0, ATTN)
            pool.memset(Vg[:, :, :, :, :], 0.0).then_inc(setup_done, 1)
            pool.memset(onehot[:, :].rearrange("p (j r) -> p j r", r=32)[:, :, ROW_MASK:ROW_MASK + 1], 1.0)\
                .then_inc(setup_done, 1)
            pool.memset(ones_row[:, :], 1.0).then_inc(setup_done, 1)
            pool.memset(ones[:, :], 1.0).then_inc(setup_done, 1)
            pool.memset(QB[:, :, :].bitcast(f32), 0.0).then_inc(setup_done, 1)
            pool.memset(KB[:, :, :].bitcast(f32), 1.0).then_inc(setup_done, 1)
            pool.memset(K2b[:, :, :, :], 0.0).then_inc(setup_done, 1)
            pool.memset(V2b[:, :, :, :], 0.0).then_inc(setup_done, 1)
            pool.wait_ge(w0_loaded, 64)
            add_bias(0, ATTN, r0[:, 1, :])
            with pool.Fori(0, NG) as g:
                for b in range(B):
                    zero_diagonal(g * B + b, b)
            inverse_std(0, CROSS)
            add_bias(0, CROSS, r0[:, 2, :])
            normalise_cross(0)
            add_bias(0, FF, r0[:, 3, :])
            with pool.Fori(0, LOOP_LAYERS) as l:
                kept = steps.enter(l, 3 * B + 2 * UNITS)
                for part in (ATTN, CROSS, FF):
                    if part != FF:
                        inverse_std(l + 1, part)
                    if part == ATTN:
                        pool.wait_ge(vec_loaded, l * 32 + 32)
                    add_bias(l + 1, part, rl[:, part, :])
                    if part == ATTN:
                        with pool.Fori(0, TURNS) as i:
                            kept_i = steps.enter(i, 8)
                            for k in range(4):
                                pool.wait_ge(s_exp, nth(l, i, k, 2, 1))
                                steps.add(pool.tensor_tensor(Psum[:, k, :], Pt[:, k, 0, :], Pt[:, k, 1, :], ALU.add))
                                steps.wait()
                                steps.add(pool.tensor_tensor(Psum[:, k, :], Psum[:, k, :], Pt[:, k, 2, :], ALU.add))
                                steps.wait()
                                pool.tensor_tensor(Psum[:, k, :], Psum[:, k, :], Pt[:, k, 3, :], ALU.add)\
                                    .then_inc(p_sum, 1)
                            steps.leave(kept_i, TURNS)
                    if part == CROSS:
                        normalise_cross(l + 1)
                steps.leave(kept, LOOP_LAYERS)

        @block.scalar
        def _(act):
            for b in range(B):
                act.dma_start(x[:, rows_of(b), :], x_dram[:, rows_of(b), :]).then_inc(x_loaded, 16)

            def finish_ln(L, part, scale, bias, l=None, halves=range(B)):
                for b in halves:
                    act.wait_ge(ln_turned, half_nth(L, part, b))
                    act.activation(hT[:, cols_of(b)], ps[:, 6 + b, :], ACT.Identity, bias=bias, scale=scale)\
                       .then_inc(ln_hT, 1)
                    if l is not None:
                        act.activation(hTh[:, cols_of(b)], ps[:, 6 + b, :], ACT.Identity, bias=bias, scale=scale)\
                           .then_inc(ln_hi, 1)

            def turn_out(L, n):
                act.wait_ge(ct_ready, L * NT + n + 1)
                if n >= 2:
                    act.wait_ge(co_ready, L * NT + n - 1)
                act.activation(P2T[:, n % 2, :, :].rearrange("p j t -> p (j t)"), ps[:, 2 + n % 2, :],
                               ACT.Copy).then_inc(ct_done, 1)

            def cross_act(L, scale, ff_scale, ff_bias):
                for n in range(NT):
                    act.wait_ge(c_sub, L * NT + n + 1)
                    if n >= 2:
                        act.wait_ge(ct_ready, L * NT + n - 1)
                    act.activation(Pc[:, n % 2, :], Ec[:, n % 2, :], ACT.Exp, scale=scale).then_inc(c_exp, 1)
                    if n >= 1:
                        turn_out(L, n - 1)
                turn_out(L, NT - 1)
                finish_ln(L, FF, ff_scale, ff_bias, halves=(0,))

            act.wait_ge(consts_loaded, 32)
            act.wait_ge(kv2_ready, 1)
            act.activation(K2T[:, :], ps[:, 4, 0:B * S], ACT.Identity, bias=v0[:, 10:11]).then_inc(kv2_done, 1)
            act.activation(V2T[:, :], ps[:, 4, B * S:2 * B * S], ACT.Identity, bias=v0[:, 11:12])\
               .then_inc(kv2_done, 1)
            finish_ln(0, ATTN, v0[:, 0:1], v0[:, 1:2])
            for b in range(B):
                act.wait_ge(g_ready, b + 1)
                act.activation(Gm[:, b, :], ps[:, b, :], ACT.Copy).then_inc(g_done, 1)
            for b in range(B):
                act.wait_ge(u_ready, b + 1)
                act.activation(Um[:, b, :, :].rearrange("p j c -> p (j c)"), ps[:, 4 + b, :], ACT.Copy)\
                   .then_inc(u_done, 1)

            def q_hi(u):
                act.wait_ge(q0_ready, u + 1)
                act.activation(QH[:, :], ps[:, 4, :], ACT.Identity, bias=wqk[:, 256:257]).then_inc(q0_hi, 1)

            def k_hi(u):
                act.wait_ge(k0_ready, u + 1)
                act.activation(KH[:, :], ps[:, 5, :], ACT.Identity, bias=wqk[:, 257:258]).then_inc(k0_hi, 1)

            def exps0(u, b, t):
                for j2 in range(2):
                    act.wait_ge(s0_ready, (u * TB + t) * 2 + j2 + 1)
                    act.activation(P0[:, b, 2 * j2:2 * j2 + 2, t * T + t * 128:(t + 1) * T],
                                   ps[:, 2 + 2 * j2:4 + 2 * j2, 0:T - t * 128], ACT.Exp, scale=SCALE0)\
                       .then_inc(s0_exp, 1)

            def sums_out(u):
                act.wait_ge(o0_ready, u + 1)
                act.activation(OS, ps[:, 7, :], ACT.Copy).then_inc(o0_copied, 1)

            def unit0_act(u, b, first=False, more=True):
                if not first:
                    sums_out(u - 2)
                for t in range(TB):
                    exps0(u, b, t)
                if more:
                    q_hi(u + 2)
                    k_hi(u + 2)

            for u in range(2):
                q_hi(u)
                k_hi(u)
            unit0_act(0, 0, first=True)
            unit0_act(1, 1, first=True)
            with act.Fori(1, NG - 1) as g:
                for b in range(B):
                    unit0_act(g * B + b, b)
            for b in range(B):
                unit0_act(UNITS0 - B + b, b, more=False)
            for u in range(UNITS0 - 2, UNITS0):
                sums_out(u)
            for b in range(B):
                act.wait_ge(ot0_ready, b + 1)
                act.activation(OT0[:, cols_of(b)], ps[:, b, :], ACT.Copy).then_inc(ot0_done, 1)
            finish_ln(0, CROSS, v0[:, 2:3], v0[:, 3:4])
            cross_act(0, SCALE0, v0[:, 4:5], v0[:, 5:6])
            for b in range(B):
                for j in range(FC):
                    n = b * FC + j
                    if n == 2:
                        finish_ln(0, FF, v0[:, 4:5], v0[:, 5:6], halves=(1,))
                    act.wait_ge(f_ready, n + 1)
                    act.activation(uT[:, b, j, :], ps[:, 2 * (n % 2), :], ACT.Gelu, bias=v0[:, 6 + j:7 + j])\
                       .then_inc(f_gelu, 1)

            act.wait_ge(setup_done, 13)
            with act.Fori(0, LOOP_LAYERS) as l:
                def weights_hi(i, n):
                    act.activation(Wh[:, n, :], of_pair(i, n), ACT.Copy).then_inc(w_hi, 1)

                act.wait_ge(wa_loaded, l * 16 + 16)
                for n in range(2):
                    weights_hi(0, n)
                for n, dst in enumerate((K2b, V2b)):
                    act.wait_ge(kv2_ready, 1 + l * 2 + n + 1)
                    for e in range(2):
                        half = slice(64 * e, 64 * e + 64)
                        ins = act.activation(
                            dst[half, :, :, e * S:(e + 1) * S].rearrange("p j b s -> p (j b) s"),
                            ps[half, n, :].rearrange("p (k s) -> p k s", s=S), ACT.Copy)
                    ins.then_inc(kv2_done, 1)
                act.wait_ge(vec_loaded, l * 32 + 32)
                finish_ln(l + 1, ATTN, vl[:, 0:1], vl[:, 1:2], l, halves=(0,))
                for r in range(2):
                    act.wait_ge(g_ready, B + l * 2 + r + 1)
                    for b in range(B):
                        src = ps[:, 2 + r, :].rearrange("p (j b n) -> p j b n", b=B, n=2 * S)[:, :, b, :]
                        half = Gm[:, b, r * 256:(r + 1) * 256].rearrange("p (j n) -> p j n", n=2 * S)
                        act.activation(half, src, ACT.Copy).then_inc(g_done, 1)
                finish_ln(l + 1, ATTN, vl[:, 0:1], vl[:, 1:2], l, halves=(1,))
                for b in range(B):
                    act.wait_ge(u_ready, B + l * 2 + b + 1)
                    act.activation(Um[:, b, :, :].rearrange("p j c -> p (j c)"), ps[:, 4 + b, :], ACT.Copy)\
                       .then_inc(u_done, 1)

                def halves(e):
                    return slice(64 * e, 64 * e + 64), slice(64 - 64 * e, 128 - 64 * e)

                def q_hi_parts(i, k, slot):
                    act.wait_ge(qk_ready, qk_nth(l, i, k))
                    for e in range(2):
                        own = halves(e)[0]
                        act.activation(QX[own, slot + e, :], ps[own, 6, :], ACT.Copy)
                        act.activation(QB[own, slot + e, :], ps[own, 6, :], ACT.Copy).then_inc(qk_hi, 1)

                def k_hi_parts(i, k, slot):
                    act.wait_ge(qk_ready, qk_nth(l, i, k))
                    for e in range(2):
                        own, other = halves(e)
                        act.activation(KX[own, slot + e, :], ps[own, 6, :], ACT.Copy)
                        act.activation(KX[other, slot + e, :], ps[own, 6, :], ACT.Copy).then_inc(qk_hi, 1)

                def v_out(i, b):
                    act.wait_ge(v_ready, couple_nth(l, i, b))
                    act.activation(V[:, b, :, :].rearrange("p t c -> p (t c)"), ps[:, 6, :], ACT.Copy)\
                       .then_inc(v_done, 1)

                def exps(i, k, e):
                    act.wait_ge(s_ready, nth(l, i, k, 2, e))
                    act.activation(Pt[:, k, 2 * e:2 * e + 2, :], ps[:, 2 * e:2 * e + 2, :], ACT.Exp,
                                   scale=SCALE).then_inc(s_exp, 1)

                def sums_out(i, b):
                    act.wait_ge(o_ready, couple_nth(l, i, b))
                    act.activation(Os, ps[:, 7, :], ACT.Copy).then_inc(o_copied, 1)

                def unit(i, k, first=False):
                    more = not (i is LAST and k >= 2)
                    if k == 3:
                        sums_out(i, 0)
                    if k == 1 and not first:
                        sums_out(i - 1, 1)
                    slot = (k // 2 * 2 + 2) % 4
                    if more and k % 2 == 0:
                        q_hi_parts(i, k, slot)
                    exps(i, k, 0)
                    exps(i, k, 1)
                    if more and k % 2 == 0:
                        k_hi_parts(i, k + 1, slot)
                    if i is not LAST and k == 1:
                        for n in range(2):
                            weights_hi(i + 1, n)
                    if more and k % 2 == 1:
                        v_out(*((i, 1) if k == 1 else (i + 1, 0)))

                q_hi_parts(0, -2, 0)
                k_hi_parts(0, -1, 0)
                v_out(0, 0)
                for k in range(4):
                    unit(0, k, first=True)
                with act.Fori(1, LAST) as i:
                    for k in range(4):
                        unit(i, k)
                for k in range(4):
                    unit(LAST, k)
                sums_out(LAST, 1)
                finish_ln(l + 1, CROSS, vl[:, 2:3], vl[:, 3:4])
                cross_act(l + 1, SCALE, vl[:, 4:5], vl[:, 5:6])
                for b in range(B):
                    for j in range(FC):
                        n = b * FC + j
                        if n == 2:
                            finish_ln(l + 1, FF, vl[:, 4:5], vl[:, 5:6], halves=(1,))
                        act.wait_ge(f_ready, (l + 1) * B * FC + n + 1)
                        act.activation(gl[:, n % 2, :], ps[:, 2 * (n % 2), :], ACT.Gelu, bias=vl[:, 10 + j:11 + j])\
                           .then_inc(f_gelu, 1)

        @block.vector
        def _(dve):
            steps = Steps(dve, dve_step)

            def ln_stats(b, x_ready, x_nth):
                dve.wait_ge(x_ready, x_nth)
                for n in range(b * TB, (b + 1) * TB):
                    ins = dve.bn_stats(stats[:, n, :], x[:, n, :])
                steps.add(ins)
                steps.wait()
                dve.memset(dve_pad[:, :], 0.0)
                for n in range(b * TB, (b + 1) * TB):
                    ins = dve.bn_aggr(mv[:, n, :], stats[:, n, :])
                ins.then_inc(ln_var, 1)

            def ln_normalise(L, part, b):
                dve.wait_ge(ln_rstd, half_nth(L, part, b))
                for n in range(b * TB, (b + 1) * TB):
                    ins = dve.tensor_scalar(xhat[:, n, :], x[:, n, :], mv[:, n, 0:1], rstd[:, n:n + 1],
                                            ALU.subtract, ALU.mult)
                ins.then_inc(ln_xhat, 1)

            def layer_norm(L, part, x_ready, x_nth):
                for b in range(B):
                    ln_stats(b, x_ready, x_nth(b))
                for b in range(B):
                    ln_normalise(L, part, b)

            def cross_dve(L):
                def softmax(n):
                    dve.wait_ge(c_ready, L * NT + n + 1)
                    sc = ps[:, score_bank(n), :].rearrange("p (h s) -> p h s", s=S)
                    steps.add(dve.tensor_reduce(cmax[:, n % 2, :], sc, X, ALU.max))
                    steps.wait()
                    if n >= 2:
                        dve.wait_ge(c_exp, L * NT + n - 1)
                    dve.tensor_tensor(Ec[:, n % 2, :].rearrange("p (h s) -> p h s", s=S), sc,
                                      cmax[:, n % 2, :].unsqueeze(2).to_broadcast([128, H, S]),
                                      ALU.subtract).then_inc(c_sub, 1)

                def sums(n):
                    dve.wait_ge(c_exp, L * NT + n + 1)
                    steps.add(dve.tensor_reduce(csum[:, n % 2, :],
                                                Pc[:, n % 2, :].rearrange("p (h s) -> p h s", s=S), X, ALU.add))
                    steps.wait()
                    if n >= 2:
                        dve.wait_ge(c_norm, L * NT + n - 1)
                    dve.reciprocal(crec[:, n % 2, :], csum[:, n % 2, :]).then_inc(c_rec, 1)

                def add_out(n):
                    dve.wait_ge(bias_added, half_nth(L, CROSS, n // TB))
                    dve.wait_ge(co_ready, L * NT + n + 1)
                    dve.tensor_tensor(x[:, n, :], ps[:, 4 + n % 2, 0:C], x[:, n, :], ALU.add).then_inc(c_added, 1)

                for n in range(NT):
                    softmax(n)
                    if n >= 1:
                        sums(n - 1)
                    if n >= 4:
                        add_out(n - 4)
                    if n == NT - 1:
                        ln_stats(0, c_added, L * NT + TB)
                sums(NT - 1)
                add_out(NT - 4)
                ln_normalise(L, FF, 0)
                for n in range(NT - 3, NT):
                    add_out(n)
                ln_stats(1, c_added, L * NT + NT)
                ln_normalise(L, FF, 1)

            def ff_out(L):
                for b in range(B):
                    dve.wait_ge(bias_added, half_nth(L, FF, b))
                    dve.wait_ge(fo_ready, L * B + b + 1)
                    dve.tensor_tensor(x[:, rows_of(b), :], ps[:, 4 + b, :].rearrange("p (t c) -> p t c", c=C),
                                      x[:, rows_of(b), :], ALU.add).then_inc(ff_added, 1)
                    ln_stats(b, ff_added, L * B + b + 1)

            dve.wait_ge(consts_loaded, 32)
            dve.tensor_copy(ident_bf[:, :], ident).then_inc(bf_done, 1)
            dve.tensor_copy(tri_bf[:, :], tri).then_inc(bf_done, 1)
            layer_norm(0, ATTN, x_loaded, lambda b: 32)
            dve.wait_ge(zeroed, 4)
            for t in range(TB):
                dve.memset(pick[32 * t:32 * t + 1, t, :], 1.0).then_inc(setup_done, 1)
            dve.wait_ge(masks_loaded, 48)
            dve.tensor_scalar(tmr[:, :, :], tm8[:, :, :], -BIG, None, ALU.mult).then_inc(masks_done, 1)
            steps.add(dve.tensor_scalar(keep[:, :], km8[:, :], -1.0, 1.0, ALU.mult, ALU.add))
            steps.add(dve.tensor_scalar(em[:, :, :], em8[:, :, :], -BIG, None, ALU.mult))
            steps.add(dve.tensor_scalar(keepn[:, :, :], em8[:, :, :], -1.0, 1.0, ALU.mult, ALU.add))
            steps.wait()
            steps.add(dve.tensor_reduce(poison[:, 0:B], keepn[:, :, :], X, ALU.add))
            steps.wait()
            steps.add(dve.reciprocal(poison[:, B:2 * B], poison[:, 0:B]))
            steps.wait()
            steps.add(dve.tensor_scalar(poison[:, 2 * B:3 * B], poison[:, B:2 * B], 0.0, None, ALU.mult))
            dve.wait_ge(kv2_done, 2)
            for b in range(B):
                for src, dst in ((K2T, Ec), (V2T, Pc)):
                    ins = dve.tensor_tensor(dst[:, b, :].rearrange("p (h s) -> p h s", s=S),
                                            src[:, b * S:(b + 1) * S].unsqueeze(1).to_broadcast([128, H, S]),
                                            head_mask.unsqueeze(2).to_broadcast([128, H, S]), ALU.mult)
                ins.then_inc(blocks_done, 1)
            dve.wait_ge(w0_loaded, 64)
            for b in range(B):
                dve.wait_ge(v0_ready, b + 1)
                for t in range(TB):
                    ins = dve.tensor_tensor(Vaug[:, b * TB + t, :, 0:D0],
                                            ps[:, 2 + b, t * C:(t + 1) * C].rearrange("p (h d) -> p h d", d=D0),
                                            r0[:, 0, :].rearrange("p (h d) -> p h d", d=D0), ALU.add)
                steps.add(ins)
                steps.wait()
                for t in range(TB):
                    n = b * TB + t
                    dve.tensor_scalar(Vaug[:, n, :, 0:D0], Vaug[:, n, :, 0:D0], keep[:, n:n + 1], None, ALU.mult)
                    ins = dve.tensor_copy(Vaug[:, n, :, D0], keep[:, n:n + 1].to_broadcast([128, H]))
                ins.then_inc(v0_done, 1)
            for b in range(B):
                dve.wait_ge(qb_ready, b + 1)
                steps.add(dve.tensor_tensor(cross_bias[:, b, :].rearrange("p (h s) -> p h s", s=S),
                                            ps[0:1, 6 + b, :].rearrange("p (h s) -> p h s", s=S),
                                            em[:, b, :].unsqueeze(1).to_broadcast([1, H, S]), ALU.add))
                steps.wait()
                dve.tensor_scalar(cross_bias[:, b, :], cross_bias[:, b, :], poison[:, 2 * B + b:2 * B + b + 1], None,
                                  ALU.add).then_inc(cross_bias_done, 1)

            def q_rest(u):
                dve.wait_ge(q0_hi, u + 1)
                steps.add(dve.tensor_scalar(Qt[:, :], ps[:, 4, :], wqk[:, 256:257], tQ, ALU.add, ALU.mult))

            def k_rest(u):
                dve.wait_ge(k0_hi, u + 1)
                steps.add(dve.tensor_scalar(Kt[:, :], ps[:, 5, :], wqk[:, 257:258], tK, ALU.add, ALU.mult))

            def k_part(parity):
                steps.wait()
                dve.scalar_tensor_tensor(out=KX0[:, parity, :], in0=KH[:, :].bitcast(f32), scalar=sK, in1=Kt[:, :],
                                         op0=ALU.mult, op1=ALU.add)

            def q_part():
                dve.scalar_tensor_tensor(out=QX0[:, :], in0=QH[:, :].bitcast(f32), scalar=sQ, in1=Qt[:, :],
                                         op0=ALU.mult, op1=ALU.add).then_inc(q0_done, 1)

            mcol0_heads = mcol0[:, :, :].rearrange("p t (j r) -> p t j r", r=32)

            def maxima0(u, steps_n):
                for n in steps_n:
                    t, j = n // G0, n % G0
                    dve.wait_ge(d0_ready, u * NMAX + n + 1)
                    dve.tensor_reduce(mcol0_heads[:, t, j, ROW_MAX:ROW_MAX + 1], ps[:, n % 2, 0:(t + 1) * 128],
                                      X, ALU.max, negate=True).then_inc(d0_max, 1)

            def outputs0(u, cols, b):
                dve.wait_ge(o0_turned, u + 1)
                o = ps[:, 7, :].rearrange("p (t j d) -> p t j d", j=G0, d=32)
                r = rden0[:, b, :].rearrange("p (t j) -> p t j", j=G0)
                steps.add(dve.reciprocal(r, o[:, :, :, D0]))
                steps.wait()
                for t in range(TB):
                    ins = dve.tensor_tensor(O0[:, b * TB + t, cols].rearrange("p (j d) -> p j d", d=D0),
                                            o[:, t, :, 0:D0], r[:, t, :].unsqueeze(2).to_broadcast([128, G0, D0]),
                                            ALU.mult)
                ins.then_inc(o0_done, 1)

            def values_of(u, g, b):
                if isinstance(u, int) and u < 2:
                    pass
                else:
                    dve.wait_ge(o0_ready, u - 1)
                for t in range(TB):
                    ins = dve.tensor_copy(Vg[:, b, t, :, 0:D0 + 1], Vaug[:, b * TB + t, heads_at(g), :])
                ins.then_inc(vg_done, 1)

            def heads_at(g):
                return bass.ds(g * G0, G0)

            def cols_at(g):
                return bass.ds(g * (G0 * D0), G0 * D0)

            def unit0(g, b, last=False, project=True, normalise=True):
                u = g * B + b
                if not last:
                    k_part((b + 1) % 2)
                dve.wait_ge(m0_ready, u + 1)
                dve.tensor_tensor(QM[:, b, :], ps[:, 6, :], QX0[:, :].bitcast(f32), ALU.add).then_inc(m0_done, 1)
                if not last:
                    dve.wait_ge(m0_done, u + 1)
                    q_part()
                    maxima0(u + 1, range(0, 4))
                values_of(u, g, b)
                if not last:
                    maxima0(u + 1, range(4, 8))
                if normalise:
                    outputs0(u - 2, cols_at(g - 1), b)
                if not last:
                    maxima0(u + 1, range(8, 14))
                    if project:
                        q_rest(u + 2)
                    maxima0(u + 1, range(14, 15))
                    if project:
                        k_rest(u + 2)
                    maxima0(u + 1, range(15, 16))

            dve.wait_ge(setup_done, 13)
            dve.wait_ge(wqk_loaded, 16)
            q_rest(0)
            k_rest(0)
            k_part(0)
            q_part()
            maxima0(0, range(0, 10))
            q_rest(1)
            maxima0(0, range(10, 12))
            k_rest(1)
            maxima0(0, range(12, NMAX))
            unit0(0, 0, normalise=False)
            unit0(0, 1, normalise=False)
            with dve.Fori(1, NG - 1) as g:
                kept = steps.enter(g - 1, 6)
                unit0(g, 0)
                unit0(g, 1)
                steps.leave(kept, NG - 2)
            unit0(NG - 1, 0, project=False)
            unit0(NG - 1, 1, last=True)
            for b in range(B):
                outputs0(UNITS0 - B + b, cols_at(NG - 1), b)
            for b in range(B):
                dve.wait_ge(bias_added, half_nth(0, ATTN, b))
                dve.wait_ge(proj_ready, b + 1)
                dve.tensor_tensor(x[:, rows_of(b), :], ps[:, 2 + b, :].rearrange("p (t c) -> p t c", c=C),
                                  x[:, rows_of(b), :], ALU.add).then_inc(proj_added, 1)
            layer_norm(0, CROSS, proj_added, lambda b: b + 1)
            cross_dve(0)
            ff_out(0)

            with dve.Fori(0, LOOP_LAYERS) as l:
                kept_l = steps.enter(l, 3 * B + 2 * NT)

                def weights_lo(i, n):
                    dve.wait_ge(w_hi, pairs_nth(l, i) - 1 + n)
                    dve.tensor_tensor(Wl[:, n, :], of_pair(i, n), Wh[:, n, :].bitcast(f32),
                                      ALU.subtract).then_inc(w_lo, 1)

                for b in range(B):
                    ln_normalise(l + 1, ATTN, b)
                for n in range(2):
                    weights_lo(0, n)
                for b in range(B):
                    dve.wait_ge(ln_hT, half_nth(l + 1, ATTN, b))
                    dve.wait_ge(ln_hi, l * B + b + 1)
                    dve.tensor_tensor(hTl[:, cols_of(b)], hT[:, cols_of(b)], hTh[:, cols_of(b)].bitcast(f32),
                                      ALU.subtract).then_inc(ln_lo, 1)

                def lo_parts(i, k, slot):
                    dve.wait_ge(qk_hi, qk_nth(l, i, k, 2, 1))
                    for e in range(2):
                        own, other = slice(64 * e, 64 * e + 64), slice(64 - 64 * e, 128 - 64 * e)
                        if k % 2 == 0:
                            ins = dve.tensor_tensor(QX[other, slot + e, :], ps[own, 6, :],
                                                    QX[own, slot + e, :].bitcast(f32), ALU.subtract)
                        else:
                            ins = dve.tensor_tensor(KB[own, slot + e, :], ps[own, 6, :],
                                                    KX[own, slot + e, :].bitcast(f32), ALU.subtract)
                    ins.then_inc(qk_lo, 1)

                def maximum(i, k, t):
                    dve.wait_ge(d_ready, nth(l, i, k, TB, t))
                    dve.tensor_reduce(mcol[:, t:t + 1], ps[:, 4 + t % 2, :], X, ALU.max, negate=True)\
                       .then_inc(d_max, 1)

                def inverse_sums(i, b):
                    dve.wait_ge(l_ready, couple_nth(l, i, b))
                    dve.reciprocal(Lr, ps[:, 5, 0:2 * 128]).then_inc(l_rec, 1)

                def normalise(i, b):
                    dve.wait_ge(o_copied, couple_nth(l, i, b))
                    dve.wait_ge(l_spread, couple_nth(l, i, b))
                    dve.tensor_tensor(On, ps[:, 7, :], Os, ALU.mult).then_inc(o_norm, 1)

                def add_output(i, b):
                    dve.wait_ge(op_ready, couple_nth(l, i, b))
                    dve.tensor_tensor(x[:, rows_of(b), :], ps[:, 7, :].rearrange("p (t c) -> p t c", c=C),
                                      x[:, rows_of(b), :], ALU.add).then_inc(o_done, 1)

                def unit(i, k, first=False, last=False):
                    e = k % 2
                    before = (i, 0) if k >= 2 else None if first else (i - 1, 1)
                    more = not (i is LAST and k >= 2)
                    dve.wait_ge(m_ready, nth(l, i, k, 1, 0))
                    dve.tensor_tensor(QB[64 - 64 * e:64 - 64 * e + TB, k, :].rearrange("p (t q) -> p t q", t=TB),
                                      ps[0:TB, 5, 0:128].unsqueeze(1).to_broadcast([TB, TB, 128]),
                                      ident[0:TB, 0:TB].unsqueeze(2).to_broadcast([TB, TB, 128]), ALU.mult)\
                       .then_inc(m_done, 1)
                    if not last:
                        maximum(i, k + 1, 0)
                        maximum(i, k + 1, 1)
                    if e == 0:
                        if not first:
                            add_output(i - 1, k // 2)
                        if before:
                            inverse_sums(*before)
                    if more:
                        lo_parts(i, k, (k // 2 * 2 + 2) % 4)
                    if not last:
                        maximum(i, k + 1, 2)
                        maximum(i, k + 1, 3)
                    if e == 1 and before:
                        normalise(*before)
                    if i is not LAST and k == 1:
                        for n in range(2):
                            weights_lo(i + 1, n)

                dve.wait_ge(bias_added, half_nth(l + 1, ATTN, B - 1))
                lo_parts(0, -2, 0)
                lo_parts(0, -1, 0)
                for t in range(TB):
                    maximum(0, 0, t)
                for k in range(4):
                    unit(0, k, first=True)
                with dve.Fori(1, LAST) as i:
                    for k in range(4):
                        unit(i, k)
                for k in range(4):
                    unit(LAST, k, last=k == 3)
                add_output(LAST, 0)
                ln_stats(0, o_done, couple_nth(l, LAST, 0))
                inverse_sums(LAST, 1)
                ln_normalise(l + 1, CROSS, 0)
                normalise(LAST, 1)
                add_output(LAST, 1)
                ln_stats(1, o_done, couple_nth(l, LAST, 1))
                ln_normalise(l + 1, CROSS, 1)
                cross_dve(l + 1)
                for b in range(B):
                    for j in range(FC):
                        n = b * FC + j
                        dve.wait_ge(f_gelu, (l + 1) * B * FC + n + 1)
                        dve.scalar_tensor_tensor(out=uT[:, b, j, :], in0=ps[:, 2 * (n % 2) + 1, :],
                                                 scalar=vl[:, 6 + j:7 + j], in1=gl[:, n % 2, :],
                                                 op0=ALU.add, op1=ALU.mult).then_inc(f_u, 1)
                ff_out(l + 1)
                steps.leave(kept_l, LOOP_LAYERS)

        @block.tensor
        def _(pe):
            def turn_ln(L, part, halves=range(B)):
                for b in halves:
                    pe.wait_ge(ln_xhat, half_nth(L, part, b))
                    for t in range(TB):
                        mm = pe.transpose(ps[:, 6 + b, t * 128:(t + 1) * 128], xhat[:, b * TB + t, :], ident)
                    mm.then_inc(ln_turned, 1)

            def cross_pe(L, with_bias):
                def scores(n):
                    b = n // TB
                    if n == 0:
                        pe.wait_ge(ln_hT, half_nth(L, CROSS, 0))
                    if n == 3:
                        pe.wait_ge(ln_hT, half_nth(L, CROSS, 1))
                    if n >= 4:
                        pe.wait_ge(c_sub, L * NT + n - 3)
                    mm = pe.matmul(ps[:, score_bank(n), :], hT[:, n * 128:(n + 1) * 128], Gm[:, b, :], start=True,
                                   stop=not with_bias)
                    if with_bias:
                        mm = pe.matmul(ps[:, score_bank(n), :], ones_row[:, :], cross_bias[:, b, :],
                                       start=False, stop=True)
                    mm.then_inc(c_ready, 1)

                def turn(n):
                    pe.wait_ge(c_norm, L * NT + n + 1)
                    if n >= 2:
                        pe.wait_ge(ct_done, L * NT + n - 1)
                    for j in range(4):
                        mm = pe.transpose(ps[:, 2 + n % 2, j * 128:(j + 1) * 128], Pc[:, n % 2, j * 128:(j + 1) * 128],
                                          ident)
                    mm.then_inc(ct_ready, 1)

                def outs(n):
                    pe.wait_ge(ct_done, L * NT + n + 1)
                    if n >= 2:
                        pe.wait_ge(c_added, L * NT + n - 1)
                    for j in range(4):
                        mm = pe.matmul(ps[:, 4 + n % 2, 0:C], P2T[:, n % 2, j, :], Um[:, n // TB, j, :],
                                       start=j == 0, stop=j == 3)
                    mm.then_inc(co_ready, 1)

                scores(0)
                scores(1)
                turn_ln(L, CROSS, (1,))
                scores(2)
                scores(3)
                for n in range(NT):
                    turn(n)
                    if n >= 1:
                        outs(n - 1)
                    if n + 4 < NT:
                        scores(n + 4)
                outs(NT - 1)
                turn_ln(L, FF, (0,))

            def ff_pe(L, hidden, w_out, used):
                def outs(b):
                    pe.wait_ge(*used(b * FC + FC - 1))
                    for t in range(TB):
                        for j in range(FC):
                            mm = pe.matmul(ps[:, 4 + b, t * C:(t + 1) * C], uT[:, b, j, t * 128:(t + 1) * 128],
                                           w_out[:, j, :], start=j == 0, stop=j == FC - 1)
                    mm.then_inc(fo_ready, 1)

                def hid(n):
                    b, j = n // FC, n % FC
                    if j == 0:
                        pe.wait_ge(ln_hT, half_nth(L, FF, b))
                    if n >= 2:
                        pe.wait_ge(*used(n - 2))
                    for bank, w in hidden(n, j):
                        mm = pe.matmul(ps[:, bank, :], w, hT[:, cols_of(b)], start=True, stop=True)
                    mm.then_inc(f_ready, 1)

                for n in range(FC + 2):
                    if n == 2:
                        turn_ln(L, FF, (1,))
                    hid(n)
                outs(0)
                for n in range(FC + 2, 2 * FC):
                    hid(n)
                outs(1)

            pe.wait_ge(w0_loaded, 64)
            pe.matmul(ps[:, 4, 0:B * S], wkv0[:, 0:C], ctxT[:, :], start=True, stop=True)
            pe.matmul(ps[:, 4, B * S:2 * B * S], wkv0[:, C:2 * C], ctxT[:, :], start=True, stop=True)\
              .then_inc(kv2_ready, 1)
            pe.wait_ge(consts_loaded, 32)
            turn_ln(0, ATTN)
            for b in range(B):
                pe.wait_ge(ln_hT, b + 1)
                for t in range(TB):
                    n = b * TB + t
                    mm = pe.matmul(ps[:, 2 + b, t * C:(t + 1) * C], hT[:, n * 128:(n + 1) * 128], w0_v, start=True,
                                   stop=True)
                mm.then_inc(v0_ready, 1)
            for b in range(B):
                pe.wait_ge(blocks_done, b + 1)
                pe.matmul(ps[:, b, :], w0_qT, Ec[:, b, :], start=True, stop=True).then_inc(g_ready, 1)
                pe.matmul(ps[0:1, 6 + b, :], v0[:, 12:13], Ec[:, b, :], start=True, stop=True).then_inc(qb_ready, 1)
            for b in range(B):
                for j in range(4):
                    mm = pe.matmul(ps[:, 4 + b, j * C:(j + 1) * C], Pc[:, b, j * 128:(j + 1) * 128], w0_out,
                                   start=True, stop=True)
                mm.then_inc(u_ready, 1)

            def q_proj(b):
                pe.matmul(ps[:, 4, :], wqk[:, 0:128], hT[:, cols_of(b)], start=True, stop=True).then_inc(q0_ready, 1)

            def k_proj(b):
                pe.matmul(ps[:, 5, :], wqk[:, 128:256], hT[:, cols_of(b)], start=True, stop=False)
                pe.matmul(ps[:, 5, :], onehot[:, :], tmr[:, b, :], start=False, stop=True).then_inc(k0_ready, 1)

            def row_max_scores(u, b, n):
                t, j = n // G0, n % G0
                if n == 0:
                    pe.wait_ge(q0_done, u + 1)
                if n >= 2:
                    pe.wait_ge(d0_max, u * NMAX + n - 1)
                w = (t + 1) * 128
                rows_j = slice(32 * j, 32 * j + 32)
                pe.matmul(ps[:, n % 2, 0:w], QX0[rows_j, t * 128:w], KX0[rows_j, b, 0:w], start=True, stop=False)
                pe.matmul(ps[:, n % 2, w - 128:w], ident_bf[:, :], tri_bf[:, :], start=False, stop=True)\
                  .then_inc(d0_ready, 1)

            def turn_maxima(u, t):
                pe.wait_ge(d0_max, u * NMAX + (t + 1) * G0)
                mm = pe.transpose(ps[:, 6, t * 128:(t + 1) * 128], mcol0[:, t, :], ident)
                if t == TB - 1:
                    mm.then_inc(m0_ready, 1)

            def turned_scores(u, b, t, j2, fresh):
                if not (fresh and t == 0):
                    pe.wait_ge(s0_exp, (u * TB + t) * 2 + j2 - 1)
                for j in (2 * j2, 2 * j2 + 1):
                    rows_j = slice(32 * j, 32 * j + 32)
                    mm = pe.matmul(ps[:, 2 + j, 0:T - t * 128], KX0[rows_j, b, t * 128:(t + 1) * 128],
                                   QM[rows_j, b, t * 128:T], start=True, stop=True)
                mm.then_inc(s0_ready, 1)

            def weighted0(b, s):
                for j in range(G0):
                    mm = pe.matmul(ps[32 * j:32 * j + 32, 7, s * 128:T], Vg[:, b, s, j, :],
                                   P0[:, b, j, s * T + s * 128:(s + 1) * T], start=s == 0, stop=s == TB - 1)
                return mm

            def turn_sums(u):
                pe.wait_ge(o0_copied, u + 1)
                for t in range(TB):
                    mm = pe.transpose(ps[:, 7, t * 128:(t + 1) * 128], OS[:, t * 128:(t + 1) * 128], ident)
                mm.then_inc(o0_turned, 1)

            def unit0(u, b, first=False, last=False, project=True, next_group=None, turns=True):
                other = (b + 1) % 2

                def row_max(*steps_n):
                    if not last:
                        for n in steps_n:
                            row_max_scores(u + 1, other, n)

                pe.wait_ge(m0_done, u + 1)
                turned_scores(u, b, 0, 0, first)
                turned_scores(u, b, 0, 1, first)
                row_max(0, 1)
                turned_scores(u, b, 1, 0, first)
                row_max(2, 3)
                turned_scores(u, b, 1, 1, first)
                row_max(4, 5)
                if turns:
                    turn_sums(u - 2)
                turned_scores(u, b, 2, 0, first)
                row_max(6, 7)
                turned_scores(u, b, 2, 1, first)
                row_max(8, 9)
                turned_scores(u, b, 3, 0, first)
                row_max(10)
                turned_scores(u, b, 3, 1, first)
                row_max(11)
                if not last:
                    turn_maxima(u + 1, 0)
                    turn_maxima(u + 1, 1)
                if project:
                    if next_group is not None:
                        pe.wait_ge(wqk_loaded, next_group * 16 + 16)
                    pe.wait_ge(s0_exp, (u + 1) * TB * 2)
                    q_proj(b)
                row_max(12, 13)
                if project:
                    k_proj(b)
                row_max(14)
                if not first:
                    pe.wait_ge(s0_masked, u * TB)
                    pe.wait_ge(vg_done, u)
                    if turns:
                        pe.wait_ge(o0_done, u - 1)
                    weighted0(other, 0)
                row_max(15)
                if not last:
                    turn_maxima(u + 1, 2)
                if not first:
                    weighted0(other, 1)
                    weighted0(other, 2)
                if not last:
                    turn_maxima(u + 1, TB - 1)
                if not first:
                    weighted0(other, 3).then_inc(o0_ready, 1)

            pe.wait_ge(bf_done, 2)
            pe.wait_ge(masks_done, 1)
            pe.wait_ge(setup_done, 13)
            pe.wait_ge(cross_bias_done, B)
            pe.wait_ge(g_done, B)
            pe.wait_ge(v0_done, B)
            pe.wait_ge(u_done, B)
            pe.wait_ge(wqk_loaded, 16)
            q_proj(0)
            k_proj(0)
            for n in range(NMAX):
                row_max_scores(0, 0, n)
                if n == 7:
                    q_proj(1)
                if n == 9:
                    k_proj(1)
            for t in range(TB):
                turn_maxima(0, t)
            unit0(0, 0, first=True, next_group=1, turns=False)
            unit0(1, 1, turns=False)
            with pe.Fori(1, NG - 1) as g:
                unit0(g * B, 0, next_group=g + 1)
                unit0(g * B + 1, 1)
            unit0(UNITS0 - 2, 0, project=False)
            unit0(UNITS0 - 1, 1, last=True, project=False)
            turn_sums(UNITS0 - 2)
            pe.wait_ge(s0_masked, UNITS0 * TB)
            pe.wait_ge(vg_done, UNITS0)
            pe.wait_ge(o0_done, UNITS0 - 1)
            for s in range(TB):
                mm = weighted0(1, s)
            mm.then_inc(o0_ready, 1)
            turn_sums(UNITS0 - 1)
            for b in range(B):
                pe.wait_ge(o0_done, UNITS0 - B + b + 1)
                for t in range(TB):
                    mm = pe.transpose(ps[:, b, t * 128:(t + 1) * 128], O0[:, b * TB + t, :], ident)
                mm.then_inc(ot0_ready, 1)
            for b in range(B):
                pe.wait_ge(ot0_done, b + 1)
                for t in range(TB):
                    n = b * TB + t
                    mm = pe.matmul(ps[:, 2 + b, t * C:(t + 1) * C], OT0[:, n * 128:(n + 1) * 128], w0_proj,
                                   start=True, stop=True)
                mm.then_inc(proj_ready, 1)
            turn_ln(0, CROSS, (0,))
            cross_pe(0, True)
            ff_pe(0, lambda n, j: [(2 * (n % 2), w0_m1[:, j * 128:(j + 1) * 128])], w0_m2, lambda n: (f_gelu, n + 1))

            with pe.Fori(0, LOOP_LAYERS) as l:
                pe.wait_ge(cross_loaded, l * 32 + 32)
                for n in range(2):
                    for j in range(H // 2):
                        mm = pe.matmul(ps[:, n, j * B * S:(j + 1) * B * S], wc[:, n, j * 128:(j + 1) * 128],
                                       ctxT[:, :], start=True, stop=True)
                    mm.then_inc(kv2_ready, 1)
                turn_ln(l + 1, ATTN, (0,))
                pe.wait_ge(kv2_done, 2 + l * 2 + 2)
                for r in range(2):
                    for j in range(4 * r, 4 * r + 4):
                        mm = pe.matmul(ps[:, 2 + r, (j % 4) * 128:(j % 4 + 1) * 128], wx[:, j, 0:C],
                                       K2b[:, j, :, :].rearrange("p b n -> p (b n)"), start=True, stop=True)
                    mm.then_inc(g_ready, 1)
                turn_ln(l + 1, ATTN, (1,))
                for b in range(B):
                    for j in range(H // 2):
                        mm = pe.matmul(ps[64 * (j % 2):64 * (j % 2) + 64, 4 + b, (j // 2) * C:(j // 2 + 1) * C],
                                       V2b[:, j, b, :], wx[:, j, C:2 * C], start=True, stop=True)
                    mm.then_inc(u_ready, 1)

                def project(i, k):
                    n, cols = k % 2, cols_of((k // 2 + 1) % 2)
                    if k // 2 != 0:
                        pe.wait_ge(w_lo, pairs_nth(l, 0 if k < 0 else i + 1) - 1 + n)
                    pe.matmul(ps[:, 6, :], Wh[:, n, :], hTh[:, cols], start=True, stop=False)
                    pe.matmul(ps[:, 6, :], Wl[:, n, :], hTh[:, cols], start=False, stop=False)
                    pe.matmul(ps[:, 6, :], Wh[:, n, :], hTl[:, cols], start=False, stop=True).then_inc(qk_ready, 1)

                def values(i, b):
                    for t in range(TB):
                        n = b * TB + t
                        mm = pe.matmul(ps[:, 6, t * C:(t + 1) * C], hT[:, n * 128:(n + 1) * 128], of_pair(i, 2),
                                       start=True, stop=True)
                    mm.then_inc(v_ready, 1)

                def row_max_scores(i, k, t, fresh=False):
                    if not fresh:
                        pe.wait_ge(d_max, nth(l, i, k, TB, t) - 2)
                    pe.matmul(ps[:, 4 + t % 2, :], QX[:, k % 4, t * 128:(t + 1) * 128], KX[:, k % 4, :],
                              start=True, stop=True).then_inc(d_ready, 1)

                def turned_scores(i, k, e, fresh):
                    if not fresh:
                        pe.wait_ge(s_exp, nth(l, i, k, 2, e) - 2)
                    for s in range(2 * e, 2 * e + 2):
                        keys = slice(s * 128, (s + 1) * 128)
                        pe.matmul(ps[:, s, :], KX[:, k, keys], QX[:, k, :], start=True, stop=False)
                        mm = pe.matmul(ps[:, s, :], KB[:, k, keys], QB[:, k, :], start=False, stop=True)
                    mm.then_inc(s_ready, 1)

                def weighted(b, s):
                    for e in range(2):
                        mm = pe.matmul(ps[64 * e:64 * e + 64, 7, :], V[:, b, s, 64 * e:64 * e + 64],
                                       Pt[:, 2 * b + e, s, :], start=s == 0, stop=s == TB - 1)
                    if s == TB - 1:
                        mm.then_inc(o_ready, 1)

                def denominators(i, b):
                    pe.wait_ge(p_sum, nth(l, i, 2 * b + 1, 1, 0))
                    for e in range(2):
                        for t in range(TB):
                            mm = pe.matmul(ps[32 * t:32 * t + 32, 5, e * 128:(e + 1) * 128], ones[:, :],
                                           Psum[:, 2 * b + e, t * 128:(t + 1) * 128], start=True, stop=True)
                    mm.then_inc(l_ready, 1)

                def spread_inverse(i, b):
                    pe.wait_ge(l_rec, couple_nth(l, i, b))
                    pe.wait_ge(o_copied, couple_nth(l, i, b))
                    for t in range(TB):
                        for e in range(2):
                            mm = pe.matmul(ps[64 * e:64 * e + 64, 7, t * 128:(t + 1) * 128], pick[:, t, :],
                                           Lr[:, e * 128:(e + 1) * 128], start=True, stop=True)
                    mm.then_inc(l_spread, 1)

                def out_rows(i, b):
                    pe.wait_ge(o_norm, couple_nth(l, i, b))
                    for t in range(TB):
                        mm = pe.matmul(ps[:, 7, t * C:(t + 1) * C], On[:, t * 128:(t + 1) * 128], of_pair(i, 3),
                                       start=True, stop=True)
                    mm.then_inc(op_ready, 1)

                def unit(i, k, first=False, last=False):
                    b, e = k // 2, k % 2
                    before = (i, 0) if b == 1 else None if first else (i - 1, 1)
                    none_before = first and k == 0
                    more = not (i is LAST and k >= 2)
                    pe.wait_ge(d_max, nth(l, i, k, TB, TB - 1))
                    pe.transpose(ps[0:TB, 5, 0:128], mcol[:, 0:TB], ident).then_inc(m_ready, 1)
                    if not last:
                        if e == 1 and more:
                            pe.wait_ge(qk_hi, qk_nth(l, i, k, 2, 0))
                        row_max_scores(i, k + 1, 0)
                    if e == 0:
                        if not first:
                            out_rows(i - 1, b)
                    elif before:
                        weighted(before[1], 3)
                    pe.wait_ge(m_done, nth(l, i, k, 1, 0))
                    if not last:
                        row_max_scores(i, k + 1, 1)
                    if e == 0:
                        pe.wait_ge(v_done, couple_nth(l, i, b))
                        if more:
                            project(i, k)
                    turned_scores(i, k, 0, none_before)
                    if e == 0 and before:
                        pe.wait_ge(d_max, nth(l, i, k + 1, TB, 1))
                        denominators(*before)
                        if not (first and b == 1):
                            pe.wait_ge(o_done, couple_nth(l, *before) - 1)
                        weighted(before[1], 0)
                        weighted(before[1], 1)
                    turned_scores(i, k, 1, none_before)
                    if not last:
                        row_max_scores(i, k + 1, 2)
                        if e == 0 and before:
                            pe.wait_ge(l_rec, couple_nth(l, *before))
                        row_max_scores(i, k + 1, 3)
                    if e == 0:
                        if more:
                            pe.wait_ge(qk_lo, qk_nth(l, i, k))
                            project(i, k + 1)
                        if before:
                            weighted(before[1], 2)
                    else:
                        if before:
                            spread_inverse(*before)
                        if more:
                            pe.wait_ge(qk_lo, qk_nth(l, i, k))
                            values(*((i, 1) if k == 1 else (i + 1, 0)))

                pe.wait_ge(setup_done, 13)
                pe.wait_ge(wa_loaded, l * 16 + 16)
                pe.wait_ge(ln_hT, half_nth(l + 1, ATTN, B - 1))
                pe.wait_ge(ln_lo, (l + 1) * B)
                project(0, -2)
                pe.wait_ge(qk_lo, qk_nth(l, 0, -2))
                project(0, -1)
                pe.wait_ge(qk_lo, qk_nth(l, 0, -1))
                values(0, 0)
                pe.wait_ge(u_done, B + (l + 1) * 2)
                for t in range(TB):
                    row_max_scores(0, 0, t, fresh=t < 2)
                for k in range(4):
                    unit(0, k, first=True)
                with pe.Fori(1, LAST) as i:
                    for k in range(4):
                        unit(i, k)
                for k in range(4):
                    unit(LAST, k, last=k == 3)
                pe.wait_ge(s_exp, nth(l, LAST, 3, 2, 1))
                out_rows(LAST, 0)
                pe.wait_ge(o_done, couple_nth(l, LAST, 0))
                for s in range(TB):
                    weighted(1, s)
                denominators(LAST, 1)
                spread_inverse(LAST, 1)
                turn_ln(l + 1, CROSS, (0,))
                out_rows(LAST, 1)
                cross_pe(l + 1, False)
                pe.wait_ge(ff_loaded, l * 16 + 16)
                ff_pe(l + 1, lambda n, j: [(2 * (n % 2), w_p[:, HID + j * 128:HID + (j + 1) * 128]),
                                           (2 * (n % 2) + 1, w_p[:, j * 128:(j + 1) * 128])], w_2,
                      lambda n: (f_u, l * B * FC + n + 1))


def kernel(**inputs):
    import numpy as _np
    import concourse.bacc as _bacc
    from concourse import mybir as _mybir
    from concourse.bass_utils import run_bass_kernel_spmd as _run

    a = {k: _np.asarray(v) for k, v in inputs.items()}
    f = a["x"].dtype
    l0 = {k[len("L0_xattn_"):]: v for k, v in a.items() if k.startswith("L0_")}

    consts = _np.zeros((128, 260 + H), f)
    consts[:, 0:128] = _np.eye(128)
    consts[:, 128:256] = _np.triu(_np.full((128, 128), -BIG), 1)
    row = _np.arange(128) % 32
    second = (row >= D0) & (row < 2 * D0)
    third = (row >= 2 * D0) & (row < 3 * D0)
    consts[:, 256] = ((row <= ROW_MASK) & ~second) * 1.0 - second
    consts[:, 257] = second
    consts[:, 258] = ((row <= ROW_MAX) & ~third) * 1.0 - third
    consts[:, 259] = third
    for h in range(H):
        consts[h * D0:(h + 1) * D0, 260 + h] = 1

    w0_qk = _np.zeros((NG, 128, 258), f)
    for g in range(NG):
        for j in range(G0):
            cols = slice((g * G0 + j) * D0, (g * G0 + j + 1) * D0)
            for copy in range(3):
                at = 32 * j + copy * D0
                for n in range(2):
                    w0_qk[g, :, 128 * n + at:128 * n + at + D0] = l0["qkv_w"][:, n * C:(n + 1) * C][:, cols]
                    w0_qk[g, at:at + D0, 256 + n] = l0["qkv_b"][n * C:(n + 1) * C][cols]
            w0_qk[g, 32 * j + ROW_MASK, 256] = 1
            w0_qk[g, 32 * j + ROW_MAX, 257] = 1

    def chunks(w):
        return w.reshape(-1, 128, w.shape[1]).transpose(1, 0, 2).reshape(128, -1)

    w0 = _np.concatenate([l0["qkv_w"][:, 2 * C:], l0["proj_w"], l0["q_w"].T, l0["out_w"], l0["mlp1_w"],
                          chunks(l0["mlp2_w"])], axis=1)
    wk0 = _np.concatenate([l0["k_w"], l0["v_w"]], axis=1)
    vec0 = _np.stack([l0["ln1_w"], l0["ln1_b"], l0["ln2_w"], l0["ln2_b"], l0["ln3_w"], l0["ln3_b"],
                      *l0["mlp1_b"].reshape(FC, 128), l0["k_b"], l0["v_b"], l0["q_b"]], axis=1)
    rows0 = _np.stack([l0["qkv_b"][2 * C:], l0["proj_b"], l0["out_b"], l0["mlp2_b"]])

    n1, n2, n3 = "L1_xattn_", "L2_xattn_", "L3_xattn_"

    def three(first, second, third, turned=True):
        second = a[n2 + second]
        return a[n1 + first], second.T if turned else second, a[n3 + third]

    def stack(*parts):
        return _np.stack([_np.concatenate(layer, axis=-1) for layer in zip(*parts)])

    def by_head(ws):
        return [w.T.reshape(H, D, C) for w in ws]

    def out_by_head(ws):
        return [w.reshape(H, D, C) for w in ws]

    def pair_cols(ws):
        return [w.reshape(C, H // 2, 2 * D).transpose(1, 0, 2) for w in ws]

    def pair_rows(ws):
        return [w.reshape(H // 2, 2 * D, C) for w in ws]

    def by_pair(ws):
        return [w.reshape(H // 2, 128, C).transpose(1, 0, 2) for w in ws]

    w_attn = stack(pair_cols(three("Wq1", "wq1", "q1_w")), pair_cols(three("Wk1", "wk1", "k1_w")),
                   pair_cols(three("Wv1", "wv1", "v1_w")), pair_rows(three("Wo1", "wo1", "o1_w")))
    w_attn = w_attn.transpose(0, 2, 1, 3).reshape(LOOP_LAYERS, 128, -1)
    w_ctx = stack(three("Wk2", "wk2", "k2_w"), three("Wv2", "wv2", "v2_w"))
    w_cross = stack(by_pair(by_head(three("Wq2", "wq2", "q2_w"))), by_pair(out_by_head(three("Wo2", "wo2", "o2_w"))))
    w_cross = w_cross.reshape(LOOP_LAYERS, 128, -1)
    w_ff = stack(three("Wp", "w_geglu", "ff1_w"), [chunks(w) for w in three("W2", "w_ffout", "ff2_w")])

    def col(ws):
        return [w.reshape(-1, 128).T for w in ws]

    vec = stack(*(col(three(*names, turned=False)) for names in (
        ("g1", "ln1_g", "n1_w"), ("be1", "ln1_b", "n1_b"), ("g2", "ln2_g", "n2_w"), ("be2", "ln2_b", "n2_b"),
        ("g3", "ln3_g", "n3_w"), ("be3", "ln3_b", "n3_b"), ("bp", "b_geglu", "ff1_b"))))
    rows = _np.stack([_np.stack(three(*names, turned=False)) for names in (
        ("bo1", "bo1", "o1_b"), ("bo2", "bo2", "o2_b"), ("b2", "b_ffout", "ff2_b"))], axis=1)
    ctx_t = a["ctx_768"].reshape(B * S, CE).T

    arrays, args = {}, []
    for name, v in (("x", a["x"]), ("ctx_t", ctx_t), ("tgt_mask", a["mask_BxS_bf0"]), ("enc_mask", a["mask_BxS2_bf0"]),
                    ("consts", consts), ("w0_qk", w0_qk), ("w0", w0), ("wk0", wk0), ("vec0", vec0), ("rows0", rows0),
                    ("w_attn", w_attn), ("w_ctx", w_ctx), ("w_cross", w_cross), ("w_ff", w_ff), ("vec", vec),
                    ("rows", rows)):
        arrays["in_" + name] = _np.ascontiguousarray(v)
    nc = _bacc.Bacc("TRN2", target_bir_lowering=False, num_devices=1)
    for name, v in arrays.items():
        args.append(nc.dram_tensor(name, v.shape, _mybir.dt.from_np(v.dtype), kind="ExternalInput").ap())
    out = nc.dram_tensor("out", (B, T, C), _mybir.dt.float32, kind="ExternalOutput").ap()
    decoder_stack_kernel(nc, *args, out)
    r = _run(nc, [arrays], core_ids=[0])
    return r.results[0]["out"]
```
